# Optimizing a Trainium2 kernel written in Bass

```python
import numpy as np
import jax
import jax.numpy as jnp

def _softmax(x, axis=-1):
    return jax.nn.softmax(x, axis=axis)

def _gelu(x):
    return jax.nn.gelu(x, approximate=True)

def _silu(x):
    return jax.nn.silu(x)

def _sigmoid(x):
    return jax.nn.sigmoid(x)

def _layernorm(x, axis=-1, eps=1e-05):
    m = jnp.mean(x, axis=axis, keepdims=True)
    v = jnp.var(x, axis=axis, keepdims=True)
    return (x - m) / jnp.sqrt(v + eps)

def _scatter_add(tgt, idx, src, axis=0):
    return tgt.at[idx].add(src)

def _segment_sum(src, seg, n):
    return jax.ops.segment_sum(src, seg, n)
kernel_name = 'mk_recurrent_d2_jaxref_r8_770110'

def setup_inputs(seed: int=0):
    np.random.seed(seed)
    _w = jnp.asarray

    def _L0_attn_setup():
        import jax, jax.numpy as jnp
        import numpy as np
        EMBED_DIM = 128
        key = jax.random.key(seed)
        ks = jax.random.split(key, 9)
        B, S, D = (4, 512, EMBED_DIM)
        s = 1.0 / np.sqrt(D)
        inp = {'x': jax.random.normal(ks[0], (B, S, D), dtype=jnp.float32)}
        names = ['q', 'k', 'v', 'out']
        for i, n in enumerate(names):
            inp[f'w_{n}'] = jax.random.uniform(ks[1 + 2 * i], (D, D), jnp.float32, -s, s)
            inp[f'b_{n}'] = jax.random.uniform(ks[2 + 2 * i], (D,), jnp.float32, -s, s)
        return inp
    _L0_attn_in = _L0_attn_setup()

    def _L0_ffn_setup():
        import jax, jax.numpy as jnp
        import numpy as np
        CAP_FACTOR = 1.5
        key = jax.random.key(seed)
        ks = jax.random.split(key, 6)
        E, S, D, M = (48, 4, 128, 128)
        K = D // S
        x = jax.random.normal(ks[0], (4, 512, D), dtype=jnp.float32)
        Wr = jax.random.normal(ks[1], (E, D), dtype=jnp.float32) * 0.02
        W1 = jax.random.normal(ks[2], (E, S, D, M), dtype=jnp.float32) * (1.0 / np.sqrt(D))
        b1 = jnp.zeros((E, S, M), dtype=jnp.float32)
        W2 = jax.random.normal(ks[3], (E, S, M, K), dtype=jnp.float32) * (1.0 / np.sqrt(M))
        b2 = jnp.zeros((E, S, K), dtype=jnp.float32)
        return {'x': x, 'Wr': Wr, 'W1': W1, 'b1': b1, 'W2': W2, 'b2': b2}
    _L0_ffn_in = _L0_ffn_setup()

    def _L1_attn_setup():
        import jax, jax.numpy as jnp
        import numpy as np
        import math
        D_MODEL = 128
        N_HEADS = 16
        LATENT = 32
        key = jax.random.key(seed)
        ks = jax.random.split(key, 9)
        B, T, C, L = (2, 256, D_MODEL, LATENT)
        s = 0.02
        return {'x': jax.random.normal(ks[0], (B, T, C), dtype=jnp.float32), 'Wq': jax.random.normal(ks[1], (C, C), dtype=jnp.float32) * s, 'bq': jnp.zeros((C,), dtype=jnp.float32), 'Wkd': jax.random.normal(ks[2], (C, 2 * L), dtype=jnp.float32) * s, 'bkd': jnp.zeros((2 * L,), dtype=jnp.float32), 'Wku': jax.random.normal(ks[3], (L, 2 * C), dtype=jnp.float32) * s, 'bku': jnp.zeros((2 * C,), dtype=jnp.float32), 'Wo': jax.random.normal(ks[4], (C, C), dtype=jnp.float32) * s, 'bo': jnp.zeros((C,), dtype=jnp.float32)}
    _L1_attn_in = _L1_attn_setup()

    def _L1_ffn_setup():
        import jax, jax.numpy as jnp
        import numpy as np
        B, S, D, F, E = (8, 128, 128, 512, 8)
        EPS = 1e-05
        key = jax.random.key(seed)
        ks = jax.random.split(key, 4)
        s = 0.02
        return {'input_features': jax.random.normal(ks[0], (B, S, D), jnp.float32), 'centroids': jax.random.normal(ks[1], (E, D), jnp.float32) * 0.1, 'ln_g': jnp.ones((E, D), jnp.float32), 'ln_b': jnp.zeros((E, D), jnp.float32), 'w1': jax.random.normal(ks[2], (E, D, F), jnp.float32) * s, 'b1': jnp.zeros((E, F), jnp.float32), 'w2': jax.random.normal(ks[3], (E, F, D), jnp.float32) * s, 'b2': jnp.zeros((E, D), jnp.float32)}
    _L1_ffn_in = _L1_ffn_setup()
    _d = {'L0_attn_x': _L0_attn_in['x'], 'L0_attn_w_q': _L0_attn_in['w_q'], 'L0_attn_b_q': _L0_attn_in['b_q'], 'L0_attn_w_k': _L0_attn_in['w_k'], 'L0_attn_b_k': _L0_attn_in['b_k'], 'L0_attn_w_v': _L0_attn_in['w_v'], 'L0_attn_b_v': _L0_attn_in['b_v'], 'L0_attn_w_out': _L0_attn_in['w_out'], 'L0_attn_b_out': _L0_attn_in['b_out'], 'L0_ffn_Wr': _L0_ffn_in['Wr'], 'L0_ffn_W1': _L0_ffn_in['W1'], 'L0_ffn_b1': _L0_ffn_in['b1'], 'L0_ffn_W2': _L0_ffn_in['W2'], 'L0_ffn_b2': _L0_ffn_in['b2'], 'L1_attn_Wq': _L1_attn_in['Wq'], 'L1_attn_bq': _L1_attn_in['bq'], 'L1_attn_Wkd': _L1_attn_in['Wkd'], 'L1_attn_bkd': _L1_attn_in['bkd'], 'L1_attn_Wku': _L1_attn_in['Wku'], 'L1_attn_bku': _L1_attn_in['bku'], 'L1_attn_Wo': _L1_attn_in['Wo'], 'L1_attn_bo': _L1_attn_in['bo'], 'L1_ffn_centroids': _L1_ffn_in['centroids'], 'L1_ffn_ln_g': _L1_ffn_in['ln_g'], 'L1_ffn_ln_b': _L1_ffn_in['ln_b'], 'L1_ffn_w1': _L1_ffn_in['w1'], 'L1_ffn_b1': _L1_ffn_in['b1'], 'L1_ffn_w2': _L1_ffn_in['w2'], 'L1_ffn_b2': _L1_ffn_in['b2']}
    _x0 = _d['L0_attn_x']
    _d['L0_attn_x'] = jax.random.normal(jax.random.fold_in(jax.random.key(seed), 1), (2, 1024, 128), dtype=_x0.dtype)
    del _x0
    return _d

def reference(L0_attn_x, L0_attn_w_q, L0_attn_b_q, L0_attn_w_k, L0_attn_b_k, L0_attn_w_v, L0_attn_b_v, L0_attn_w_out, L0_attn_b_out, L0_ffn_Wr, L0_ffn_W1, L0_ffn_b1, L0_ffn_W2, L0_ffn_b2, L1_attn_Wq, L1_attn_bq, L1_attn_Wkd, L1_attn_bkd, L1_attn_Wku, L1_attn_bku, L1_attn_Wo, L1_attn_bo, L1_ffn_centroids, L1_ffn_ln_g, L1_ffn_ln_b, L1_ffn_w1, L1_ffn_b1, L1_ffn_w2, L1_ffn_b2):

    def _L0_attn_ref(x, w_q, b_q, w_k, b_k, w_v, b_v, w_out, b_out):
        import jax, jax.numpy as jnp
        import numpy as np
        EMBED_DIM = 128
        D = x.shape[-1]
        scaling = 1.0 / jnp.sqrt(jnp.asarray(D, x.dtype))
        q = jnp.einsum('bsd,ed->bse', x, w_q) + b_q
        k = jnp.einsum('bsd,ed->bse', x, w_k) + b_k
        v = jnp.einsum('bsd,ed->bse', x, w_v) + b_v
        scores = jnp.einsum('bqd,bkd->bqk', q, k) * scaling
        attn = jax.nn.softmax(scores, axis=-1)
        out = jnp.einsum('bqk,bkd->bqd', attn, v)
        return jnp.einsum('bsd,ed->bse', out, w_out) + b_out

    def _L0_ffn_ref(x, Wr, W1, b1, W2, b2):
        import jax, jax.numpy as jnp
        import numpy as np
        CAP_FACTOR = 1.5
        orig_shape = x.shape
        D = x.shape[-1]
        E = Wr.shape[0]
        xf = x.reshape(-1, D)
        T = xf.shape[0]
        cap = int(CAP_FACTOR * T / E)
        logits = xf @ Wr.T
        vals, idx = jax.lax.top_k(logits.T, cap)
        w = jax.nn.softmax(vals, axis=-1)
        xg = xf[idx]
        h = jax.nn.gelu(jnp.einsum('ecd,esdm->ecsm', xg, W1) + b1[:, None], approximate=False)
        y = jnp.einsum('ecsm,esmk->ecsk', h, W2) + b2[:, None]
        y = y.reshape(E, cap, D) * w[..., None]
        out = jnp.zeros_like(xf).at[idx.reshape(-1)].add(y.reshape(-1, D))
        return out.reshape(orig_shape)

    def _L1_attn_ref(x, Wq, bq, Wkd, bkd, Wku, bku, Wo, bo):
        import jax, jax.numpy as jnp
        import numpy as np
        import math
        D_MODEL = 128
        N_HEADS = 16
        LATENT = 32
        B, T, C = x.shape
        H = N_HEADS
        D = C // H
        L = LATENT
        q = (x @ Wq + bq).reshape(B, T, H, D)
        kv_latent = jax.nn.gelu(x @ Wkd + bkd, approximate=False)
        lat = kv_latent[..., :L] + kv_latent[..., L:]
        kv = lat @ Wku + bku
        k = kv[..., :C].reshape(B, T, H, D)
        v = kv[..., C:].reshape(B, T, H, D)
        scale = 1.0 / math.sqrt(D)
        attn = jnp.einsum('bqhd,bkhd->bhqk', q, k) * scale
        causal = jnp.tril(jnp.ones((T, T), dtype=bool))
        attn = jnp.where(causal, attn, -jnp.inf)
        attn = jax.nn.softmax(attn, axis=-1)
        out = jnp.einsum('bhqk,bkhd->bqhd', attn, v).reshape(B, T, C)
        return out @ Wo + bo

    def _L1_ffn_ref(input_features, centroids, ln_g, ln_b, w1, b1, w2, b2):
        import jax, jax.numpy as jnp
        import numpy as np
        B, S, D, F, E = (8, 128, 128, 512, 8)
        EPS = 1e-05
        x = input_features.reshape(-1, D)
        aff = jax.lax.stop_gradient(x @ centroids.T)
        eid = jnp.argmax(aff, axis=-1)
        alpha = jax.nn.sigmoid(jnp.sum(x * centroids[eid], axis=-1, keepdims=True))
        mu = jnp.mean(x, axis=-1, keepdims=True)
        var = jnp.mean((x - mu) ** 2, axis=-1, keepdims=True)
        xn = (x - mu) * jax.lax.rsqrt(var + EPS)
        xln = xn * ln_g[eid] + ln_b[eid]
        onehot = jax.nn.one_hot(eid, E, dtype=x.dtype)
        ffn = jnp.zeros_like(x)
        for e in range(E):
            h = jax.nn.relu(xln @ w1[e] + b1[e])
            ffn = ffn + onehot[:, e:e + 1] * (h @ w2[e] + b2[e])
        out = x + alpha * ffn
        return out.reshape(input_features.shape)
    x = L0_attn_x
    xn = _layernorm(x, axis=-1)
    s = _L0_attn_ref(xn, L0_attn_w_q, L0_attn_b_q, L0_attn_w_k, L0_attn_b_k, L0_attn_w_v, L0_attn_b_v, L0_attn_w_out, L0_attn_b_out)
    g = _silu(_L0_ffn_ref(xn, L0_ffn_Wr, L0_ffn_W1, L0_ffn_b1, L0_ffn_W2, L0_ffn_b2))
    x = x + s * g
    xn = _layernorm(x, axis=-1)
    s = _L1_attn_ref(xn, L1_attn_Wq, L1_attn_bq, L1_attn_Wkd, L1_attn_bkd, L1_attn_Wku, L1_attn_bku, L1_attn_Wo, L1_attn_bo)
    g = _silu(_L1_ffn_ref(xn, L1_ffn_centroids, L1_ffn_ln_g, L1_ffn_ln_b, L1_ffn_w1, L1_ffn_b1, L1_ffn_w2, L1_ffn_b2))
    x = x + s * g
    return x

_drawn_inputs = setup_inputs


def setup_inputs(seed=0):
    import zlib

    import numpy as np

    out = dict(_drawn_inputs(seed))
    spreads = {'L0_ffn_b1': (0.0, 0.8),
     'L0_ffn_b2': (0.0, 2.0),
     'L1_attn_bq': (0.0, 2.0),
     'L1_attn_bkd': (0.0, 0.8),
     'L1_attn_bku': (0.0, 0.736),
     'L1_attn_bo': (0.0, 0.8),
     'L1_ffn_ln_g': (1.0, 0.6),
     'L1_ffn_ln_b': (0.0, 0.8),
     'L1_ffn_b1': (0.0, 2.0),
     'L1_ffn_b2': (0.0, 2.0)}
    factors = {'L0_attn_w_q': 8.0,
     'L0_attn_b_q': 8.0,
     'L0_attn_w_k': 8.0,
     'L0_attn_b_k': 200.0,
     'L0_attn_w_v': 8.0,
     'L0_attn_b_v': 8.0,
     'L0_attn_w_out': 8.0,
     'L0_attn_b_out': 21.34,
     'L0_ffn_Wr': 8.0,
     'L0_ffn_W1': 8.0,
     'L0_ffn_W2': 8.0,
     'L1_attn_Wq': 8.0,
     'L1_attn_Wkd': 8.0,
     'L1_attn_Wku': 8.0,
     'L1_attn_Wo': 4.83,
     'L1_ffn_centroids': 8.0,
     'L1_ffn_w1': 8.0,
     'L1_ffn_w2': 8.0}
    for name, (base, spread) in spreads.items():
        noise = np.random.default_rng([zlib.crc32(name.encode()), seed]).standard_normal(out[name].shape)
        drawn = base * np.exp(spread * noise) if base else spread * noise
        out[name] = jnp.asarray(drawn.astype(out[name].dtype))
    for name, factor in factors.items():
        out[name] = (out[name] * factor).astype(out[name].dtype)
    return out
```

```python
import concourse.bass as bass
from concourse import mybir
from contextlib import ExitStack


def build(nc, a, out):
    fp32 = mybir.dt.float32
    bf16 = mybir.dt.bfloat16
    u32 = mybir.dt.uint32
    ALU = mybir.AluOpType
    ACT = mybir.ActivationFunctionType
    AX = mybir.AxisListType

    x_dram, wr_dram = a["L0_attn_x"], a["L0_ffn_Wr"]
    B, S, D = x_dram.shape
    P = 128
    T = B * S
    NT = T // P
    BT = S // P
    E0 = wr_dram.shape[0]
    NS, KY = a["L0_ffn_W2"].shape[1], a["L0_ffn_W2"].shape[3]
    CAP = int(1.5 * T / E0)
    NP = E0 // 2
    RING = 12
    EPS = 1e-5
    SC0 = float(D) ** -0.5
    NC = T // 512
    H1, DH = 16, 8
    SC1 = float(DH) ** -0.5
    E1, _, F1 = a["L1_ffn_w1"].shape
    FC = F1 // P
    LAT = a["L1_attn_Wku"].shape[0]
    GH = 4
    NG = B * H1 // GH
    KQ = 72
    KM = KQ + 3
    NSORT = NT + E1 - 1
    NEG = -1.0e30
    STEPS = []
    for qc in range(S // 512):
        for kt in range(4 * qc + 4):
            q0 = max(kt * P, qc * 512)
            STEPS.append((qc, kt, q0, (qc + 1) * 512 - q0))
    NSTEP = len(STEPS)
    UNITS = []
    for u in range(8):
        UNITS += [(u // 2, 1, 4 + 2 * (u % 2)), (u // 2, 1, 5 + 2 * (u % 2)), (2 * (u // 4), 2, u % 4)]
    NU = len(UNITS)
    AHEAD = NU + 8
    FFN0 = NSTEP
    OUT0 = FFN0 + 3 * NSORT + 1

    ctx = ExitStack()
    with ctx:
        def sb(name, shape, dt=fp32):
            return ctx.enter_context(nc.sbuf_tensor(name, shape, dt))

        def pb(name, shape, dt=fp32):
            return ctx.enter_context(nc.psum_tensor(name, shape, dt))

        def sem(name):
            return ctx.enter_context(nc.semaphore(name))

        xn_rows = nc.dram_tensor("xn_rows", [T, D], fp32, kind="Internal").ap()
        NACC = 4
        acc_rows = nc.dram_tensor("acc_rows", [NACC * T, D], fp32, kind="Internal").ap()
        q_scr = nc.dram_tensor("q_scr", [B, 3, NG // B, DH, GH * S], bf16, kind="Internal").ap()
        k_scr = nc.dram_tensor("k_scr", [B, 3, NG // B, DH, GH * S], bf16, kind="Internal").ap()
        m_scr = nc.dram_tensor("m_scr", [NG, 3 * GH * BT, P], bf16, kind="Internal").ap()
        xs_rows = nc.dram_tensor("xs_rows", [NSORT * P, D], fp32, kind="Internal").ap()
        ys_rows = nc.dram_tensor("ys_rows", [NSORT * P, D], fp32, kind="Internal").ap()

        ident = sb("ident", [P, P])
        x_sb = sb("x_sb", [P, NT, D])
        xn = sb("xn", [P, NT, D])
        xnT = sb("xnT", [P, T])
        qk_mem = sb("qk_mem", [P, 2, T])
        qT, kT = qk_mem[:, 0, :], qk_mem[:, 1, :]
        v_sb = sb("v_sb", [P, NT, D])
        s_sb = sb("s_sb", [P, NT, D])
        stats = sb("stats", [P, NT, 6])
        mv = sb("mv", [P, NT, 2])
        rstd = sb("rstd", [P, NT])
        var_e = sb("var_e", [P, NT])
        sdev = sb("sdev", [P, NT])
        newt = sb("newt", [P, NT])
        w_in = sb("w_in", [P, 4, P])
        w_T = sb("w_T", [P, 4, P])
        wr_in = sb("wr_in", [E0, D])
        wr_T = sb("wr_T", [P, 64])
        bqk = sb("bqk", [P, 2])
        bvo = sb("bvo", [P, 2, D])
        zeros = s_sb
        mem1 = sb("mem1", [P, E1 * (2 * F1 + D)])
        logits = mem1[:, 0:S]
        top_v = sb("top_v", [P, CAP])
        top_i = sb("top_i", [P, CAP], u32)
        top_f = sb("top_f", [P, CAP])
        half_off = sb("half_off", [P, 1])
        hi_v = sb("hi_v", [E0, CAP])
        hi_f = sb("hi_f", [E0, CAP])
        slot_v = sb("slot_v", [E0, CAP])
        slot_m = sb("slot_m", [E0, CAP])
        slot_d = sb("slot_d", [E0, CAP])
        slot_s = sb("slot_s", [E0, 4])
        slots = sb("slots", [E0, 4, CAP])
        w_col = sb("w_col", [P, NP])
        i_col = sb("i_col", [P, NP])
        s_off = sb("s_off", [P, NP])
        g_idx = sb("g_idx", [P, NP], u32)
        s_idx = sb("s_idx", [P, NP], u32)
        probs = mem1[:, S:3 * S].rearrange("p (a s) -> p a s", a=2)
        probsT = mem1[:, 3 * S:5 * S].rearrange("p (a s) -> p a s", a=2)
        nmax = sb("nmax", [P, NT])
        nbias = sb("nbias", [P, NT])
        rsum = sb("rsum", [P, NT])
        rinv = sb("rinv", [P, NT])
        oT = sb("oT", [P, P])
        w1r = sb("w1r", [P, RING, 2 * NS, P])
        w2s = sb("w2s", [P, E0 * NS, KY])
        b1_in = sb("b1_in", [96, 2, P])
        b1T = sb("b1T", [P, E0 * NS])
        pairind = sb("pairind", [2, P])
        b2p = mem1[0:2, S:S + NP * D].rearrange("p (n d) -> p n d", d=D)
        xg = mem1[:, 5 * S:5 * S + NP * D].rearrange("p (n d) -> p n d", d=D)
        xgT = sb("xgT", [P, 2, P])
        hb = sb("hb", [P, 2, 512])
        hg = sb("hg", [P, 2, 512])
        y_sb = sb("y_sb", [P, 4, D])
        w1r_flat = w1r[:, :, :, :].rearrange("p a b c -> p (a b c)")
        w2s_flat = w2s[:, :, :].rearrange("p a b -> p (a b)")
        accs = w1r_flat[:, 0:NACC * T].rearrange("p (a t d) -> p a t d", a=NACC, d=D)
        identb = sb("identb", [P, P], bf16)
        causal = sb("causal", [P, P], bf16)
        before = sb("before", [P, P], bf16)
        onesb = sb("onesb", [P, P], bf16)
        wq1 = sb("wq1", [P, P])
        wkd = sb("wkd", [P, 2 * LAT])
        wku = sb("wku", [LAT, 2 * P])
        wo1 = sb("wo1", [P, P])
        brow_qk = sb("brow_qk", [2, P])
        brow_p = sb("brow_p", [2, P])
        wqp = sb("wqp", [P, P])
        wkp = sb("wkp", [LAT, P])
        bcol1 = sb("bcol1", [P, 2])
        bkd = sb("bkd", [LAT, 2])
        brow1 = sb("brow1", [P, 2, D])
        cen_in = sb("cen_in", [E1, D])
        cenT = sb("cenT", [P, E1])
        small_in = sb("small_in", [6 * E1, D])
        smallT = sb("smallT", [P, 6 * E1])
        wall = mem1[:, :].rearrange("p (e n) -> p e n", e=E1)
        w_tile = s_sb[:, :, :].rearrange("p t d -> p (t d)").rearrange("p (a n) -> p a n", a=2)
        b2_tile = sb("b2_tile", [P, 2, D])
        s_tile = sb("s_tile", [P, 2, 6])
        latA = hb[0:LAT, :, :].rearrange("p a n -> p (a n)")
        latB = hg[0:LAT, :, :].rearrange("p a n -> p (a n)")
        latT = w1r_flat[0:LAT, NACC * T:NACC * T + T]
        parts_mem = w2s_flat.bitcast(bf16)
        parts = [parts_mem[:, 3 * T * i:3 * T * i + 3 * T].rearrange("p (a t) -> p a t", a=3) for i in range(2)]
        stack_mem = w1r_flat.bitcast(bf16)
        SM = GH * S

        def stack(side, g):
            o = (2 * (g % 3) + side) * SM
            return stack_mem[:, o:o + SM].rearrange("p (j t) -> p j t", j=GH)
        pr1 = qk_mem[:, :, :].rearrange("p a t -> p (a t)").rearrange("p (r j t) -> p r j t", r=2, j=GH)
        v_ext = xnT[:, :].rearrange("p (a t j c) -> p a t j c", a=2, t=BT, j=GH)
        s_fin = s_sb
        o_sb = w2s_flat[:, 0:T].rearrange("p (t d) -> p t d", d=D)
        f_sb = w2s_flat[:, T:2 * T].rearrange("p (t d) -> p t d", d=D)
        acc_sb = hb
        smallW = sb("smallW", [P, E1, 6])
        xs_in = y_sb
        xlT = sb("xlT", [P, P])
        hs = hg
        ys_sb = sb("ys_sb", [P, 2, D])
        negm = sb("negm", [P, GH, BT])
        negr = sb("negr", [P, GH, BT])
        mparts = sb("mparts", [P, 3, GH, BT], bf16)
        mrows = sb("mrows", [3 * GH * BT, P], bf16)
        rden = sb("rden", [P, 4, GH])
        rt_mem = hg[:, :, :].rearrange("p a n -> p (a n)")
        aff, cand, onehot, full = [rt_mem[:, i * NT * E1:(i + 1) * NT * E1] for i in range(4)]
        aff, cand, onehot = [v.rearrange("p (t e) -> p t e", e=E1) for v in (aff, cand, onehot)]
        full = full.rearrange("p (e t) -> p e t", e=E1)
        rank = rt_mem[:, 4 * NT * E1:6 * NT * E1].rearrange("p (a t e) -> p a t e", a=2, e=E1)
        cum = rt_mem[:, 6 * NT * E1:8 * NT * E1].rearrange("p (a t e) -> p a t e", a=2, e=E1)
        tile_c = hb[:, 0, 0:NSORT * E1].rearrange("p (j e) -> p j e", e=E1)
        amax = sb("amax", [P, NT])
        emin = sb("emin", [P, NT])
        onehotb = sb("onehotb", [P, NT, E1], bf16)
        ctile = sb("ctile", [P, 3, E1])
        em8 = sb("em8", [P, E1])
        m128 = sb("m128", [P, NT])
        iota_j = sb("iota_j", [P, NSORT])
        tile_f = sb("tile_f", [P, NSORT])
        tile_e = sb("tile_e", [P, NSORT], mybir.dt.int32)
        pos_f = sb("pos_f", [P, NT])
        pos = sb("pos", [P, NT], u32)
        alpha = sb("alpha", [P, 3, NT])

        pS = pb("pS", [P, 2, S])
        pT = pb("pT", [P, 2, 512])
        pM = pb("pM", [P, 512])
        pH = pb("pH", [P, 512])

        names = ("s_const s_xrows s_zero s_ones "
                 "s_st s_mv s_ve s_sd s_rstd s_xn s_wload s_wrload s_bload s_b1load s_b2load s_w2load "
                 "s_wtr s_wt s_xtr s_xt s_lg s_lgc s_pj s_pje_a s_pje_v "
                 "s_S s_max s_nm s_exp s_tr s_ev s_pv s_oT s_op s_ri s_fin "
                 "s_t1 s_t2 s_t3 s_tf s_hb s_sl s_we s_wn s_ctr s_cc s_so "
                 "s_k1 s_w1load s_b1load1 s_cload s_wall s_xs0 s_silu s_x1 s_af s_rt s_oh s_rk s_rkc "
                 "s_q1 s_q1e s_la s_lae s_lat s_kk s_kke s_vv s_v1e s_cp s_sub s_scr "
                 "s_u s_um s_msp s_mt s_mte s_mrow s_s1 s_e1 s_sel s_pv1 s_ace s_tr1 s_rd1 s_nrm s_ve_b "
                 "s_pos s_te s_wj s_fa s_fae s_fb s_fbe s_relu s_fc s_fce s_al s_als s_g1 s_gate "
                 "s_fin2 s_perm s_btr s_bte s_mscr s_ot s_ote s_pj1 s_fin1 s_vz s_vo s_smw "
                 "s_xgt s_xge s_h s_hbias s_gelu s_y s_ysc s_accz s_sum s_out").split()
        sm = {n: sem(n) for n in names}
        s_x = [sem(f"s_xin{c}") for c in range(4)]
        s_g = [sem(f"s_gat{i}") for i in range(4)]
        s_w1 = [sem(f"s_w1_{i}") for i in range(RING)]
        s_sc = [sem(f"s_sc{i}") for i in range(2)]
        s_stk = [sem(f"s_stk{i}") for i in range(3)]
        s_ysd = [sem(f"s_ysd{i}") for i in range(2)]
        s_xsl = [sem(f"s_xsl{i}") for i in range(4)]
        block = ctx.enter_context(nc.Block())

        x_t = x_dram.rearrange("b (t p) d -> p (b t) d", p=P)
        out_t = out.rearrange("b (t p) d -> p (b t) d", p=P)
        xn_t = xn_rows.rearrange("(t p) d -> p t d", p=P)
        acc_t = acc_rows.rearrange("(a t p) d -> p a t d", p=P, a=NACC)
        w1_v = a["L0_ffn_W1"].rearrange("e s d m -> d (e s) m")
        w2_v = a["L0_ffn_W2"].rearrange("e s m k -> m (e s) k")

        def ffn_part(n):
            m = n - FFN0
            return (m // 3, m % 3) if 0 <= m < 3 * NSORT else (-1, -1)

        def sel_count(n):
            return sum(1 for m in range(n + 1) if STEPS[m % NSTEP][2] == STEPS[m % NSTEP][1] * P)

        def ends(n):
            if n < 0 or n >= NG * NSTEP:
                return -1
            qc, kt = STEPS[n % NSTEP][:2]
            return 2 * (n // NSTEP) + qc if kt == 4 * qc + 3 else -1

        def ffn_count(n):
            return min(max(n - FFN0, 0), 3 * NSORT)

        def wait_ffn(eng, m):
            j, sub = (m - 1) // 3, (m - 1) % 3
            eng.wait_ge(sm[("s_fae", "s_fbe", "s_fce")[sub]], j + 1)

        def stack_ready(eng, g):
            eng.wait_ge(s_stk[g % 3], 16 * 18 * (g // 3 + 1))

        @block.sync
        def _(sp):
            for c in range(4):
                sp.dma_start(x_sb[:, 4 * c:4 * c + 4, :], x_t[:, 4 * c:4 * c + 4, :]).then_inc(s_x[c], 16)
            for j in range(4):
                w = a[("L0_attn_w_q", "L0_attn_w_k", "L0_attn_w_v", "L0_attn_w_out")[j]]
                sp.dma_start(w_in[:, j, :], w).then_inc(sm["s_wload"], 16)
            sp.dma_start(wr_in[:, :], wr_dram).then_inc(sm["s_wrload"], 16)
            for j in range(2):
                bcol = a[("L0_attn_b_q", "L0_attn_b_k")[j]]
                sp.dma_start(bqk[:, j:j + 1], bcol.rearrange("(p a) -> p a", a=1)).then_inc(sm["s_bload"], 16)
                brow = a[("L0_attn_b_v", "L0_attn_b_out")[j]]
                sp.dma_start(bvo[:, j, :], brow.partition_broadcast(P)).then_inc(sm["s_bload"], 16)
            b1_v = a["L0_ffn_b1"].rearrange("e s m -> (e s) m")
            for j in range(2):
                sp.dma_start(b1_in[:, j, :], b1_v[96 * j:96 * j + 96, :]).then_inc(sm["s_b1load"], 16)
            sp.dma_start(wq1[:, :], a["L1_attn_Wq"]).then_inc(sm["s_w1load"], 16)
            sp.dma_start(wkd[:, :], a["L1_attn_Wkd"]).then_inc(sm["s_w1load"], 16)
            sp.dma_start(wku[:, :], a["L1_attn_Wku"]).then_inc(sm["s_w1load"], 16)
            sp.dma_start(wo1[:, :], a["L1_attn_Wo"]).then_inc(sm["s_w1load"], 16)
            col = lambda v: v.rearrange("(p a) -> p a", a=1)
            bku, bkd_v = a["L1_attn_bku"], a["L1_attn_bkd"]
            row = lambda v: v.rearrange("(a p) -> a p", a=1)
            sp.dma_start(brow_qk[0:1, :], row(a["L1_attn_bq"])).then_inc(sm["s_b1load1"], 16)
            sp.dma_start(brow_qk[1:2, :], row(bku[0:P])).then_inc(sm["s_b1load1"], 16)
            sp.dma_start(bkd[:, 0:1], col(bkd_v[0:LAT])).then_inc(sm["s_b1load1"], 16)
            sp.dma_start(bkd[:, 1:2], col(bkd_v[LAT:2 * LAT])).then_inc(sm["s_b1load1"], 16)
            sp.dma_start(brow1[:, 0, :], bku[P:2 * P].partition_broadcast(P)).then_inc(sm["s_b1load1"], 16)
            sp.dma_start(brow1[:, 1, :], a["L1_attn_bo"].partition_broadcast(P)).then_inc(sm["s_b1load1"], 16)
            sp.dma_start(cen_in[:, :], a["L1_ffn_centroids"]).then_inc(sm["s_cload"], 16)
            sp.dma_start(small_in[0:4 * E1, :], a["L1_ffn_b1"].rearrange("e (c p) -> (e c) p", p=P)).then_inc(sm["s_cload"], 16)
            sp.dma_start(small_in[4 * E1:5 * E1, :], a["L1_ffn_ln_g"]).then_inc(sm["s_cload"], 16)
            sp.dma_start(small_in[5 * E1:6 * E1, :], a["L1_ffn_ln_b"]).then_inc(sm["s_cload"], 16)
            sp.wait_ge(sm["s_const"], 1)
            xs_t = xs_rows.rearrange("(j p) d -> p j d", p=P)
            zer = zeros[:, :, :]
            sp.dma_start(xs_t[:, 0:NT, :], zer).then_inc(sm["s_xs0"], 16)
            sp.dma_start(xs_t[:, NT:NSORT, :], zer[:, 0:NSORT - NT, :]).then_inc(sm["s_xs0"], 16)
            for j in range(NACC):
                sp.dma_start(acc_t[:, j, :, :], zeros[:, :, :]).then_inc(sm["s_accz"], 16)
            for c in range(4):
                sp.wait_ge(sm["s_xn"], 4 * c + 4)
                sp.dma_start(xn_t[:, 4 * c:4 * c + 4, :], xn[:, 4 * c:4 * c + 4, :]).then_inc(sm["s_xrows"], 16)
            for p in range(4):
                sp.dma_start(w1r[:, p, :, :], w1_v[:, 8 * p:8 * p + 8, :]).then_inc(s_w1[p], 16)
            for j in range(4):
                sp.dma_start(w2s[:, 48 * j:48 * j + 48, :], w2_v[:, 48 * j:48 * j + 48, :]).then_inc(sm["s_w2load"], 16)
            for p in range(4, RING):
                sp.dma_start(w1r[:, p, :, :], w1_v[:, 8 * p:8 * p + 8, :]).then_inc(s_w1[p], 16)
            sp.wait_ge(sm["s_tf"], 1)
            sp.dma_start(hi_v[:, :], top_v[64:64 + E0, :]).then_inc(sm["s_hb"], 16)
            sp.dma_start(hi_f[:, :], top_f[64:64 + E0, :]).then_inc(sm["s_hb"], 16)
            sp.wait_ge(sm["s_pv"], NT)
            sp.dma_start(b2p, a["L0_ffn_b2"].rearrange("(p r) s k -> r p (s k)", r=2)).then_inc(sm["s_b2load"], 16)
            for p in range(RING, NP):
                sp.wait_ge(sm["s_h"], p - RING + 1)
                sp.dma_start(w1r[:, p - RING, :, :], w1_v[:, 8 * p:8 * p + 8, :]).then_inc(s_w1[p - RING], 16)
            for i in range(2):
                sp.wait_ge(s_sc[i], 16 * (NP // 2))
            sp.wait_ge(sm["s_h"], NP)
            for c in range(4):
                for j in range(NACC):
                    sp.dma_start(accs[:, j, 4 * c:4 * c + 4, :], acc_t[:, j, 4 * c:4 * c + 4, :]).then_inc(s_x[c], 16)
            w1f = a["L1_ffn_w1"].rearrange("e d f -> d e f")
            w2f = a["L1_ffn_w2"].rearrange("e (c p) d -> p e c d", p=P)
            sp.dma_start(wall[:, :, 0:F1], w1f).then_inc(sm["s_wall"], 16)
            for e in range(E1):
                sp.dma_start(wall[:, e, F1:2 * F1].rearrange("p (c d) -> p c d", d=D), w2f[:, e, :, :]).then_inc(sm["s_wall"], 16)
            sp.dma_start(wall[:, :, 2 * F1:2 * F1 + D], a["L1_ffn_b2"].partition_broadcast(P)).then_inc(sm["s_wall"], 16)

            def load_stack(g):
                b, g4 = g // (NG // B), g % (NG // B)
                sp.wait_ge(sm["s_scr"], 16 * 6 * (b + 1))
                if g < 3:
                    sp.wait_ge(sm["s_vo"], g + 1)
                    sp.wait_ge(sm["s_vv"], NC)
                if g >= 3:
                    sp.wait_ge(sm["s_s1"], GH * NSTEP * (g - 2))
                for x in range(3):
                    for y in range(3):
                        r = 24 * x + 8 * y
                        for side in range(2):
                            src = (q_scr[b, x, g4], k_scr[b, y, g4])[side]
                            sp.dma_start(stack(side, g)[r:r + DH, :, :].rearrange("p j t -> p (j t)"),
                                         src).then_inc(s_stk[g % 3], 16)

            def store_parts(b):
                for st in range(3):
                    for side in range(2):
                        sp.wait_ge(sm["s_cp"], 6 * b + 2 * st + side + 1)
                        sp.dma_start((q_scr, k_scr)[side][b, st].rearrange("g d (j t) -> (g d j) t", j=GH),
                                     parts[side][:, st, b * S:b * S + S]).then_inc(sm["s_scr"], 16)

            def store_m(g):
                sp.wait_ge(sm["s_mte"], g + 1)
                sp.dma_start(m_scr[g], mrows[:, :]).then_inc(sm["s_mscr"], 16)
                sp.wait_ge(sm["s_mscr"], 16 * (g + 1))
                sp.dma_start(stack(0, g)[KQ:KM, :, :].rearrange("p j t -> p (j t)"),
                             m_scr[g].rearrange("(a n) q -> a (n q)", a=3)).then_inc(sm["s_mrow"], 16)

            store_parts(0)
            load_stack(0)
            load_stack(1)
            store_parts(1)
            load_stack(2)
            store_m(0)
            sp.wait_ge(sm["s_pos"], 16 * NT)
            for j in range(3):
                sp.dma_start(xs_in[:, j % 4, :], xs_t[:, j, :]).then_inc(s_xsl[j % 4], 16)
            for n in range(NG * NSTEP + 2):
                g = (n + 4) // NSTEP
                if (n + 4) % NSTEP == 0 and g < NG:
                    store_m(g)
                if n % NSTEP == 0 and n // NSTEP + 2 < NG and n:
                    load_stack(n // NSTEP + 2)
                j, sub = ffn_part(n)
                if sub == 0 and j + 3 < NSORT:
                    if j >= 1:
                        sp.wait_ge(sm["s_fa"], j)
                    sp.dma_start(xs_in[:, (j + 3) % 4, :], xs_t[:, j + 3, :]).then_inc(s_xsl[(j + 3) % 4], 16)
                if sub == 2:
                    sp.wait_ge(sm["s_fce"], j + 1)
                    sp.dma_start(ys_rows[j * P:j * P + P, :], ys_sb[:, j % 2, :]).then_inc(s_ysd[j % 2], 16)
            for c in range(4):
                sp.wait_ge(sm["s_fin2"], 2 * c + 2)
                sp.dma_start(out_t[:, 4 * c:4 * c + 4, :], x_sb[:, 4 * c:4 * c + 4, :]).then_inc(sm["s_out"], 16)
            for i in range(2):
                sp.wait_ge(s_ysd[i], 16 * ((NSORT + 1 - i) // 2))
            sp.wait_ge(sm["s_scr"], 16 * 12)
            sp.wait_ge(sm["s_xrows"], 64)
            sp.wait_ge(sm["s_xs0"], 32)
            sp.wait_ge(sm["s_accz"], 16 * NACC)
            sp.wait_ge(sm["s_out"], 64)

        @block.gpsimd
        def _(pool):
            pool.memset(zeros[:, :, :], 0.0).then_inc(sm["s_const"], 1)
            pool.memset(ident[:, :], 0.0).then_inc(sm["s_zero"], 1)
            pool.memset(wr_T[:, :], 0.0).then_inc(sm["s_zero"], 1)
            pool.memset(pairind[:, :], 0.0).then_inc(sm["s_zero"], 1)
            pool.memset(identb[:, :], 0.0).then_inc(sm["s_k1"], 1)
            pool.memset(causal[:, :], 0.0).then_inc(sm["s_k1"], 1)
            pool.memset(before[:, :], 1.0).then_inc(sm["s_k1"], 1)
            pool.memset(onesb[:, :], 1.0).then_inc(sm["s_k1"], 1)
            pool.iota(em8[:, :], [[1, E1]], base=-E1, channel_multiplier=0, allow_small_or_imprecise_dtypes=True).then_inc(sm["s_k1"], 1)
            pool.iota(m128[:, :], [[P, NT]], base=0, channel_multiplier=0, allow_small_or_imprecise_dtypes=True).then_inc(sm["s_k1"], 1)
            pool.iota(iota_j[:, :], [[1, NSORT]], base=0, channel_multiplier=0, allow_small_or_imprecise_dtypes=True).then_inc(sm["s_k1"], 1)
            pool.wait_ge(sm["s_k1"], 7)
            pool.affine_select(out=identb[:, :], in_=identb[:, :], compare_op=ALU.not_equal, fill=1.0,
                               base=0, pattern=[[-1, P]], channel_multiplier=1).then_inc(sm["s_k1"], 1)
            pool.affine_select(out=causal[:, :], in_=causal[:, :], compare_op=ALU.is_ge, fill=NEG,
                               base=0, pattern=[[-1, P]], channel_multiplier=1).then_inc(sm["s_k1"], 1)
            pool.affine_select(out=before[:, :], in_=before[:, :], compare_op=ALU.is_gt, fill=0.0,
                               base=0, pattern=[[1, P]], channel_multiplier=-1).then_inc(sm["s_k1"], 1)
            pool.wait_ge(sm["s_zero"], 3)
            pool.affine_select(out=ident[:, :], in_=ident[:, :], compare_op=ALU.not_equal, fill=1.0,
                               base=0, pattern=[[-1, P]], channel_multiplier=1).then_inc(sm["s_const"], 1)
            pool.affine_select(out=pairind[:, :].rearrange("r (e c) -> r e c", e=2),
                               in_=pairind[:, :].rearrange("r (e c) -> r e c", e=2), compare_op=ALU.not_equal, fill=1.0,
                               base=0, pattern=[[-1, 2], [0, 64]], channel_multiplier=1).then_inc(sm["s_const"], 1)

            pool.wait_ge(sm["s_xrows"], 64)
            pool.wait_ge(sm["s_so"], 2)

            def gather(p):
                if p >= 4:
                    pool.wait_ge(s_g[p % 4], 16 * (p // 4))
                pool.indirect_dma_start(out=xg[:, p, :], out_offset=None, in_=xn_rows,
                                        in_offset=bass.IndirectOffsetOnAxis(ap=g_idx[:, p:p + 1], axis=0),
                                        ).then_inc(s_g[p % 4], 16)
            for p in range(6):
                gather(p)
            pool.wait_ge(sm["s_accz"], 16 * NACC)
            for p in range(NP):
                if p + 6 < NP:
                    gather(p + 6)
                pool.wait_ge(sm["s_ysc"], p + 1)
                if p >= 2:
                    pool.wait_ge(s_sc[p % 2], 16 * (p // 2))
                pool.indirect_dma_start(out=acc_rows,
                                        out_offset=bass.IndirectOffsetOnAxis(ap=s_idx[:, p:p + 1], axis=0),
                                        in_=y_sb[:, p % 4, :], in_offset=None,
                                        compute_op=ALU.add).then_inc(s_sc[p % 2], 16)

            def build_v(g):
                if g >= 2:
                    pool.wait_ge(sm["s_pv1"], NSTEP * (g - 1))
                b, g4 = g // (NG // B), g % (NG // B)
                src = v_sb[:, b * BT:b * BT + BT, g4 * GH * DH:(g4 + 1) * GH * DH].rearrange("p t (j d) -> p t j d", d=DH)
                pool.tensor_copy(v_ext[:, g % 2, :, :, 0:DH], src).then_inc(sm["s_ve_b"], 1)

            pool.wait_ge(sm["s_x1"], 8)
            for g in range(3):
                pool.memset(stack(1, g)[64:KM, :, :], 1.0).then_inc(sm["s_vo"], 1)
            pool.wait_ge(sm["s_v1e"], NC)
            pool.wait_ge(sm["s_vv"], NC)
            pool.wait_ge(sm["s_vo"], 3)
            pool.memset(xnT[:, :], 0.0).then_inc(sm["s_vz"], 1)
            pool.wait_ge(sm["s_vz"], 1)
            pool.memset(v_ext[:, :, :, :, DH:DH + 1], 1.0).then_inc(sm["s_vz"], 1)
            build_v(0)
            build_v(1)
            pool.wait_ge(sm["s_te"], 7)
            pool.wait_ge(sm["s_xn"], 3 * NT)
            pool.wait_ge(sm["s_xs0"], 32)
            for t in range(NT):
                pool.indirect_dma_start(out=xs_rows, out_offset=bass.IndirectOffsetOnAxis(ap=pos[:, t:t + 1], axis=0),
                                        in_=s_sb[:, t, :], in_offset=None).then_inc(sm["s_pos"], 16)

            for n in range(NG * NSTEP + 2):
                if n < NG * NSTEP:
                    qc, kt, q0, cols = STEPS[n % NSTEP]
                    if q0 == kt * P:
                        pool.wait_ge(sm["s_e1"], GH * n + GH)
                        blk_ = pr1[:, n % 2, :, 0:P]
                        pool.affine_select(out=blk_, in_=blk_, compare_op=ALU.is_ge, fill=0.0, base=0,
                                           pattern=[[0, GH], [1, P]], channel_multiplier=-1).then_inc(sm["s_sel"], 1)
                if n % NSTEP == NSTEP - 3 and 2 <= n // NSTEP + 1 < NG:
                    build_v(n // NSTEP + 1)
                m = n - (FFN0 + 3 * NSORT + 1)
                if m == 0:
                    for i in range(2):
                        pool.wait_ge(s_ysd[i], 16 * ((NSORT + 1 - i) // 2))
                for t in range(2 * m, 2 * m + 2) if 0 <= m < NT // 2 else ():
                    pool.indirect_dma_start(out=f_sb[:, t, :], out_offset=None, in_=ys_rows,
                                            in_offset=bass.IndirectOffsetOnAxis(ap=pos[:, t:t + 1], axis=0)).then_inc(sm["s_g1"], 16)

        @block.tensor
        def _(pe):
            pe.wait_ge(sm["s_const"], 3)
            pe.wait_ge(sm["s_wload"], 64)
            for j in range(4):
                last = nc.tensor.transpose(pT[:, 0, j * P:j * P + P], w_in[:, j, :], ident[:, :])
            last.then_inc(sm["s_wtr"], 1)
            pe.wait_ge(sm["s_wrload"], 16)
            pe.wait_ge(sm["s_b1load"], 32)
            nc.tensor.transpose(pM[:, 0:E0], wr_in[:, :], ident[0:E0, 0:E0])
            for j in range(2):
                last = nc.tensor.transpose(pM[:, 64 + 96 * j:160 + 96 * j], b1_in[:, j, :], ident[0:96, 0:96])
            pe.wait_ge(sm["s_cload"], 64)
            nc.tensor.transpose(pM[:, 256:256 + E1], cen_in[:, :], ident[0:E1, 0:E1])
            last = nc.tensor.transpose(pM[:, 272:272 + 6 * E1], small_in[:, :], ident[0:6 * E1, 0:6 * E1])
            last.then_inc(sm["s_wtr"], 1)
            for c in range(NC):
                pe.wait_ge(sm["s_xn"], 4 * c + 4)
                if c == 1:
                    pe.wait_ge(sm["s_wt"], 1)
                if c >= 2:
                    pe.wait_ge(sm["s_xt"], c - 1)
                for j in range(4):
                    last = nc.tensor.transpose(pT[:, (c + 1) % 2, j * P:j * P + P], xn[:, 4 * c + j, :], ident[:, :])
                last.then_inc(sm["s_xtr"], 1)
            pe.wait_ge(sm["s_wt"], 5)
            for c in range(NC):
                pe.wait_ge(sm["s_xt"], c + 1)
                h = c // 2
                last = nc.tensor.matmul(pS[64 * h:64 * h + 64, 0, (c % 2) * 512:(c % 2) * 512 + 512], wr_T[:, :],
                                        xnT[:, c * 512:c * 512 + 512], start=True, stop=True)
            last.then_inc(sm["s_lg"], 1)
            dst = [pS[:, 1, 0:512], pS[:, 1, 512:1024], pM[:, :], pH[:, :]]
            n = 0
            for c in range(NC):
                for j in range(3):
                    if n >= 4:
                        cc, jj = (n - 4) // 3, (n - 4) % 3
                        if jj < 2:
                            pe.wait_ge(sm["s_pje_a"], 2 * cc + jj + 1)
                        else:
                            pe.wait_ge(sm["s_pje_v"], cc + 1)
                    if j < 2:
                        last = nc.tensor.matmul(dst[n % 4], w_T[:, j, :], xnT[:, c * 512:c * 512 + 512], start=True, stop=True)
                    else:
                        for t in range(4):
                            last = nc.tensor.matmul(dst[n % 4][:, t * P:t * P + P],
                                                    xnT[:, c * 512 + t * P:c * 512 + t * P + P], w_T[:, 2, :],
                                                    start=True, stop=True)
                    last.then_inc(sm["s_pj"], 1)
                    n += 1

            def scores(i):
                b = i // BT
                if i == 0:
                    pe.wait_ge(sm["s_lgc"], 1)
                    pe.wait_ge(sm["s_pje_a"], 2 * NC)
                    pe.wait_ge(sm["s_pje_v"], NC)
                if i >= 2:
                    pe.wait_ge(sm["s_exp"], i - 1)
                for h in range(2):
                    last = nc.tensor.matmul(pS[:, i % 2, h * 512:h * 512 + 512], qT[:, i * P:i * P + P],
                                            kT[:, b * S + h * 512:b * S + h * 512 + 512], start=True, stop=True)
                last.then_inc(sm["s_S"], 1)

            def turn(i):
                pe.wait_ge(sm["s_exp"], i + 1)
                for h in range(2):
                    if i:
                        pe.wait_ge(sm["s_ev"], 2 * (i - 1) + h + 1)
                    for j in range(4):
                        last = nc.tensor.transpose(pT[:, h, j * P:j * P + P],
                                                   probs[:, i % 2, (4 * h + j) * P:(4 * h + j + 1) * P], ident[:, :])
                    last.then_inc(sm["s_tr"], 1)

            def values(i):
                b = i // BT
                pe.wait_ge(sm["s_ev"], 2 * i + 2)
                if i:
                    pe.wait_ge(sm["s_oT"], i)
                for j in range(BT):
                    last = nc.tensor.matmul(pM[:, 0:P], v_sb[:, b * BT + j, :], probsT[:, i % 2, j * P:j * P + P],
                                            start=(j == 0), stop=(j == BT - 1))
                last.then_inc(sm["s_pv"], 1)

            def project(i):
                pe.wait_ge(sm["s_oT"], i + 1)
                if i:
                    pe.wait_ge(sm["s_fin"], i)
                nc.tensor.matmul(pH[:, 0:P], oT[:, :], w_T[:, 3, :], start=True, stop=True).then_inc(sm["s_op"], 1)

            scores(0)
            for i in range(NT):
                if i + 1 < NT:
                    scores(i + 1)
                if i:
                    values(i - 1)
                turn(i)
                if i:
                    project(i - 1)
            values(NT - 1)
            project(NT - 1)
            pe.wait_ge(sm["s_sl"], 7)
            nc.tensor.transpose(pM[:, 256:256 + E0], slots[:, 0:2, :].rearrange("e a c -> e (a c)"), ident[0:E0, 0:E0])
            nc.tensor.transpose(pM[:, 304:304 + E0], slots[:, 2:4, :].rearrange("e a c -> e (a c)"),
                                ident[0:E0, 0:E0]).then_inc(sm["s_ctr"], 1)

            def spread(p):
                pe.wait_ge(s_g[p % 4], 16 * (p // 4 + 1))
                if p >= 2:
                    pe.wait_ge(sm["s_xge"], p - 1)
                nc.tensor.transpose(pT[:, p % 2, 0:P], xg[:, p, :], ident[:, :]).then_inc(sm["s_xgt"], 1)

            def up(p):
                pe.wait_ge(sm["s_xge"], p + 1)
                pe.wait_ge(s_w1[p % RING], 16 * (p // RING + 1))
                if p >= 2:
                    pe.wait_ge(sm["s_hbias"], p - 1)
                for n in range(2 * NS):
                    last = nc.tensor.matmul(pS[:, p % 2, 64 * n:64 * n + 64], w1r[:, p % RING, n, :],
                                            xgT[:, p % 2, 64 * (n // NS):64 * (n // NS) + 64], start=True, stop=True)
                last.then_inc(sm["s_h"], 1)

            def down(p):
                pe.wait_ge(sm["s_gelu"], p + 1)
                if p == 0:
                    pe.wait_ge(sm["s_b2load"], 16)
                    pe.wait_ge(sm["s_w2load"], 64)
                    pe.wait_ge(sm["s_cc"], 4)
                    pe.wait_ge(sm["s_fin"], NT)
                if p >= 2:
                    pe.wait_ge(sm["s_ysc"], p - 1)
                yb = (pM, pH)[p % 2]
                nc.tensor.matmul(yb[:, 0:D], pairind[:, :], b2p[:, p, :], start=True, stop=False,
                                 skip_group_check=True)
                for n in range(2 * NS):
                    e, s = n // NS, n % NS
                    last = nc.tensor.matmul(yb[64 * e:64 * e + 64, KY * s:KY * s + KY],
                                            hg[:, p % 2, 64 * n:64 * n + 64], w2s[:, (2 * p + e) * NS + s, :],
                                            start=False, stop=(n == 2 * NS - 1), skip_group_check=True)
                last.then_inc(sm["s_y"], 1)

            spread(0)
            for p in range(NP):
                up(p)
                if p + 1 < NP:
                    spread(p + 1)
                if p:
                    down(p - 1)
            down(NP - 1)

            pe.wait_ge(sm["s_perm"], 3)
            pe.wait_ge(sm["s_ysc"], NP - 1)
            nc.tensor.transpose(pM[:, 0:2], brow_p[:, :], ident[0:2, 0:2]).then_inc(sm["s_btr"], 1)
            pe.wait_ge(sm["s_w1load"], 64)
            for b in range(B):
                for c in (2 * b, 2 * b + 1):
                    pe.wait_ge(sm["s_xn"], NT + 4 * c + 4)
                    if b:
                        pe.wait_ge(sm["s_lae"], 4)
                    for j in range(4):
                        last = nc.tensor.transpose(pT[:, c % 2, j * P:j * P + P], xn[:, 4 * c + j, :], ident[:, :])
                    last.then_inc(sm["s_xtr"], 1)
                for c in (2 * b, 2 * b + 1):
                    pe.wait_ge(sm["s_xt"], NC + c + 1)
                    if b:
                        pe.wait_ge(sm["s_q1e"], c - 1)
                    nc.tensor.matmul(pS[:, 0, (c % 2) * 512:(c % 2) * 512 + 512], wqp[:, :],
                                     xnT[:, c * 512:c * 512 + 512], start=True, stop=True).then_inc(sm["s_q1"], 1)
                for c in (2 * b, 2 * b + 1):
                    if c % 2:
                        pe.wait_ge(sm["s_lae"], 2 * c)
                    for h in range(2):
                        last = nc.tensor.matmul(pT[0:LAT, h, :], wkd[:, h * LAT:h * LAT + LAT],
                                                xnT[:, c * 512:c * 512 + 512], start=True, stop=True)
                    last.then_inc(sm["s_la"], 1)
                for c in (2 * b, 2 * b + 1):
                    if b:
                        pe.wait_ge(sm["s_kke"], c - 1)
                    pe.wait_ge(sm["s_lat"], c + 1)
                    nc.tensor.matmul(pS[:, 1, (c % 2) * 512:(c % 2) * 512 + 512], wkp[:, :],
                                     latT[:, c * 512:c * 512 + 512], start=True, stop=True).then_inc(sm["s_kk"], 1)
            pe.wait_ge(sm["s_bte"], 1)
            for t in range(NT):
                last = nc.tensor.matmul(pM[:, t * E1:t * E1 + E1], xnT[:, t * P:t * P + P], cenT[:, :], start=True, stop=True)
            last.then_inc(sm["s_af"], 1)
            pe.wait_ge(sm["s_rt"], 1)
            for c in range(NC):
                if c >= 2:
                    pe.wait_ge(sm["s_v1e"], c - 1)
                for t in range(4):
                    last = nc.tensor.matmul((pM, pH)[c % 2][:, t * P:t * P + P], latT[:, (4 * c + t) * P:(4 * c + t + 1) * P],
                                            wku[:, P:2 * P], start=True, stop=True)
                last.then_inc(sm["s_vv"], 1)
            pe.wait_ge(sm["s_oh"], 2)
            pe.wait_ge(sm["s_lae"], 2 * NC)
            pe.wait_ge(sm["s_k1"], 10)
            oh = onehotb[:, :, :].rearrange("p t e -> p (t e)")
            nc.tensor.matmul(pT[:, 0, 0:NT * E1], before[:, :], oh, start=True, stop=True)
            nc.tensor.matmul(pT[:, 0, NT * E1:2 * NT * E1], onesb[:, :], oh, start=True, stop=True).then_inc(sm["s_rk"], 1)
            pe.wait_ge(sm["s_rkc"], 1)

            def unit(u):
                g = u // NU
                j, heads, qt = UNITS[u % NU]
                if u % NU == 0:
                    stack_ready(pe, g)
                if u == 0:
                    pe.wait_ge(sm["s_kke"], NC)
                if u >= 2:
                    pe.wait_ge(sm["s_um"], u - 1)
                keys = (qt + 1) * P
                if heads == 2:
                    spans = [(j, 0, 0, keys), (j + 1, 512, 0, keys)]
                else:
                    spans = [(j, 0, 0, 512), (j, 512, 512, keys - 512)]
                for h, at, k0, w in spans:
                    diag = heads == 2 or k0
                    last = nc.tensor.matmul(pS[:, u % 2, at:at + w], stack(0, g)[0:KQ, h, qt * P:qt * P + P],
                                            stack(1, g)[0:KQ, h, k0:k0 + w], start=True, stop=not diag)
                    if diag:
                        last = nc.tensor.matmul(pS[:, u % 2, at + w - P:at + w], identb[:, :], causal[:, :],
                                                start=False, stop=True)
                last.then_inc(sm["s_u"], 1)

            def turn_m(g):
                pe.wait_ge(sm["s_msp"], 5 * g + 5)
                nc.tensor.transpose(pH[:, :].bitcast(bf16)[0:3 * GH * BT, 0:P],
                                    mparts[:, :, :, :].rearrange("p a j t -> p (a j t)"), identb[:, :]).then_inc(sm["s_mt"], 1)

            def score(n, j):
                e = GH * n + j
                g = n // NSTEP
                qc, kt, q0, cols = STEPS[n % NSTEP]
                if n % NSTEP == 0 and j == 0:
                    pe.wait_ge(sm["s_mrow"], 16 * (g + 1))
                if e >= 2:
                    pe.wait_ge(sm["s_e1"], e - 1)
                nc.tensor.matmul(pT[:, j % 2, 0:cols], stack(1, g)[0:KM, j, kt * P:kt * P + P],
                                 stack(0, g)[0:KM, j, q0:q0 + cols], start=True, stop=True).then_inc(sm["s_s1"], 1)

            def weigh(n):
                g = n // NSTEP
                qc, kt, q0, cols = STEPS[n % NSTEP]
                pe.wait_ge(sm["s_e1"], GH * n + GH)
                if q0 == kt * P:
                    pe.wait_ge(sm["s_sel"], sel_count(n))
                if n % NSTEP == 0:
                    pe.wait_ge(sm["s_ve_b"], g + 1)
                if kt == 0 and n:
                    pe.wait_ge(sm["s_nrm"], 2 * g + qc)
                for j in range(GH):
                    last = nc.tensor.matmul(pM[32 * j:32 * j + 32, q0 - qc * 512:q0 - qc * 512 + cols],
                                            v_ext[:, g % 2, kt, j, :], pr1[:, n % 2, j, 0:cols],
                                            start=(kt == 0), stop=(kt == 4 * qc + 3))
                last.then_inc(sm["s_pv1"], 1)

            def turn_acc(r):
                pe.wait_ge(sm["s_ace"], r + 1)
                for t in range(4):
                    last = nc.tensor.transpose(pM[:, t * P:t * P + P], acc_sb[:, r % 2, t * P:t * P + P], ident[:, :])
                last.then_inc(sm["s_tr1"], 1)

            def ffn(j, sub):
                if sub == 0:
                    pe.wait_ge(s_xsl[j % 4], 16 * (j // 4 + 1))
                    if j:
                        pe.wait_ge(sm["s_fce"], j)
                    nc.tensor.transpose(pH[:, 0:P], xs_in[:, j % 4, :], ident[:, :]).then_inc(sm["s_fa"], 1)
                elif sub == 1:
                    pe.wait_ge(sm["s_fae"], j + 1)
                    for c in range(FC):
                        last = nc.tensor.matmul(pH[:, c * P:c * P + P], w_tile[:, j % 2, c * P:c * P + P], xlT[:, :],
                                                start=True, stop=True)
                    last.then_inc(sm["s_fb"], 1)
                else:
                    pe.wait_ge(sm["s_relu"], j + 1)
                    for c in range(FC):
                        last = nc.tensor.matmul(pH[:, 0:D], hs[:, j % 2, c * P:c * P + P],
                                                w_tile[:, j % 2, F1 + c * D:F1 + c * D + D],
                                                start=(c == 0), stop=(c == FC - 1))
                    last.then_inc(sm["s_fc"], 1)

            def turn_heads(c):
                pe.wait_ge(sm["s_nrm"], NG * (c // 2 + 1))
                if c:
                    pe.wait_ge(sm["s_fin1"], c)
                for t in range(4):
                    last = nc.tensor.transpose(pH[:, t * P:t * P + P], o_sb[:, 4 * c + t, :], ident[:, :])
                last.then_inc(sm["s_ot"], 1)

            def project1(c):
                pe.wait_ge(sm["s_ote"], c + 1)
                for t in range(4):
                    last = nc.tensor.matmul(pH[:, t * P:t * P + P], hs[:, c % 2, t * P:t * P + P], wo1[:, :],
                                            start=True, stop=True)
                last.then_inc(sm["s_pj1"], 1)

            for u in range(NU):
                unit(u)
            turn_m(0)
            for u in range(NU, AHEAD):
                unit(u)
            for n in range(NG * NSTEP + 2):
                last_step = n >= NG * NSTEP
                if not last_step:
                    score(n, 0)
                if n >= 2 and ends(n - 2) >= 0:
                    turn_acc(ends(n - 2))
                if AHEAD + 2 * n < NG * NU:
                    unit(AHEAD + 2 * n)
                if not last_step:
                    score(n, 1)
                if AHEAD + 2 * n + 1 < NG * NU:
                    unit(AHEAD + 2 * n + 1)
                if 1 <= n <= NG * NSTEP:
                    weigh(n - 1)
                if not last_step:
                    score(n, 2)
                    score(n, 3)
                if (n + 4) % NSTEP == 0 and (n + 4) // NSTEP < NG:
                    if ffn_count(n):
                        wait_ffn(pe, ffn_count(n))
                    turn_m((n + 4) // NSTEP)
                j, sub = ffn_part(n)
                if sub >= 0:
                    pe.wait_ge(sm["s_mte"], 1 + (n + 4) // NSTEP if (n + 4) // NSTEP < NG else NG)
                    ffn(j, sub)
                for c in range(NC // 2):
                    if n == OUT0 + 4 * c:
                        if c == 0:
                            pe.wait_ge(sm["s_fce"], NSORT)
                        turn_heads(c)
                    if n == OUT0 + 4 * c + 1:
                        project1(c)

            for c in range(NC // 2, NC):
                turn_heads(c)
                project1(c)

        @block.vector
        def _(dve):
            def ln_rest(turn_, k, tiles, src, dst):
                n0, n1 = tiles[0], tiles[-1] + 1
                for t in tiles:
                    dve.wait_ge(sm["s_st"], turn_ * NT + t + 1)
                    nc.vector.bn_aggr(mv[:, t, :], stats[:, t, :]).then_inc(sm["s_mv"], 1)
                dve.wait_ge(sm["s_mv"], turn_ * NT + n1)
                rs_, ve_, nw_ = rstd[:, n0:n1], var_e[:, n0:n1], newt[:, n0:n1]
                nc.vector.tensor_scalar(ve_, mv[:, n0:n1, 1], EPS, None, ALU.add).then_inc(sm["s_ve"], 1)
                dve.wait_ge(sm["s_sd"], k + 1)
                nc.vector.reciprocal(rs_, sdev[:, n0:n1]).then_inc(sm["s_rstd"], 1)
                dve.wait_ge(sm["s_rstd"], 5 * k + 1)
                nc.vector.tensor_tensor(nw_, rs_, rs_, ALU.mult).then_inc(sm["s_rstd"], 1)
                dve.wait_ge(sm["s_rstd"], 5 * k + 2)
                nc.vector.tensor_tensor(nw_, nw_, ve_, ALU.mult).then_inc(sm["s_rstd"], 1)
                dve.wait_ge(sm["s_rstd"], 5 * k + 3)
                nc.vector.tensor_scalar(nw_, nw_, -0.5, 1.5, ALU.mult, ALU.add).then_inc(sm["s_rstd"], 1)
                dve.wait_ge(sm["s_rstd"], 5 * k + 4)
                nc.vector.tensor_tensor(rs_, rs_, nw_, ALU.mult).then_inc(sm["s_rstd"], 1)
                dve.wait_ge(sm["s_rstd"], 5 * k + 5)
                for t in tiles:
                    nc.vector.tensor_scalar(dst[:, t, :], src[:, t, :], mv[:, t, 0:1], rstd[:, t:t + 1],
                                            ALU.subtract, ALU.mult).then_inc(sm["s_xn"], 1)

            def route_a(dve):
                dve.wait_ge(sm["s_rt"], 1)
                nc.vector.tensor_reduce(amax[:, :], aff[:, :, :], AX.X, ALU.max).then_inc(sm["s_rt"], 1)
                dve.wait_ge(sm["s_rt"], 2)
                wide = amax[:, :].unsqueeze(2).to_broadcast([P, NT, E1])
                nc.vector.tensor_tensor(cand[:, :, :], aff[:, :, :], wide, ALU.is_equal).then_inc(sm["s_rt"], 1)
                dve.wait_ge(sm["s_rt"], 3)
                dve.wait_ge(sm["s_k1"], 10)
                em = em8[:, :].unsqueeze(1).to_broadcast([P, NT, E1])
                nc.vector.tensor_tensor(cand[:, :, :], cand[:, :, :], em, ALU.mult).then_inc(sm["s_rt"], 1)
                dve.wait_ge(sm["s_rt"], 4)
                nc.vector.tensor_reduce(emin[:, :], cand[:, :, :], AX.X, ALU.min).then_inc(sm["s_rt"], 1)
                dve.wait_ge(sm["s_rt"], 5)
                em_w = emin[:, :].unsqueeze(2).to_broadcast([P, NT, E1])
                nc.vector.tensor_tensor(onehot[:, :, :], em, em_w, ALU.is_equal).then_inc(sm["s_oh"], 1)
                nc.vector.tensor_tensor(onehotb[:, :, :], em, em_w, ALU.is_equal).then_inc(sm["s_oh"], 1)
                nc.vector.tensor_copy(smallW[:, :, 0:FC], smallT[:, 0:FC * E1].rearrange("p (e c) -> p e c", c=FC)).then_inc(sm["s_smw"], 1)
                nc.vector.tensor_copy(smallW[:, :, FC], smallT[:, FC * E1:(FC + 1) * E1]).then_inc(sm["s_smw"], 1)
                nc.vector.tensor_copy(smallW[:, :, FC + 1], smallT[:, (FC + 1) * E1:(FC + 2) * E1]).then_inc(sm["s_smw"], 1)

            def route_b(dve):
                n = 5

                def step(ins):
                    nonlocal n
                    n += 1
                    ins.then_inc(sm["s_rt"], 1)
                    dve.wait_ge(sm["s_rt"], n)
                dve.wait_ge(sm["s_rkc"], 1)
                src = rank[:, 1, :, :]
                for k in range(4):
                    sh, dst = 1 << k, cum[:, k % 2, :, :]
                    step(nc.vector.tensor_copy(dst[:, 0:sh, :], src[:, 0:sh, :]))
                    step(nc.vector.tensor_tensor(dst[:, sh:NT, :], src[:, sh:NT, :], src[:, 0:NT - sh, :], ALU.add))
                    src = dst
                count = src[:, NT - 1, :].unsqueeze(2).to_broadcast([P, E1, NT])
                step(nc.vector.tensor_tensor(full[:, :, :], count, m128[:, :].unsqueeze(1).to_broadcast([P, E1, NT]), ALU.is_gt))
                step(nc.vector.tensor_reduce(ctile[:, 0, :], full[:, :, :], AX.X, ALU.add))
                step(nc.vector.tensor_copy(ctile[:, 1, :], ctile[:, 0, :]))
                for e in range(1, E1):
                    step(nc.vector.tensor_tensor(ctile[:, 1, e:e + 1], ctile[:, 1, e:e + 1], ctile[:, 1, e - 1:e], ALU.add))
                step(nc.vector.tensor_tensor(ctile[:, 2, :], ctile[:, 1, :], ctile[:, 0, :], ALU.subtract))
                base = ctile[:, 2, :].unsqueeze(1).to_broadcast([P, NT, E1])
                step(nc.vector.tensor_tensor(cand[:, :, :], src, rank[:, 1, :, :], ALU.subtract))
                step(nc.vector.scalar_tensor_tensor(cand[:, :, :], base, float(P), cand[:, :, :], ALU.mult, ALU.add))
                nc.vector.tensor_tensor(tile_c[:, :, :], ctile[:, 1, :].unsqueeze(1).to_broadcast([P, NSORT, E1]),
                                        iota_j[:, :].unsqueeze(2).to_broadcast([P, NSORT, E1]), ALU.is_le).then_inc(sm["s_te"], 1)
                dve.wait_ge(sm["s_te"], 1)
                nc.vector.tensor_reduce(tile_f[:, :], tile_c[:, :, :], AX.X, ALU.add).then_inc(sm["s_te"], 1)
                dve.wait_ge(sm["s_te"], 2)
                nc.vector.tensor_scalar(tile_e[:, :], tile_f[:, :], float(E1 - 1), None, ALU.min).then_inc(sm["s_te"], 1)
                dve.wait_ge(sm["s_te"], 3)
                nc.vector.tensor_tensor(cand[:, :, :], cand[:, :, :], rank[:, 0, :, :], ALU.add).then_inc(sm["s_te"], 1)
                dve.wait_ge(sm["s_te"], 4)
                nc.vector.tensor_tensor(cand[:, :, :], cand[:, :, :], onehot[:, :, :], ALU.mult).then_inc(sm["s_te"], 1)
                dve.wait_ge(sm["s_te"], 5)
                nc.vector.tensor_reduce(pos_f[:, :], cand[:, :, :], AX.X, ALU.add).then_inc(sm["s_te"], 1)
                dve.wait_ge(sm["s_te"], 6)
                nc.vector.tensor_copy(pos[:, :], pos_f[:, :]).then_inc(sm["s_te"], 1)

            nc.vector.memset(half_off[0:64, :], 0.0).then_inc(sm["s_ones"], 1)
            nc.vector.memset(half_off[64:P, :], float(S)).then_inc(sm["s_ones"], 1)
            so = s_off[:, :].rearrange("p (n two) -> p n two", two=2)
            for h in range(2):
                for c in range(2):
                    nc.vector.memset(so[64 * h:64 * h + 64, :, c], float(T * (2 * c + h))).then_inc(sm["s_ones"], 1)
            for c in range(4):
                dve.wait_ge(s_x[c], 16)
                for t in range(4 * c, 4 * c + 4):
                    nc.vector.bn_stats(stats[:, t, :], x_sb[:, t, :]).then_inc(sm["s_st"], 1)
                ln_rest(0, c, range(4 * c, 4 * c + 4), x_sb, xn)
            dve.wait_ge(sm["s_bload"], 64)
            dve.wait_ge(sm["s_lg"], 1)
            nc.vector.tensor_copy(logits[:, :], pS[:, 0, :]).then_inc(sm["s_lgc"], 1)
            dst = [pS[:, 1, 0:512], pS[:, 1, 512:1024], pM[:, :], pH[:, :]]
            for c in range(NC):
                dve.wait_ge(sm["s_pj"], 3 * c + 3)
                nc.vector.tensor_tensor(v_sb[:, 4 * c:4 * c + 4, :],
                                        dst[(3 * c + 2) % 4].rearrange("p (t d) -> p t d", d=D),
                                        bvo[:, 0:1, :].to_broadcast([P, 4, D]), ALU.add).then_inc(sm["s_pje_v"], 1)

            dve.wait_ge(sm["s_w1load"], 64)
            dve.wait_ge(sm["s_b1load1"], 96)
            for dst_, src_ in ((brow_p, brow_qk[:, :]), (wqp, wq1[:, :]), (wkp, wku[:, 0:P])):
                nc.vector.tensor_copy(dst_[:, :].rearrange("p (g d j) -> p g d j", d=DH, j=GH),
                                      src_.rearrange("p (g j d) -> p g d j", d=DH, j=GH)).then_inc(sm["s_perm"], 1)

            def finish(i):
                dve.wait_ge(sm["s_exp"], i + 1)
                nc.vector.reciprocal(rinv[:, i:i + 1], rsum[:, i:i + 1]).then_inc(sm["s_ri"], 1)
                dve.wait_ge(sm["s_op"], i + 1)
                if i == 0:
                    dve.wait_ge(sm["s_accz"], 16 * NACC)
                    dve.wait_ge(sm["s_xs0"], 32)
                dve.wait_ge(sm["s_ri"], i + 1)
                nc.vector.scalar_tensor_tensor(s_sb[:, i, :], pH[:, 0:P], rinv[:, i:i + 1], bvo[:, 1, :],
                                               ALU.mult, ALU.add).then_inc(sm["s_fin"], 1)

            def rowmax(i):
                dve.wait_ge(sm["s_S"], i + 1)
                nc.vector.tensor_reduce(nmax[:, i:i + 1], pS[:, i % 2, :], AX.X, ALU.max, negate=True).then_inc(sm["s_max"], 1)
                dve.wait_ge(sm["s_max"], i + 1)
                nc.vector.tensor_scalar(nbias[:, i:i + 1], nmax[:, i:i + 1], SC0, None, ALU.mult).then_inc(sm["s_nm"], 1)

            def top_round(r):
                if r == 0:
                    dve.wait_ge(sm["s_lgc"], 1)
                else:
                    dve.wait_ge(sm["s_t3"], r)
                r8 = slice(8 * r, 8 * r + 8)
                nc.vector.max(top_v[:, r8], logits[:, :]).then_inc(sm["s_t1"], 1)
                dve.wait_ge(sm["s_t1"], r + 1)
                nc.vector.max_index(top_i[:, r8], top_v[:, r8], logits[:, :]).then_inc(sm["s_t2"], 1)
                nc.vector.match_replace(logits[:, :], top_v[:, r8], logits[:, :], -3.0e38).then_inc(sm["s_t3"], 1)

            def merge():
                dve.wait_ge(sm["s_t2"], CAP // 8)
                dve.wait_ge(sm["s_ones"], 6)
                nc.vector.tensor_scalar(top_f[:, :], top_i[:, :], half_off[:, 0:1], None, ALU.add).then_inc(sm["s_tf"], 1)
                dve.wait_ge(sm["s_tf"], 1)
                dve.wait_ge(sm["s_hb"], 32)
                lo, hi = top_v[0:E0, :], hi_v[:, ::-1]
                lo_i, hi_i = top_f[0:E0, :], hi_f[:, ::-1]
                nc.vector.tensor_tensor(slot_v[:, :], lo, hi, ALU.max).then_inc(sm["s_sl"], 1)
                nc.vector.tensor_tensor(slot_m[:, :], lo, hi, ALU.is_ge).then_inc(sm["s_sl"], 1)
                nc.vector.tensor_tensor(slot_d[:, :], lo_i, hi_i, ALU.subtract).then_inc(sm["s_sl"], 1)
                dve.wait_ge(sm["s_sl"], 3)
                nc.vector.tensor_reduce(slot_s[:, 0:1], slot_v[:, :], AX.X, ALU.max, negate=True).then_inc(sm["s_wn"], 1)
                nc.vector.tensor_tensor(slot_d[:, :], slot_d[:, :], slot_m[:, :], ALU.mult).then_inc(sm["s_sl"], 1)
                dve.wait_ge(sm["s_sl"], 4)
                for j in range(2):
                    nc.vector.tensor_tensor(slots[:, 2 + j, :], slot_d[:, :], hi_i, ALU.add).then_inc(sm["s_sl"], 1)

            def weights():
                dve.wait_ge(sm["s_we"], 1)
                nc.vector.reciprocal(slot_s[:, 2:3], slot_s[:, 1:2]).then_inc(sm["s_wn"], 1)
                dve.wait_ge(sm["s_wn"], 2)
                nc.vector.tensor_scalar(slots[:, 0:2, :], slot_m[:, :].unsqueeze(1).to_broadcast([E0, 2, CAP]),
                                        slot_s[:, 2:3], None, ALU.mult).then_inc(sm["s_sl"], 1)

            def columns():
                dve.wait_ge(sm["s_ctr"], 1)
                for h in range(2):
                    part = slice(64 * h, 64 * h + 64)
                    for k, dst_ in ((0, w_col), (1, i_col)):
                        src = pM[part, 256 + E0 * k:256 + E0 * k + E0].rearrange("p (n two) -> p n two", two=2)
                        nc.vector.tensor_copy(dst_[part, :], src[:, :, h]).then_inc(sm["s_cc"], 1)
                dve.wait_ge(sm["s_cc"], 4)
                nc.vector.tensor_copy(g_idx[:, :], i_col[:, :]).then_inc(sm["s_so"], 1)
                nc.vector.tensor_tensor(s_idx[:, :], i_col[:, :], s_off[:, :], ALU.add).then_inc(sm["s_so"], 1)

            for i in range(NT):
                rowmax(i)
                if i >= 2:
                    finish(i - 2)
                if i < CAP // 8:
                    top_round(i)
                if i == CAP // 8:
                    merge()
                if i == CAP // 8 + 2:
                    weights()
            finish(NT - 2)
            finish(NT - 1)
            columns()

            def lift(p):
                dve.wait_ge(sm["s_xgt"], p + 1)
                if p >= 2:
                    dve.wait_ge(sm["s_h"], p - 1)
                nc.vector.tensor_copy(xgT[:, p % 2, :], pT[:, p % 2, 0:P]).then_inc(sm["s_xge"], 1)

            def scale_y(p):
                dve.wait_ge(sm["s_y"], p + 1)
                if p >= 4:
                    dve.wait_ge(s_sc[p % 2], 16 * (p // 2 - 1))
                nc.vector.tensor_scalar(y_sb[:, p % 4, :], (pM, pH)[p % 2][:, 0:D], w_col[:, p:p + 1], None,
                                        ALU.mult).then_inc(sm["s_ysc"], 1)

            lift(0)
            for p in range(NP):
                dve.wait_ge(sm["s_h"], p + 1)
                if p >= 2:
                    dve.wait_ge(sm["s_gelu"], p - 1)
                nc.vector.tensor_tensor(hb[:, p % 2, :].rearrange("p (n c) -> p n c", c=64),
                                        pS[:, p % 2, 0:512].rearrange("p (n c) -> p n c", c=64),
                                        b1T[:, 8 * p:8 * p + 8].unsqueeze(2).to_broadcast([P, 8, 64]),
                                        ALU.add).then_inc(sm["s_hbias"], 1)
                if p + 1 < NP:
                    lift(p + 1)
                if p:
                    scale_y(p - 1)
            scale_y(NP - 1)
            dve.wait_ge(sm["s_xrows"], 64)
            for b in range(B):
                for c in (2 * b, 2 * b + 1):
                    t4 = slice(4 * c, 4 * c + 4)
                    dve.wait_ge(s_x[c], 16 + 16 * NACC)
                    nc.vector.tensor_tensor(accs[:, 0:2, t4, :], accs[:, 0:2, t4, :], accs[:, 2:4, t4, :], ALU.add).then_inc(sm["s_sum"], 1)
                    dve.wait_ge(sm["s_sum"], 2 * c + 1)
                    nc.vector.tensor_tensor(accs[:, 0, t4, :], accs[:, 0, t4, :], accs[:, 1, t4, :], ALU.add).then_inc(sm["s_sum"], 1)
                for c in (2 * b, 2 * b + 1):
                    t4 = slice(4 * c, 4 * c + 4)
                    dve.wait_ge(sm["s_silu"], c + 1)
                    nc.vector.tensor_tensor(s_sb[:, t4, :], s_sb[:, t4, :], accs[:, 1, t4, :], ALU.mult).then_inc(sm["s_x1"], 1)
                    dve.wait_ge(sm["s_x1"], 2 * c + 1)
                    nc.vector.tensor_tensor(x_sb[:, t4, :], x_sb[:, t4, :], s_sb[:, t4, :], ALU.add).then_inc(sm["s_x1"], 1)
                    dve.wait_ge(sm["s_x1"], 2 * c + 2)
                    for t in range(4 * c, 4 * c + 4):
                        nc.vector.bn_stats(stats[:, t, :], x_sb[:, t, :]).then_inc(sm["s_st"], 1)
                ln_rest(1, 4 + b, range(b * BT, b * BT + BT), x_sb, xn)

            def join_latents(c):
                dve.wait_ge(sm["s_lae"], 2 * c + 2)
                half = slice(512 * (c % 2), 512 * (c % 2) + 512)
                nc.vector.tensor_tensor(latT[:, 512 * c:512 * c + 512], latA[:, half], latB[:, half], ALU.add).then_inc(sm["s_lat"], 1)

            for b in range(B):
                for c in (2 * b, 2 * b + 1):
                    join_latents(c)
                bs = slice(b * S, b * S + S)
                for st in range(2):
                    for side in range(2):
                        dve.wait_ge(sm["s_cp"], 6 * b + 2 * st + side + 1)
                        full_ = qk_mem[:, side, bs]
                        nc.vector.tensor_tensor(full_, full_, parts[side][:, st, bs], ALU.subtract).then_inc(sm["s_sub"], 1)
            dve.wait_ge(sm["s_af"], 1)
            nc.vector.tensor_copy(aff[:, :, :].rearrange("p t e -> p (t e)"), pM[:, 0:NT * E1]).then_inc(sm["s_rt"], 1)
            for c in range(NC):
                dve.wait_ge(sm["s_vv"], c + 1)
                nc.vector.tensor_tensor(v_sb[:, 4 * c:4 * c + 4, :], (pM, pH)[c % 2][:, :].rearrange("p (t d) -> p t d", d=D),
                                        brow1[:, 0:1, :].to_broadcast([P, 4, D]), ALU.add).then_inc(sm["s_v1e"], 1)
                if c == 0:
                    route_a(dve)
            dve.wait_ge(sm["s_rk"], 1)
            nc.vector.tensor_copy(rank[:, :, :, :].rearrange("p a t e -> p (a t e)"), pT[:, 0, 0:2 * NT * E1]).then_inc(sm["s_rkc"], 1)
            for t in range(NT):
                nc.vector.bn_stats(stats[:, t, :], xn[:, t, :]).then_inc(sm["s_st"], 1)
            ln_rest(2, 6, range(NT), xn, s_sb)
            route_b(dve)

            def unit(u):
                g = u // NU
                j, heads, qt = UNITS[u % NU]
                dve.wait_ge(sm["s_u"], u + 1)
                if u % NU == 0 and g:
                    dve.wait_ge(sm["s_msp"], 5 * g)
                keys = (qt + 1) * P
                if heads == 2:
                    nc.vector.tensor_reduce(negm[:, j:j + 2, qt],
                                            pS[:, u % 2, :].rearrange("p (a k) -> p a k", a=2)[:, :, 0:keys],
                                            AX.X, ALU.max, negate=True).then_inc(sm["s_um"], 1)
                else:
                    nc.vector.tensor_reduce(negm[:, j, qt:qt + 1], pS[:, u % 2, 0:keys],
                                            AX.X, ALU.max, negate=True).then_inc(sm["s_um"], 1)
                if u % NU == NU - 1:
                    split_m(g)

            def split_m(g):
                dve.wait_ge(sm["s_um"], NU * (g + 1))
                if g:
                    dve.wait_ge(sm["s_mt"], g)
                nc.vector.tensor_copy(mparts[:, 0, :, :], negm[:, :, :]).then_inc(sm["s_msp"], 1)
                dve.wait_ge(sm["s_msp"], 5 * g + 1)
                nc.vector.tensor_tensor(negr[:, :, :], negm[:, :, :], mparts[:, 0, :, :], ALU.subtract).then_inc(sm["s_msp"], 1)
                dve.wait_ge(sm["s_msp"], 5 * g + 2)
                nc.vector.tensor_copy(mparts[:, 1, :, :], negr[:, :, :]).then_inc(sm["s_msp"], 1)
                dve.wait_ge(sm["s_msp"], 5 * g + 3)
                nc.vector.tensor_tensor(negr[:, :, :], negr[:, :, :], mparts[:, 1, :, :], ALU.subtract).then_inc(sm["s_msp"], 1)
                dve.wait_ge(sm["s_msp"], 5 * g + 4)
                nc.vector.tensor_copy(mparts[:, 2, :, :], negr[:, :, :]).then_inc(sm["s_msp"], 1)

            def rows_m(g):
                dve.wait_ge(sm["s_mt"], g + 1)
                if g:
                    dve.wait_ge(sm["s_mscr"], 16 * g)
                nc.vector.tensor_copy(mrows[:, :], pH[:, :].bitcast(bf16)[0:3 * GH * BT, 0:P]).then_inc(sm["s_mte"], 1)

            def fetch_w(j):
                if j >= 2:
                    dve.wait_ge(sm["s_fc"], j - 1)
                    dve.wait_ge(sm["s_fae"], j - 1)
                    dve.wait_ge(sm["s_fbe"], j - 1)
                    dve.wait_ge(sm["s_fce"], j - 1)
                if j == 0:
                    dve.wait_ge(sm["s_te"], 3)
                    dve.wait_ge(sm["s_pos"], 16 * NT)
                    dve.wait_ge(sm["s_wall"], 16 * (2 + E1))
                    dve.wait_ge(sm["s_smw"], 3)
                e = dve.value_load(tile_e[0:1, j:j + 1], min_val=0, max_val=E1 - 1)
                nc.vector.tensor_copy(w_tile[:, j % 2, :], wall[:, bass.ds(e, 1), 0:2 * F1].rearrange("p a n -> p (a n)")).then_inc(sm["s_wj"], 1)
                nc.vector.tensor_copy(b2_tile[:, j % 2, :], wall[:, bass.ds(e, 1), 2 * F1:2 * F1 + D].rearrange("p a n -> p (a n)")).then_inc(sm["s_wj"], 1)
                nc.vector.tensor_copy(s_tile[:, j % 2, :], smallW[:, bass.ds(e, 1), :].rearrange("p a n -> p (a n)")).then_inc(sm["s_wj"], 1)

            def add_bias(c):
                dve.wait_ge(sm["s_pj1"], c + 1)
                if c == 0:
                    dve.wait_ge(sm["s_fc"], NSORT)
                nc.vector.tensor_tensor(s_fin[:, 4 * c:4 * c + 4, :], pH[:, :].rearrange("p (t d) -> p t d", d=D),
                                        brow1[:, 1:2, :].to_broadcast([P, 4, D]), ALU.add).then_inc(sm["s_fin1"], 1)

            def weigh_experts():
                dve.wait_ge(sm["s_al"], 1)
                nc.vector.tensor_scalar(alpha[:, 1, :], alpha[:, 0, :], 1.0, None, ALU.add).then_inc(sm["s_als"], 1)
                dve.wait_ge(sm["s_als"], 1)
                nc.vector.reciprocal(alpha[:, 2, :], alpha[:, 1, :]).then_inc(sm["s_als"], 1)
                dve.wait_ge(sm["s_als"], 2)
                dve.wait_ge(sm["s_g1"], 16 * NT)
                for t in range(NT):
                    nc.vector.scalar_tensor_tensor(f_sb[:, t, :], f_sb[:, t, :], alpha[:, 2, t:t + 1], xn[:, t, :],
                                                   ALU.mult, ALU.add).then_inc(sm["s_als"], 1)

            def normalise(r):
                g, qc = r // 2, r % 2
                b, g4 = g // (NG // B), g % (NG // B)
                dve.wait_ge(sm["s_tr1"], r + 1)
                acc = pM[:, :].rearrange("p (t j c) -> p t j c", t=4, j=GH)
                nc.vector.reciprocal(rden[:, :, :], acc[:, :, :, DH]).then_inc(sm["s_rd1"], 1)
                dve.wait_ge(sm["s_rd1"], r + 1)
                t0 = b * BT + 4 * qc
                o = o_sb[:, t0:t0 + 4, g4 * GH * DH:(g4 + 1) * GH * DH].rearrange("p t (j d) -> p t j d", d=DH)
                nc.vector.tensor_tensor(o, acc[:, :, :, 0:DH], rden[:, :, :].unsqueeze(3).to_broadcast([P, 4, GH, DH]),
                                        ALU.mult).then_inc(sm["s_nrm"], 1)

            for u in range(NU):
                unit(u)
            rows_m(0)
            for u in range(NU, AHEAD):
                unit(u)
            dve.wait_ge(sm["s_scr"], 16 * 12)
            for n in range(NG * NSTEP + 2):
                if AHEAD + 2 * n < NG * NU:
                    unit(AHEAD + 2 * n)
                if n >= 2 and ends(n - 2) >= 0:
                    normalise(ends(n - 2))
                if AHEAD + 2 * n + 1 < NG * NU:
                    unit(AHEAD + 2 * n + 1)
                if (n + 4) % NSTEP == 0 and (n + 4) // NSTEP < NG:
                    rows_m((n + 4) // NSTEP)
                if n == FFN0 - 2:
                    fetch_w(0)
                if n == FFN0 - 1:
                    fetch_w(1)
                j, sub = ffn_part(n)
                if sub == 0 and 1 <= j and j + 1 < NSORT:
                    fetch_w(j + 1)
                if sub == 1:
                    dve.wait_ge(sm["s_fb"], j + 1)
                    if j >= 2:
                        dve.wait_ge(sm["s_fc"], j - 1)
                    nc.vector.tensor_tensor(hs[:, j % 2, :].rearrange("p (c t) -> p c t", c=FC),
                                            pH[:, :].rearrange("p (c t) -> p c t", c=FC),
                                            s_tile[:, j % 2, 0:FC].unsqueeze(2).to_broadcast([P, FC, P]),
                                            ALU.add).then_inc(sm["s_fbe"], 1)
                if sub == 2:
                    dve.wait_ge(sm["s_fc"], j + 1)
                    if j >= 2:
                        dve.wait_ge(s_ysd[j % 2], 16 * (j // 2))
                    nc.vector.tensor_tensor(ys_sb[:, j % 2, :], pH[:, 0:D], b2_tile[:, j % 2, :],
                                            ALU.add).then_inc(sm["s_fce"], 1)
                for c in range(NC // 2):
                    if n == OUT0 + 4 * c + 1:
                        add_bias(c)
                if n == NG * NSTEP:
                    weigh_experts()
            for c in range(NC // 2, NC):
                add_bias(c)
            for c in range(NC):
                t4 = slice(4 * c, 4 * c + 4)
                dve.wait_ge(sm["s_gate"], c + 1)
                nc.vector.tensor_tensor(s_fin[:, t4, :], s_fin[:, t4, :], f_sb[:, t4, :], ALU.mult).then_inc(sm["s_fin2"], 1)
                dve.wait_ge(sm["s_fin2"], 2 * c + 1)
                nc.vector.tensor_tensor(x_sb[:, t4, :], x_sb[:, t4, :], s_fin[:, t4, :], ALU.add).then_inc(sm["s_fin2"], 1)

        @block.scalar
        def _(act):
            for c in range(4):
                act.wait_ge(sm["s_ve"], c + 1)
                nc.scalar.activation(sdev[:, 4 * c:4 * c + 4], var_e[:, 4 * c:4 * c + 4], ACT.Sqrt).then_inc(sm["s_sd"], 1)
            act.wait_ge(sm["s_wtr"], 1)
            nc.scalar.copy(w_T[:, :, :].rearrange("p a b -> p (a b)"), pT[:, 0, :]).then_inc(sm["s_wt"], 1)
            act.wait_ge(sm["s_wtr"], 2)
            act.wait_ge(sm["s_zero"], 3)
            nc.scalar.copy(wr_T[:, 0:E0], pM[:, 0:E0]).then_inc(sm["s_wt"], 1)
            nc.scalar.copy(b1T[:, :], pM[:, 64:64 + E0 * NS]).then_inc(sm["s_wt"], 1)
            nc.scalar.copy(cenT[:, :], pM[:, 256:256 + E1]).then_inc(sm["s_wt"], 1)
            nc.scalar.copy(smallT[:, :], pM[:, 272:272 + 6 * E1]).then_inc(sm["s_wt"], 1)
            for c in range(NC):
                act.wait_ge(sm["s_xtr"], c + 1)
                nc.scalar.copy(xnT[:, c * 512:c * 512 + 512], pT[:, (c + 1) % 2, :]).then_inc(sm["s_xt"], 1)
            act.wait_ge(sm["s_bload"], 64)
            dst = [pS[:, 1, 0:512], pS[:, 1, 512:1024], pM[:, :], pH[:, :]]
            for c in range(NC):
                for j in range(2):
                    n = 3 * c + j
                    act.wait_ge(sm["s_pj"], n + 1)
                    nc.scalar.activation((qT, kT)[j][:, c * 512:c * 512 + 512], dst[n % 4], ACT.Identity,
                                         bias=bqk[:, j:j + 1]).then_inc(sm["s_pje_a"], 1)

            def exps(i):
                act.wait_ge(sm["s_nm"], i + 1)
                if i >= 2:
                    act.wait_ge(sm["s_tr"], 2 * (i - 1))
                nc.scalar.activation(probs[:, i % 2, :], pS[:, i % 2, :], ACT.Exp, bias=nbias[:, i:i + 1], scale=SC0,
                                     accum_out=rsum[:, i:i + 1]).then_inc(sm["s_exp"], 1)

            def move_out(i):
                act.wait_ge(sm["s_pv"], i + 1)
                if i:
                    act.wait_ge(sm["s_op"], i)
                nc.scalar.copy(oT[:, :], pM[:, 0:P]).then_inc(sm["s_oT"], 1)

            for i in range(NT):
                exps(i)
                if i:
                    move_out(i - 1)
                for h in range(2):
                    act.wait_ge(sm["s_tr"], 2 * i + h + 1)
                    if i >= 2:
                        act.wait_ge(sm["s_pv"], i - 1)
                    nc.scalar.copy(probsT[:, i % 2, h * 512:h * 512 + 512], pT[:, h, :]).then_inc(sm["s_ev"], 1)
                if i == CAP // 8 + 1:
                    act.wait_ge(sm["s_wn"], 1)
                    nc.scalar.activation(slot_m[:, :], slot_v[:, :], ACT.Exp, bias=slot_s[:, 0:1],
                                         accum_out=slot_s[:, 1:2]).then_inc(sm["s_we"], 1)
            move_out(NT - 1)
            for p in range(NP):
                act.wait_ge(sm["s_hbias"], p + 1)
                if p >= 2:
                    act.wait_ge(sm["s_y"], p - 1)
                nc.scalar.activation(hg[:, p % 2, :], hb[:, p % 2, :], ACT.Gelu).then_inc(sm["s_gelu"], 1)

            for b in range(B):
                for c in (2 * b, 2 * b + 1):
                    t4 = slice(4 * c, 4 * c + 4)
                    act.wait_ge(sm["s_sum"], 2 * c + 2)
                    nc.scalar.activation(accs[:, 1, t4, :], accs[:, 0, t4, :], ACT.Silu).then_inc(sm["s_silu"], 1)
                act.wait_ge(sm["s_ve"], 4 + b + 1)
                bt = slice(b * BT, b * BT + BT)
                nc.scalar.activation(sdev[:, bt], var_e[:, bt], ACT.Sqrt).then_inc(sm["s_sd"], 1)
                if b == 0:
                    act.wait_ge(sm["s_btr"], 1)
                    nc.scalar.copy(bcol1[:, :], pM[:, 0:2]).then_inc(sm["s_bte"], 1)
                    act.wait_ge(sm["s_bte"], 1)
            for b in range(B):
                for c in (2 * b, 2 * b + 1):
                    act.wait_ge(sm["s_xtr"], NC + c + 1)
                    nc.scalar.copy(xnT[:, c * 512:c * 512 + 512], pT[:, c % 2, :]).then_inc(sm["s_xt"], 1)
                for c in (2 * b, 2 * b + 1):
                    act.wait_ge(sm["s_q1"], c + 1)
                    nc.scalar.activation(qT[:, c * 512:c * 512 + 512], pS[:, 0, (c % 2) * 512:(c % 2) * 512 + 512],
                                         ACT.Identity, bias=bcol1[:, 0:1]).then_inc(sm["s_q1e"], 1)
                for c in (2 * b, 2 * b + 1):
                    act.wait_ge(sm["s_la"], c + 1)
                    if b:
                        act.wait_ge(sm["s_lat"], c - 1)
                    for h in range(2):
                        nc.scalar.activation((latA, latB)[h][:, (c % 2) * 512:(c % 2) * 512 + 512], pT[0:LAT, h, :], ACT.Gelu,
                                             bias=bkd[:, h:h + 1]).then_inc(sm["s_lae"], 1)
                for c in (2 * b, 2 * b + 1):
                    act.wait_ge(sm["s_kk"], c + 1)
                    nc.scalar.activation(kT[:, c * 512:c * 512 + 512], pS[:, 1, (c % 2) * 512:(c % 2) * 512 + 512],
                                         ACT.Identity, bias=bcol1[:, 1:2]).then_inc(sm["s_kke"], 1)
                act.wait_ge(sm["s_q1e"], 2 * b + 2)
                act.wait_ge(sm["s_kke"], 2 * b + 2)
                bs = slice(b * S, b * S + S)
                for st in range(3):
                    for side in range(2):
                        if st:
                            act.wait_ge(sm["s_sub"], 4 * b + 2 * (st - 1) + side + 1)
                        nc.scalar.copy(parts[side][:, st, bs], qk_mem[:, side, bs]).then_inc(sm["s_cp"], 1)
            act.wait_ge(sm["s_ve"], 7)
            nc.scalar.activation(sdev[:, :], var_e[:, :], ACT.Sqrt).then_inc(sm["s_sd"], 1)
            act.wait_ge(sm["s_oh"], 2)
            nc.scalar.activation(alpha[:, 0, :], amax[:, :], ACT.Exp, scale=-1.0).then_inc(sm["s_al"], 1)

            def exps1(n, j):
                qc, kt, q0, cols = STEPS[n % NSTEP]
                act.wait_ge(sm["s_s1"], GH * n + j + 1)
                if n >= 2:
                    act.wait_ge(sm["s_pv1"], n - 1)
                nc.scalar.activation(pr1[:, n % 2, j, 0:cols], pT[:, j % 2, 0:cols], ACT.Exp, scale=SC1).then_inc(sm["s_e1"], 1)

            def move_heads(c):
                act.wait_ge(sm["s_ot"], c + 1)
                nc.scalar.copy(hs[:, c % 2, :], pH[:, :]).then_inc(sm["s_ote"], 1)

            for n in range(NG * NSTEP + 2):
                if n < NG * NSTEP:
                    exps1(n, 0)
                    exps1(n, 1)
                r = ends(n - 1)
                if r >= 0:
                    act.wait_ge(sm["s_pv1"], n)
                    if r >= 2:
                        act.wait_ge(sm["s_tr1"], r - 1)
                    nc.scalar.copy(acc_sb[:, r % 2, :], pM[:, :]).then_inc(sm["s_ace"], 1)
                if n < NG * NSTEP:
                    exps1(n, 2)
                    exps1(n, 3)
                for c in range(NC // 2):
                    if n == OUT0 + 4 * c:
                        move_heads(c)
                j, sub = ffn_part(n)
                if sub == 0:
                    act.wait_ge(sm["s_fa"], j + 1)
                    act.wait_ge(sm["s_wj"], 3 * j + 3)
                    if j:
                        act.wait_ge(sm["s_fb"], j)
                    nc.scalar.activation(xlT[:, :], pH[:, 0:P], ACT.Identity, bias=s_tile[:, j % 2, FC + 1:FC + 2],
                                         scale=s_tile[:, j % 2, FC:FC + 1]).then_inc(sm["s_fae"], 1)
                if sub == 1:
                    act.wait_ge(sm["s_fbe"], j + 1)
                    nc.scalar.activation(hs[:, j % 2, :], hs[:, j % 2, :], ACT.Relu).then_inc(sm["s_relu"], 1)
            for c in range(NC // 2, NC):
                move_heads(c)
            for c in range(NC):
                t4 = slice(4 * c, 4 * c + 4)
                act.wait_ge(sm["s_als"], 2 + 4 * c + 4)
                nc.scalar.activation(f_sb[:, t4, :], f_sb[:, t4, :], ACT.Silu).then_inc(sm["s_gate"], 1)


_INS = ['L0_attn_x', 'L0_attn_w_q', 'L0_attn_b_q', 'L0_attn_w_k', 'L0_attn_b_k', 'L0_attn_w_v', 'L0_attn_b_v',
        'L0_attn_w_out', 'L0_attn_b_out', 'L0_ffn_Wr', 'L0_ffn_W1', 'L0_ffn_b1', 'L0_ffn_W2', 'L0_ffn_b2']
_INS1 = ['L1_attn_Wq', 'L1_attn_bq', 'L1_attn_Wkd', 'L1_attn_bkd', 'L1_attn_Wku', 'L1_attn_bku', 'L1_attn_Wo',
         'L1_attn_bo', 'L1_ffn_centroids', 'L1_ffn_ln_g', 'L1_ffn_ln_b', 'L1_ffn_w1', 'L1_ffn_b1', 'L1_ffn_w2',
         'L1_ffn_b2']


def kernel(**inputs):
    import numpy as _np
    import concourse.bacc as _bacc
    from concourse import mybir as _mybir
    from concourse.bass_utils import run_bass_kernel_spmd as _run
    nc = _bacc.Bacc("TRN2", target_bir_lowering=False, num_devices=1)
    arrays, aps = {}, {}
    for name in _INS + _INS1:
        v = _np.ascontiguousarray(inputs[name])
        arrays[f"in_{name}_dram"] = v
        aps[name] = nc.dram_tensor(f"in_{name}_dram", v.shape, _mybir.dt.from_np(v.dtype), kind="ExternalInput").ap()
    o = nc.dram_tensor("out_0_dram", (2, 1024, 128), _mybir.dt.float32, kind="ExternalOutput").ap()
    build(nc, aps, o)
    r = _run(nc, [arrays], core_ids=[0])
    return r.results[0]["out_0_dram"]
```

```python
import concourse.bass as bass
from concourse import mybir
from contextlib import ExitStack


def build(nc, a, out):
    fp32 = mybir.dt.float32
    bf16 = mybir.dt.bfloat16
    u32 = mybir.dt.uint32
    ALU = mybir.AluOpType
    ACT = mybir.ActivationFunctionType
    AX = mybir.AxisListType

    x_dram, wr_dram = a["L0_attn_x"], a["L0_ffn_Wr"]
    B, S, D = x_dram.shape
    P = 128
    T = B * S
    NT = T // P
    BT = S // P
    E0 = wr_dram.shape[0]
    NS, KY = a["L0_ffn_W2"].shape[1], a["L0_ffn_W2"].shape[3]
    CAP = int(1.5 * T / E0)
    NP = E0 // 2
    RING = 12
    EPS = 1e-5
    SC0 = float(D) ** -0.5
    NC = T // 512
    H1, DH = 16, 8
    SC1 = float(DH) ** -0.5
    E1, _, F1 = a["L1_ffn_w1"].shape
    FC = F1 // P
    LAT = a["L1_attn_Wku"].shape[0]
    GH = 4
    NG = B * H1 // GH
    KQ = 72
    KM = KQ + 3
    NSORT = NT + E1 - 1
    NEG = -1.0e30
    STEPS = []
    for qc in range(S // 512):
        for kt in range(4 * qc + 4):
            q0 = max(kt * P, qc * 512)
            STEPS.append((qc, kt, q0, (qc + 1) * 512 - q0))
    NSTEP = len(STEPS)
    UNITS = []
    for u in range(8):
        UNITS += [(u // 2, 1, 4 + 2 * (u % 2)), (u // 2, 1, 5 + 2 * (u % 2)), (2 * (u // 4), 2, u % 4)]
    NU = len(UNITS)
    SLOT_STEP = 12
    AHEAD = NU + 8
    FFN0 = 13
    OUT0 = FFN0 + 3 * NSORT + 1
    OUTS = [OUT0, OUT0 + 3, NG * NSTEP - 6]

    def gathered(n):
        m = sum(1 if STEPS[i % NSTEP][2] == STEPS[i % NSTEP][1] * P else 2 for i in range(OUT0 + 1, n))
        return min(NT, m)

    def units_before(n):
        return min(NG * NU, NU + 2 + 3 * n, AHEAD + 2 * n)

    ctx = ExitStack()
    with ctx:
        def sb(name, shape, dt=fp32):
            return ctx.enter_context(nc.sbuf_tensor(name, shape, dt))

        def pb(name, shape, dt=fp32):
            return ctx.enter_context(nc.psum_tensor(name, shape, dt))

        def sem(name):
            return ctx.enter_context(nc.semaphore(name))

        xn_rows = nc.dram_tensor("xn_rows", [T, D], fp32, kind="Internal").ap()
        NACC = 4
        acc_rows = nc.dram_tensor("acc_rows", [NACC * T, D], fp32, kind="Internal").ap()
        q_scr = nc.dram_tensor("q_scr", [B, 3, NG // B, DH, GH * S], bf16, kind="Internal").ap()
        k_scr = nc.dram_tensor("k_scr", [B, 3, NG // B, DH, GH * S], bf16, kind="Internal").ap()
        m_scr = nc.dram_tensor("m_scr", [NG, 3 * GH * BT, P], bf16, kind="Internal").ap()
        xs_rows = nc.dram_tensor("xs_rows", [NSORT * P, D], fp32, kind="Internal").ap()
        ys_rows = nc.dram_tensor("ys_rows", [NSORT * P, D], fp32, kind="Internal").ap()

        ident = sb("ident", [P, P])
        x_sb = sb("x_sb", [P, NT, D])
        xn = sb("xn", [P, NT, D])
        xnT = sb("xnT", [P, T])
        qk_mem = sb("qk_mem", [P, 2, T])
        qT, kT = qk_mem[:, 0, :], qk_mem[:, 1, :]
        v_sb = sb("v_sb", [P, NT, D])
        s_sb = sb("s_sb", [P, NT, D])
        stats = sb("stats", [P, NT, 6])
        mv = sb("mv", [P, NT, 2])
        rstd = sb("rstd", [P, NT])
        var_e = sb("var_e", [P, NT])
        sdev = sb("sdev", [P, NT])
        newt = sb("newt", [P, NT])
        w_in = sb("w_in", [P, 4, P])
        w_T = sb("w_T", [P, 4, P])
        wr_in = sb("wr_in", [E0, D])
        wr_T = sb("wr_T", [P, 64])
        bqk = sb("bqk", [P, 2])
        bvo = sb("bvo", [P, 2, D])
        zeros = s_sb
        mem1 = sb("mem1", [P, E1 * (2 * F1 + D)])
        logits = mem1[:, 0:S]
        top_v = sb("top_v", [P, CAP])
        top_i = sb("top_i", [P, CAP], u32)
        top_f = sb("top_f", [P, CAP])
        half_off = sb("half_off", [P, 1])
        hi_v = sb("hi_v", [E0, CAP])
        hi_f = sb("hi_f", [E0, CAP])
        slot_v = sb("slot_v", [E0, CAP])
        slot_m = sb("slot_m", [E0, CAP])
        slot_d = sb("slot_d", [E0, CAP])
        slot_s = sb("slot_s", [E0, 4])
        slots = sb("slots", [E0, 4, CAP])
        w_col = sb("w_col", [P, NP])
        i_col = sb("i_col", [P, NP])
        s_off = sb("s_off", [P, NP])
        g_idx = sb("g_idx", [P, NP], u32)
        s_idx = sb("s_idx", [P, NP], u32)
        probs = mem1[:, S:3 * S].rearrange("p (a s) -> p a s", a=2)
        probsT = mem1[:, 3 * S:5 * S].rearrange("p (a s) -> p a s", a=2)
        nmax = sb("nmax", [P, NT])
        nbias = sb("nbias", [P, NT])
        rsum = sb("rsum", [P, NT])
        rinv = sb("rinv", [P, NT])
        bvT = sb("bvT", [P, P])
        w_vo = w_in[:, 0, :]
        w1r = sb("w1r", [P, RING, 2 * NS, P])
        w2s = sb("w2s", [P, E0 * NS, KY])
        b1_in = sb("b1_in", [96, 2, P])
        b1T = sb("b1T", [P, E0 * NS])
        pairind = sb("pairind", [2, P])
        b2p = mem1[0:2, S:S + NP * D].rearrange("p (n d) -> p n d", d=D)
        xg = mem1[:, 5 * S:5 * S + NP * D].rearrange("p (n d) -> p n d", d=D)
        xgT = sb("xgT", [P, 2, P])
        hb = sb("hb", [P, 2, 512])
        hg = sb("hg", [P, 2, 512])
        y_sb = sb("y_sb", [P, 4, D])
        w1r_flat = w1r[:, :, :, :].rearrange("p a b c -> p (a b c)")
        w2s_flat = w2s[:, :, :].rearrange("p a b -> p (a b)")
        accs = w1r_flat[:, 0:NACC * T].rearrange("p (a t d) -> p a t d", a=NACC, d=D)
        identb = sb("identb", [P, P], bf16)
        causal = sb("causal", [P, P], bf16)
        before = sb("before", [P, P], bf16)
        onesb = sb("onesb", [P, P], bf16)
        wq1 = sb("wq1", [P, P])
        wkd = sb("wkd", [P, 2 * LAT])
        wku = sb("wku", [LAT, 2 * P])
        wo1 = sb("wo1", [P, P])
        brow_qk = sb("brow_qk", [2, P])
        brow_p = sb("brow_p", [2, P])
        wqp = sb("wqp", [P, P])
        wkp = sb("wkp", [LAT, P])
        bcol1 = sb("bcol1", [P, 2])
        bkd = sb("bkd", [LAT, 2])
        brow1 = sb("brow1", [P, 2, D])
        cen_in = sb("cen_in", [E1, D])
        cenT = sb("cenT", [P, E1])
        small_in = sb("small_in", [6 * E1, D])
        smallT = sb("smallT", [P, 6 * E1])
        wall = mem1[:, :].rearrange("p (e n) -> p e n", e=E1)
        w_tile = s_sb[:, :, :].rearrange("p t d -> p (t d)").rearrange("p (a n) -> p a n", a=2)
        b2_tile = sb("b2_tile", [P, 2, D])
        s_tile = sb("s_tile", [P, 2, 6])
        latA = hb[0:LAT, :, :].rearrange("p a n -> p (a n)")
        latB = hg[0:LAT, :, :].rearrange("p a n -> p (a n)")
        latT = w1r_flat[0:LAT, NACC * T:NACC * T + T]
        parts_mem = w2s_flat.bitcast(bf16)
        parts = [parts_mem[:, 3 * T * i:3 * T * i + 3 * T].rearrange("p (a t) -> p a t", a=3) for i in range(2)]
        stack_mem = w1r_flat.bitcast(bf16)
        SM = GH * S

        def stack(side, g):
            o = (2 * (g % 3) + side) * SM
            return stack_mem[:, o:o + SM].rearrange("p (j t) -> p j t", j=GH)
        pr1 = qk_mem[:, :, :].rearrange("p a t -> p (a t)").rearrange("p (r j t) -> p r j t", r=2, j=GH)
        v_ext = xnT[:, :].rearrange("p (a t j c) -> p a t j c", a=2, t=BT, j=GH)
        s_fin = s_sb
        o_sb = w2s_flat[:, 0:T].rearrange("p (t d) -> p t d", d=D)
        f_sb = w2s_flat[:, T:2 * T].rearrange("p (t d) -> p t d", d=D)
        acc_sb = hb
        smallW = sb("smallW", [P, E1, 6])
        xs_in = y_sb
        xlT = sb("xlT", [P, P])
        hs = hg
        ys_sb = sb("ys_sb", [P, 2, D])
        negm = sb("negm", [P, GH, BT])
        negr = sb("negr", [P, GH, BT])
        mparts = sb("mparts", [P, 3, GH, BT], bf16)
        mrows = sb("mrows", [3 * GH * BT, P], bf16)
        rden = sb("rden", [P, 4, GH])
        rt_mem = hg[:, :, :].rearrange("p a n -> p (a n)")
        aff, cand, onehot, full = [rt_mem[:, i * NT * E1:(i + 1) * NT * E1] for i in range(4)]
        aff, cand, onehot = [v.rearrange("p (t e) -> p t e", e=E1) for v in (aff, cand, onehot)]
        full = full.rearrange("p (e t) -> p e t", e=E1)
        rank = rt_mem[:, 4 * NT * E1:6 * NT * E1].rearrange("p (a t e) -> p a t e", a=2, e=E1)
        cum = rt_mem[:, 6 * NT * E1:8 * NT * E1].rearrange("p (a t e) -> p a t e", a=2, e=E1)
        tile_c = hb[:, 0, 0:NSORT * E1].rearrange("p (j e) -> p j e", e=E1)
        amax = sb("amax", [P, NT])
        emin = sb("emin", [P, NT])
        onehotb = sb("onehotb", [P, NT, E1], bf16)
        ctile = sb("ctile", [P, 3, E1])
        em8 = sb("em8", [P, E1])
        m128 = sb("m128", [P, NT])
        iota_j = sb("iota_j", [P, NSORT])
        tile_f = sb("tile_f", [P, NSORT])
        tile_e = sb("tile_e", [P, NSORT], mybir.dt.int32)
        pos_f = sb("pos_f", [P, NT])
        pos = sb("pos", [P, NT], u32)
        alpha = sb("alpha", [P, 3, NT])

        pS = pb("pS", [P, 2, S])
        pT = pb("pT", [P, 2, 512])
        pM = pb("pM", [P, 512])
        pH = pb("pH", [P, 512])

        names = ("s_const s_xrows s_zero s_ones "
                 "s_st s_mv s_ve s_sd s_rstd s_xn s_wload s_wrload s_bload s_b1load s_b2load s_w2load "
                 "s_wtr s_wt s_xtr s_xt s_vo0 s_vo0e s_lg s_lgc s_pj s_pje_a s_pje_v "
                 "s_S s_max s_nm s_exp s_tr s_ev s_pv s_ri s_fin "
                 "s_t1 s_t2 s_t3 s_tf s_hb s_sl s_we s_wn s_ctr s_cc s_so "
                 "s_k1 s_w1load s_b1load1 s_cload s_wall s_xs0 s_silu s_x1 s_af s_rt s_oh s_rk s_rkc "
                 "s_q1 s_q1e s_la s_lae s_lat s_kk s_kke s_vv s_v1e s_cp s_sub s_scr "
                 "s_u s_um s_msp s_mt s_mte s_mrow s_s1 s_e1 s_sel s_pv1 s_ace s_tr1 s_rd1 s_nrm s_ve_b "
                 "s_pos s_te s_wj s_fa s_fae s_fb s_fbe s_relu s_fc s_fce s_al s_als s_g1 s_gate "
                 "s_fin2 s_perm s_btr s_bte s_mscr s_ot s_ote s_pj1 s_fin1 s_vz s_vo s_smw s_lnb "
                 "s_xgt s_xge s_h s_hr s_ht s_hbias s_gelu s_y s_ysc s_accz s_sum s_out").split()
        sm = {n: sem(n) for n in names}
        s_x = [sem(f"s_xin{c}") for c in range(4)]
        s_g = [sem(f"s_gat{i}") for i in range(4)]
        s_w1 = [sem(f"s_w1_{i}") for i in range(RING)]
        s_sc = [sem(f"s_sc{i}") for i in range(2)]
        s_stk = [sem(f"s_stk{i}") for i in range(3)]
        s_ysd = [sem(f"s_ysd{i}") for i in range(2)]
        s_xsl = [sem(f"s_xsl{i}") for i in range(4)]
        block = ctx.enter_context(nc.Block())

        x_t = x_dram.rearrange("b (t p) d -> p (b t) d", p=P)
        out_t = out.rearrange("b (t p) d -> p (b t) d", p=P)
        xn_t = xn_rows.rearrange("(t p) d -> p t d", p=P)
        acc_t = acc_rows.rearrange("(a t p) d -> p a t d", p=P, a=NACC)
        w1_v = a["L0_ffn_W1"].rearrange("e s d m -> d (e s) m")
        w2_v = a["L0_ffn_W2"].rearrange("e s m k -> m (e s) k")

        def ffn_part(n):
            m = n - FFN0
            return (m // 3, m % 3) if 0 <= m < 3 * NSORT else (-1, -1)

        def sel_count(n):
            return sum(1 for m in range(n + 1) if STEPS[m % NSTEP][2] == STEPS[m % NSTEP][1] * P)

        def ends(n):
            if n < 0 or n >= NG * NSTEP:
                return -1
            qc, kt = STEPS[n % NSTEP][:2]
            return 2 * (n // NSTEP) + qc if kt == 4 * qc + 3 else -1

        def ffn_count(n):
            return min(max(n - FFN0, 0), 3 * NSORT)

        def wait_ffn(eng, m):
            j, sub = (m - 1) // 3, (m - 1) % 3
            eng.wait_ge(sm[("s_fae", "s_fbe", "s_fce")[sub]], j + 1)

        def stack_ready(eng, g):
            eng.wait_ge(s_stk[g % 3], 16 * 18 * (g // 3 + 1))

        @block.sync
        def _(sp):
            for c in range(4):
                sp.dma_start(x_sb[:, 4 * c:4 * c + 4, :], x_t[:, 4 * c:4 * c + 4, :]).then_inc(s_x[c], 16)
            for j in range(4):
                w = a[("L0_attn_w_q", "L0_attn_w_k", "L0_attn_w_v", "L0_attn_w_out")[j]]
                sp.dma_start(w_in[:, j, :], w).then_inc(sm["s_wload"], 16)
            sp.dma_start(wr_in[:, :], wr_dram).then_inc(sm["s_wrload"], 16)
            for j in range(2):
                bcol = a[("L0_attn_b_q", "L0_attn_b_k")[j]]
                sp.dma_start(bqk[:, j:j + 1], bcol.rearrange("(p a) -> p a", a=1)).then_inc(sm["s_bload"], 16)
                brow = a[("L0_attn_b_v", "L0_attn_b_out")[j]]
                sp.dma_start(bvo[:, j, :], brow.partition_broadcast(P)).then_inc(sm["s_bload"], 16)
            b1_v = a["L0_ffn_b1"].rearrange("e s m -> (e s) m")
            for j in range(2):
                sp.dma_start(b1_in[:, j, :], b1_v[96 * j:96 * j + 96, :]).then_inc(sm["s_b1load"], 16)
            sp.dma_start(cen_in[:, :], a["L1_ffn_centroids"]).then_inc(sm["s_cload"], 16)
            sp.dma_start(small_in[0:4 * E1, :], a["L1_ffn_b1"].rearrange("e (c p) -> (e c) p", p=P)).then_inc(sm["s_cload"], 16)
            sp.dma_start(small_in[4 * E1:5 * E1, :], a["L1_ffn_ln_g"]).then_inc(sm["s_cload"], 16)
            sp.dma_start(small_in[5 * E1:6 * E1, :], a["L1_ffn_ln_b"]).then_inc(sm["s_cload"], 16)
            sp.dma_start(wq1[:, :], a["L1_attn_Wq"]).then_inc(sm["s_w1load"], 16)
            sp.dma_start(wkd[:, :], a["L1_attn_Wkd"]).then_inc(sm["s_w1load"], 16)
            sp.dma_start(wku[:, :], a["L1_attn_Wku"]).then_inc(sm["s_w1load"], 16)
            sp.dma_start(wo1[:, :], a["L1_attn_Wo"]).then_inc(sm["s_w1load"], 16)
            col = lambda v: v.rearrange("(p a) -> p a", a=1)
            bku, bkd_v = a["L1_attn_bku"], a["L1_attn_bkd"]
            row = lambda v: v.rearrange("(a p) -> a p", a=1)
            sp.dma_start(brow_qk[0:1, :], row(a["L1_attn_bq"])).then_inc(sm["s_b1load1"], 16)
            sp.dma_start(brow_qk[1:2, :], row(bku[0:P])).then_inc(sm["s_b1load1"], 16)
            sp.dma_start(bkd[:, 0:1], col(bkd_v[0:LAT])).then_inc(sm["s_b1load1"], 16)
            sp.dma_start(bkd[:, 1:2], col(bkd_v[LAT:2 * LAT])).then_inc(sm["s_b1load1"], 16)
            sp.dma_start(brow1[:, 0, :], bku[P:2 * P].partition_broadcast(P)).then_inc(sm["s_b1load1"], 16)
            sp.dma_start(brow1[:, 1, :], a["L1_attn_bo"].partition_broadcast(P)).then_inc(sm["s_b1load1"], 16)
            sp.wait_ge(sm["s_const"], 1)
            xs_t = xs_rows.rearrange("(j p) d -> p j d", p=P)
            zer = zeros[:, :, :]
            sp.dma_start(xs_t[:, 0:NT, :], zer).then_inc(sm["s_xs0"], 16)
            sp.dma_start(xs_t[:, NT:NSORT, :], zer[:, 0:NSORT - NT, :]).then_inc(sm["s_xs0"], 16)
            for j in range(NACC):
                sp.dma_start(acc_t[:, j, :, :], zeros[:, :, :]).then_inc(sm["s_accz"], 16)
            for c in range(4):
                sp.wait_ge(sm["s_xn"], 4 * c + 4)
                sp.dma_start(xn_t[:, 4 * c:4 * c + 4, :], xn[:, 4 * c:4 * c + 4, :]).then_inc(sm["s_xrows"], 16)
            for p in range(4):
                sp.dma_start(w1r[:, p, :, :], w1_v[:, 8 * p:8 * p + 8, :]).then_inc(s_w1[p], 16)
            for j in range(4):
                sp.dma_start(w2s[:, 48 * j:48 * j + 48, :], w2_v[:, 48 * j:48 * j + 48, :]).then_inc(sm["s_w2load"], 16)
            for p in range(4, RING):
                sp.dma_start(w1r[:, p, :, :], w1_v[:, 8 * p:8 * p + 8, :]).then_inc(s_w1[p], 16)
            sp.wait_ge(sm["s_tf"], 1)
            sp.dma_start(hi_v[:, :], top_v[64:64 + E0, :]).then_inc(sm["s_hb"], 16)
            sp.dma_start(hi_f[:, :], top_f[64:64 + E0, :]).then_inc(sm["s_hb"], 16)
            sp.wait_ge(sm["s_pv"], NT)
            sp.dma_start(b2p, a["L0_ffn_b2"].rearrange("(p r) s k -> r p (s k)", r=2)).then_inc(sm["s_b2load"], 16)
            for p in range(RING, NP):
                sp.wait_ge(sm["s_h"], p - RING + 1)
                sp.dma_start(w1r[:, p - RING, :, :], w1_v[:, 8 * p:8 * p + 8, :]).then_inc(s_w1[p - RING], 16)
            for i in range(2):
                sp.wait_ge(s_sc[i], 16 * (NP // 2))
            sp.wait_ge(sm["s_h"], NP)
            for c in range(4):
                for j in range(NACC):
                    sp.dma_start(accs[:, j, 4 * c:4 * c + 4, :], acc_t[:, j, 4 * c:4 * c + 4, :]).then_inc(s_x[c], 16)
            w1f = a["L1_ffn_w1"].rearrange("e d f -> d e f")
            w2f = a["L1_ffn_w2"].rearrange("e (c p) d -> p e c d", p=P)
            sp.dma_start(wall[:, :, 0:F1], w1f).then_inc(sm["s_wall"], 16)
            for e in range(E1):
                sp.dma_start(wall[:, e, F1:2 * F1].rearrange("p (c d) -> p c d", d=D), w2f[:, e, :, :]).then_inc(sm["s_wall"], 16)
            sp.dma_start(wall[:, :, 2 * F1:2 * F1 + D], a["L1_ffn_b2"].partition_broadcast(P)).then_inc(sm["s_wall"], 16)

            def load_stack(g):
                b, g4 = g // (NG // B), g % (NG // B)
                sp.wait_ge(sm["s_scr"], 16 * 6 * (b + 1))
                if g < 3:
                    sp.wait_ge(sm["s_vo"], g + 1)
                if g == 2:
                    sp.wait_ge(sm["s_vv"], NC)
                if g >= 3:
                    sp.wait_ge(sm["s_s1"], GH * NSTEP * (g - 2))
                for x in range(3):
                    for y in range(3):
                        r = 24 * x + 8 * y
                        for side in range(2):
                            src = (q_scr[b, x, g4], k_scr[b, y, g4])[side]
                            sp.dma_start(stack(side, g)[r:r + DH, :, :].rearrange("p j t -> p (j t)"),
                                         src).then_inc(s_stk[g % 3], 16)

            def store_parts(b):
                for st in range(3):
                    for side in range(2):
                        sp.wait_ge(sm["s_cp"], 6 * b + 2 * st + side + 1)
                        sp.dma_start((q_scr, k_scr)[side][b, st].rearrange("g d (j t) -> (g d j) t", j=GH),
                                     parts[side][:, st, b * S:b * S + S]).then_inc(sm["s_scr"], 16)

            def store_m(g):
                sp.wait_ge(sm["s_mte"], g + 1)
                sp.dma_start(m_scr[g], mrows[:, :]).then_inc(sm["s_mscr"], 16)
                sp.wait_ge(sm["s_mscr"], 16 * (g + 1))
                sp.dma_start(stack(0, g)[KQ:KM, :, :].rearrange("p j t -> p (j t)"),
                             m_scr[g].rearrange("(a n) q -> a (n q)", a=3)).then_inc(sm["s_mrow"], 16)

            store_parts(0)
            load_stack(0)
            store_parts(1)
            load_stack(1)
            load_stack(2)
            store_m(0)
            sp.wait_ge(sm["s_pos"], 16 * NT)
            for j in range(3):
                sp.dma_start(xs_in[:, j % 4, :], xs_t[:, j, :]).then_inc(s_xsl[j % 4], 16)
            for n in range(NG * NSTEP + 2):
                g = (n + 4) // NSTEP
                if (n + 4) % NSTEP == 0 and g < NG:
                    store_m(g)
                if n % NSTEP == 0 and n // NSTEP + 2 < NG and n:
                    load_stack(n // NSTEP + 2)
                j, sub = ffn_part(n)
                if sub == 0 and j + 3 < NSORT:
                    if j >= 1:
                        sp.wait_ge(sm["s_fa"], j)
                    sp.dma_start(xs_in[:, (j + 3) % 4, :], xs_t[:, j + 3, :]).then_inc(s_xsl[(j + 3) % 4], 16)
                if sub == 2:
                    sp.wait_ge(sm["s_fce"], j + 1)
                    sp.dma_start(ys_rows[j * P:j * P + P, :], ys_sb[:, j % 2, :]).then_inc(s_ysd[j % 2], 16)
            for c in range(4):
                sp.wait_ge(sm["s_fin2"], 2 * c + 2)
                sp.dma_start(out_t[:, 4 * c:4 * c + 4, :], x_sb[:, 4 * c:4 * c + 4, :]).then_inc(sm["s_out"], 16)
            for i in range(2):
                sp.wait_ge(s_ysd[i], 16 * ((NSORT + 1 - i) // 2))
            sp.wait_ge(sm["s_scr"], 16 * 12)
            sp.wait_ge(sm["s_xrows"], 64)
            sp.wait_ge(sm["s_xs0"], 32)
            sp.wait_ge(sm["s_accz"], 16 * NACC)
            sp.wait_ge(sm["s_out"], 64)

        @block.gpsimd
        def _(pool):
            pool.memset(zeros[:, :, :], 0.0).then_inc(sm["s_const"], 1)
            pool.memset(ident[:, :], 0.0).then_inc(sm["s_zero"], 1)
            pool.memset(wr_T[:, :], 0.0).then_inc(sm["s_zero"], 1)
            pool.memset(pairind[:, :], 0.0).then_inc(sm["s_zero"], 1)
            pool.memset(identb[:, :], 0.0).then_inc(sm["s_k1"], 1)
            pool.memset(causal[:, :], 0.0).then_inc(sm["s_k1"], 1)
            pool.memset(before[:, :], 1.0).then_inc(sm["s_k1"], 1)
            pool.memset(onesb[:, :], 1.0).then_inc(sm["s_k1"], 1)
            pool.iota(em8[:, :], [[1, E1]], base=-E1, channel_multiplier=0, allow_small_or_imprecise_dtypes=True).then_inc(sm["s_k1"], 1)
            pool.iota(m128[:, :], [[P, NT]], base=0, channel_multiplier=0, allow_small_or_imprecise_dtypes=True).then_inc(sm["s_k1"], 1)
            pool.iota(iota_j[:, :], [[1, NSORT]], base=0, channel_multiplier=0, allow_small_or_imprecise_dtypes=True).then_inc(sm["s_k1"], 1)
            pool.wait_ge(sm["s_k1"], 7)
            pool.affine_select(out=identb[:, :], in_=identb[:, :], compare_op=ALU.not_equal, fill=1.0,
                               base=0, pattern=[[-1, P]], channel_multiplier=1).then_inc(sm["s_k1"], 1)
            pool.affine_select(out=causal[:, :], in_=causal[:, :], compare_op=ALU.is_ge, fill=NEG,
                               base=0, pattern=[[-1, P]], channel_multiplier=1).then_inc(sm["s_k1"], 1)
            pool.affine_select(out=before[:, :], in_=before[:, :], compare_op=ALU.is_gt, fill=0.0,
                               base=0, pattern=[[1, P]], channel_multiplier=-1).then_inc(sm["s_k1"], 1)
            pool.wait_ge(sm["s_zero"], 3)
            pool.affine_select(out=ident[:, :], in_=ident[:, :], compare_op=ALU.not_equal, fill=1.0,
                               base=0, pattern=[[-1, P]], channel_multiplier=1).then_inc(sm["s_const"], 1)
            pool.affine_select(out=pairind[:, :].rearrange("r (e c) -> r e c", e=2),
                               in_=pairind[:, :].rearrange("r (e c) -> r e c", e=2), compare_op=ALU.not_equal, fill=1.0,
                               base=0, pattern=[[-1, 2], [0, 64]], channel_multiplier=1).then_inc(sm["s_const"], 1)

            pool.wait_ge(sm["s_xrows"], 64)
            pool.wait_ge(sm["s_so"], 2)

            def gather(p):
                if p >= 4:
                    pool.wait_ge(s_g[p % 4], 16 * (p // 4))
                pool.indirect_dma_start(out=xg[:, p, :], out_offset=None, in_=xn_rows,
                                        in_offset=bass.IndirectOffsetOnAxis(ap=g_idx[:, p:p + 1], axis=0),
                                        ).then_inc(s_g[p % 4], 16)
            for p in range(6):
                gather(p)
            pool.wait_ge(sm["s_accz"], 16 * NACC)
            for p in range(NP):
                if p + 6 < NP:
                    gather(p + 6)
                pool.wait_ge(sm["s_ysc"], p + 1)
                if p >= 2:
                    pool.wait_ge(s_sc[p % 2], 16 * (p // 2))
                pool.indirect_dma_start(out=acc_rows,
                                        out_offset=bass.IndirectOffsetOnAxis(ap=s_idx[:, p:p + 1], axis=0),
                                        in_=y_sb[:, p % 4, :], in_offset=None,
                                        compute_op=ALU.add).then_inc(s_sc[p % 2], 16)

            def build_v(g):
                if g >= 2:
                    pool.wait_ge(sm["s_pv1"], NSTEP * (g - 1))
                b, g4 = g // (NG // B), g % (NG // B)
                src = v_sb[:, b * BT:b * BT + BT, g4 * GH * DH:(g4 + 1) * GH * DH].rearrange("p t (j d) -> p t j d", d=DH)
                pool.tensor_copy(v_ext[:, g % 2, :, :, 0:DH], src).then_inc(sm["s_ve_b"], 1)

            pool.wait_ge(sm["s_x1"], 8)
            for g in range(3):
                pool.memset(stack(1, g)[64:KM, :, :], 1.0).then_inc(sm["s_vo"], 1)
            pool.wait_ge(sm["s_v1e"], NC)
            pool.wait_ge(sm["s_vv"], NC)
            pool.wait_ge(sm["s_vo"], 3)
            pool.memset(xnT[:, :], 0.0).then_inc(sm["s_vz"], 1)
            pool.wait_ge(sm["s_vz"], 1)
            pool.memset(v_ext[:, :, :, :, DH:DH + 1], 1.0).then_inc(sm["s_vz"], 1)
            build_v(0)
            build_v(1)
            pool.wait_ge(sm["s_te"], 7)
            pool.wait_ge(sm["s_xn"], 3 * NT)
            pool.wait_ge(sm["s_xs0"], 32)

            def sort_tile(t):
                pool.indirect_dma_start(out=xs_rows, out_offset=bass.IndirectOffsetOnAxis(ap=pos[:, t:t + 1], axis=0),
                                        in_=s_sb[:, t, :], in_offset=None).then_inc(sm["s_pos"], 16)

            for t in range(2):
                sort_tile(t)

            for n in range(NG * NSTEP + 2):
                if n < NG * NSTEP:
                    qc, kt, q0, cols = STEPS[n % NSTEP]
                    if q0 == kt * P:
                        pool.wait_ge(sm["s_e1"], GH * n + GH)
                        blk_ = pr1[:, n % 2, :, 0:P]
                        pool.affine_select(out=blk_, in_=blk_, compare_op=ALU.is_ge, fill=0.0, base=0,
                                           pattern=[[0, GH], [1, P]], channel_multiplier=-1).then_inc(sm["s_sel"], 1)
                for t in range(2 * n + 2, 2 * n + 4) if 2 * n + 2 < NT else ():
                    sort_tile(t)
                if n % NSTEP == NSTEP - 3 and 2 <= n // NSTEP + 1 < NG:
                    build_v(n // NSTEP + 1)
                if n == OUT0 + 1:
                    for i in range(2):
                        pool.wait_ge(s_ysd[i], 16 * ((NSORT + 1 - i) // 2))
                for t in range(gathered(n), gathered(n + 1)):
                    pool.indirect_dma_start(out=f_sb[:, t, :], out_offset=None, in_=ys_rows,
                                            in_offset=bass.IndirectOffsetOnAxis(ap=pos[:, t:t + 1], axis=0)).then_inc(sm["s_g1"], 16)

        @block.tensor
        def _(pe):
            def turn_first(c):
                pe.wait_ge(sm["s_xn"], 4 * c + 4)
                if c == 1:
                    pe.wait_ge(sm["s_wt"], 1)
                if c >= 2:
                    pe.wait_ge(sm["s_xt"], c - 1)
                for j in range(4):
                    last = nc.tensor.transpose(pT[:, (c + 1) % 2, j * P:j * P + P], xn[:, 4 * c + j, :], ident[:, :])
                last.then_inc(sm["s_xtr"], 1)

            pe.wait_ge(sm["s_const"], 3)
            pe.wait_ge(sm["s_wload"], 64)
            for j in range(4):
                last = nc.tensor.transpose(pT[:, 0, j * P:j * P + P], w_in[:, j, :], ident[:, :])
            last.then_inc(sm["s_wtr"], 1)
            turn_first(0)
            turn_first(1)
            pe.wait_ge(sm["s_wrload"], 16)
            pe.wait_ge(sm["s_b1load"], 32)
            nc.tensor.transpose(pM[:, 0:E0], wr_in[:, :], ident[0:E0, 0:E0])
            for j in range(2):
                last = nc.tensor.transpose(pM[:, 64 + 96 * j:160 + 96 * j], b1_in[:, j, :], ident[0:96, 0:96])
            pe.wait_ge(sm["s_bload"], 64)
            nc.tensor.transpose(pM[:, 320:448], bvo[:, 0, :], ident[:, :])
            pe.wait_ge(sm["s_cload"], 64)
            nc.tensor.transpose(pM[:, 256:256 + E1], cen_in[:, :], ident[0:E1, 0:E1])
            last = nc.tensor.transpose(pM[:, 272:272 + 6 * E1], small_in[:, :], ident[0:6 * E1, 0:6 * E1])
            last.then_inc(sm["s_wtr"], 1)
            turn_first(2)
            turn_first(3)
            pe.wait_ge(sm["s_wt"], 6)
            nc.tensor.matmul(pH[:, 0:P], w_in[:, 2, :], w_T[:, 3, :], start=True, stop=True)
            nc.tensor.matmul(pH[:, P:2 * P], bvT[:, :], w_T[:, 3, :], start=True, stop=True).then_inc(sm["s_vo0"], 1)
            for c in range(NC):
                pe.wait_ge(sm["s_xt"], c + 1)
                h = c // 2
                last = nc.tensor.matmul(pS[64 * h:64 * h + 64, 0, (c % 2) * 512:(c % 2) * 512 + 512], wr_T[:, :],
                                        xnT[:, c * 512:c * 512 + 512], start=True, stop=True)
            last.then_inc(sm["s_lg"], 1)
            dst = [pS[:, 1, 0:512], pS[:, 1, 512:1024], pM[:, :], pH[:, :]]
            pe.wait_ge(sm["s_vo0e"], 2)
            n = 0
            for c in range(NC):
                for j in range(3):
                    if n >= 4:
                        cc, jj = (n - 4) // 3, (n - 4) % 3
                        if jj < 2:
                            pe.wait_ge(sm["s_pje_a"], 2 * cc + jj + 1)
                        else:
                            pe.wait_ge(sm["s_pje_v"], cc + 1)
                    if j < 2:
                        last = nc.tensor.matmul(dst[n % 4], w_T[:, j, :], xnT[:, c * 512:c * 512 + 512], start=True, stop=True)
                    else:
                        for t in range(4):
                            last = nc.tensor.matmul(dst[n % 4][:, t * P:t * P + P],
                                                    xnT[:, c * 512 + t * P:c * 512 + t * P + P], w_vo,
                                                    start=True, stop=True)
                    last.then_inc(sm["s_pj"], 1)
                    n += 1

            def scores(i):
                b = i // BT
                if i == 0:
                    pe.wait_ge(sm["s_lgc"], 1)
                    pe.wait_ge(sm["s_pje_a"], 2 * NC)
                    pe.wait_ge(sm["s_pje_v"], NC)
                if i >= 2:
                    pe.wait_ge(sm["s_exp"], i - 1)
                for h in range(2):
                    last = nc.tensor.matmul(pS[:, i % 2, h * 512:h * 512 + 512], qT[:, i * P:i * P + P],
                                            kT[:, b * S + h * 512:b * S + h * 512 + 512], start=True, stop=True)
                last.then_inc(sm["s_S"], 1)

            def turn(i):
                pe.wait_ge(sm["s_exp"], i + 1)
                for h in range(2):
                    if i:
                        pe.wait_ge(sm["s_ev"], 2 * (i - 1) + h + 1)
                    for j in range(4):
                        last = nc.tensor.transpose(pT[:, h, j * P:j * P + P],
                                                   probs[:, i % 2, (4 * h + j) * P:(4 * h + j + 1) * P], ident[:, :])
                    last.then_inc(sm["s_tr"], 1)

            def values(i):
                b = i // BT
                pe.wait_ge(sm["s_ev"], 2 * i + 2)
                if i >= 2:
                    pe.wait_ge(sm["s_fin"], i - 1)
                if i == SLOT_STEP:
                    pe.wait_ge(sm["s_cc"], 4)
                for j in range(BT):
                    last = nc.tensor.matmul((pM, pH)[i % 2][:, 0:D], probsT[:, i % 2, j * P:j * P + P], v_sb[:, b * BT + j, :],
                                            start=(j == 0), stop=(j == BT - 1))
                last.then_inc(sm["s_pv"], 1)

            def turn_slots():
                pe.wait_ge(sm["s_sl"], 7)
                pe.wait_ge(sm["s_fin"], SLOT_STEP - 1)
                nc.tensor.transpose(pM[:, 256:256 + E0], slots[:, 0:2, :].rearrange("e a c -> e (a c)"), ident[0:E0, 0:E0])
                nc.tensor.transpose(pM[:, 304:304 + E0], slots[:, 2:4, :].rearrange("e a c -> e (a c)"),
                                    ident[0:E0, 0:E0]).then_inc(sm["s_ctr"], 1)

            scores(0)
            for i in range(NT):
                if i + 1 < NT:
                    scores(i + 1)
                if i:
                    values(i - 1)
                if i == SLOT_STEP:
                    turn_slots()
                turn(i)
            values(NT - 1)

            def spread(p):
                pe.wait_ge(s_g[p % 4], 16 * (p // 4 + 1))
                if p >= 2:
                    pe.wait_ge(sm["s_xge"], p - 1)
                nc.tensor.transpose(pT[:, p % 2, 0:P], xg[:, p, :], ident[:, :]).then_inc(sm["s_xgt"], 1)

            def up(p):
                pe.wait_ge(sm["s_xge"], p + 1)
                pe.wait_ge(s_w1[p % RING], 16 * (p // RING + 1))
                if p >= 2:
                    pe.wait_ge(sm["s_hr"], p - 1)
                for e in range(2):
                    last = nc.tensor.matmul(pS[64 * e:64 * e + 64, p % 2, 0:512], xgT[:, p % 2, 64 * e:64 * e + 64],
                                            w1r[:, p % RING, NS * e:NS * e + NS, :], start=True, stop=True)
                last.then_inc(sm["s_h"], 1)

            def turn_h(p):
                pe.wait_ge(sm["s_hr"], p + 1)
                if p >= 2:
                    pe.wait_ge(sm["s_hbias"], p - 1)
                for s in range(NS):
                    last = nc.tensor.transpose(pS[:, p % 2, 512 + P * s:512 + P * s + P], hb[:, p % 2, P * s:P * s + P], ident[:, :])
                last.then_inc(sm["s_ht"], 1)

            def down(p):
                pe.wait_ge(sm["s_gelu"], p + 1)
                if p == 0:
                    pe.wait_ge(sm["s_b2load"], 16)
                    pe.wait_ge(sm["s_w2load"], 64)
                    pe.wait_ge(sm["s_cc"], 4)
                    pe.wait_ge(sm["s_fin"], NT)
                if p >= 2:
                    pe.wait_ge(sm["s_ysc"], p - 1)
                yb = (pM, pH)[p % 2]
                nc.tensor.matmul(yb[:, 0:D], pairind[:, :], b2p[:, p, :], start=True, stop=False,
                                 skip_group_check=True)
                for n in range(2 * NS):
                    e, s = n // NS, n % NS
                    last = nc.tensor.matmul(yb[64 * e:64 * e + 64, KY * s:KY * s + KY],
                                            hg[:, p % 2, 64 * n:64 * n + 64], w2s[:, (2 * p + e) * NS + s, :],
                                            start=False, stop=(n == 2 * NS - 1), skip_group_check=True)
                last.then_inc(sm["s_y"], 1)

            spread(0)
            for p in range(NP):
                up(p)
                if p:
                    turn_h(p - 1)
                if p + 1 < NP:
                    spread(p + 1)
                if p >= 2:
                    down(p - 2)
            turn_h(NP - 1)
            down(NP - 2)
            down(NP - 1)

            pe.wait_ge(sm["s_perm"], 3)
            pe.wait_ge(sm["s_ysc"], NP - 1)
            nc.tensor.transpose(pM[:, 0:2], brow_p[:, :], ident[0:2, 0:2]).then_inc(sm["s_btr"], 1)
            pe.wait_ge(sm["s_w1load"], 64)

            def turn_tokens(b):
                for c in (2 * b, 2 * b + 1):
                    pe.wait_ge(sm["s_xn"], NT + 4 * c + 4)
                    if b:
                        pe.wait_ge(sm["s_lae"], 4)
                    for j in range(4):
                        last = nc.tensor.transpose(pT[:, c % 2, j * P:j * P + P], xn[:, 4 * c + j, :], ident[:, :])
                    last.then_inc(sm["s_xtr"], 1)

            def make_qk(b):
                for c in (2 * b, 2 * b + 1):
                    pe.wait_ge(sm["s_xt"], NC + c + 1)
                    if b:
                        pe.wait_ge(sm["s_q1e"], c - 1)
                    nc.tensor.matmul(pS[:, 0, (c % 2) * 512:(c % 2) * 512 + 512], wqp[:, :],
                                     xnT[:, c * 512:c * 512 + 512], start=True, stop=True).then_inc(sm["s_q1"], 1)
                for c in (2 * b, 2 * b + 1):
                    if c % 2:
                        pe.wait_ge(sm["s_lae"], 2 * c)
                    for h in range(2):
                        last = nc.tensor.matmul(pT[0:LAT, h, :], wkd[:, h * LAT:h * LAT + LAT],
                                                xnT[:, c * 512:c * 512 + 512], start=True, stop=True)
                    last.then_inc(sm["s_la"], 1)
                for c in (2 * b, 2 * b + 1):
                    if b:
                        pe.wait_ge(sm["s_kke"], c - 1)
                    pe.wait_ge(sm["s_lat"], c + 1)
                    nc.tensor.matmul(pS[:, 1, (c % 2) * 512:(c % 2) * 512 + 512], wkp[:, :],
                                     latT[:, c * 512:c * 512 + 512], start=True, stop=True).then_inc(sm["s_kk"], 1)

            def make_v(b):
                for c in (2 * b, 2 * b + 1):
                    if c >= 2:
                        pe.wait_ge(sm["s_v1e"], c - 1)
                    for t in range(4):
                        last = nc.tensor.matmul((pM, pH)[c % 2][:, t * P:t * P + P], latT[:, (4 * c + t) * P:(4 * c + t + 1) * P],
                                                wku[:, P:2 * P], start=True, stop=True)
                    last.then_inc(sm["s_vv"], 1)

            turn_tokens(0)
            make_qk(0)
            turn_tokens(1)
            pe.wait_ge(sm["s_bte"], 1)
            make_v(0)
            make_qk(1)
            pe.wait_ge(sm["s_q1e"], NC)
            for t in range(NT):
                last = nc.tensor.matmul(pS[:, 0, t * E1:t * E1 + E1], xnT[:, t * P:t * P + P], cenT[:, :], start=True, stop=True)
            last.then_inc(sm["s_af"], 1)
            make_v(1)

            def count_earlier():
                pe.wait_ge(sm["s_oh"], 2)
                pe.wait_ge(sm["s_lae"], 2 * NC)
                pe.wait_ge(sm["s_k1"], 10)
                oh = onehotb[:, :, :].rearrange("p t e -> p (t e)")
                nc.tensor.matmul(pT[:, 0, 0:NT * E1], before[:, :], oh, start=True, stop=True)
                nc.tensor.matmul(pT[:, 0, NT * E1:2 * NT * E1], onesb[:, :], oh, start=True, stop=True).then_inc(sm["s_rk"], 1)

            def unit(u):
                g = u // NU
                j, heads, qt = UNITS[u % NU]
                if u % NU == 0:
                    stack_ready(pe, g)
                if u == 0:
                    pe.wait_ge(sm["s_kke"], NC)
                    pe.wait_ge(sm["s_rt"], 1)
                if u >= 2:
                    pe.wait_ge(sm["s_um"], u - 1)
                keys = (qt + 1) * P
                if heads == 2:
                    spans = [(j, 0, 0, keys), (j + 1, 512, 0, keys)]
                else:
                    spans = [(j, 0, 0, 512), (j, 512, 512, keys - 512)]
                for h, at, k0, w in spans:
                    diag = heads == 2 or k0
                    last = nc.tensor.matmul(pS[:, u % 2, at:at + w], stack(0, g)[0:KQ, h, qt * P:qt * P + P],
                                            stack(1, g)[0:KQ, h, k0:k0 + w], start=True, stop=not diag)
                    if diag:
                        last = nc.tensor.matmul(pS[:, u % 2, at + w - P:at + w], identb[:, :], causal[:, :],
                                                start=False, stop=True)
                last.then_inc(sm["s_u"], 1)

            def turn_m(g):
                pe.wait_ge(sm["s_msp"], 5 * g + 5)
                nc.tensor.transpose(pH[:, :].bitcast(bf16)[0:3 * GH * BT, 0:P],
                                    mparts[:, :, :, :].rearrange("p a j t -> p (a j t)"), identb[:, :]).then_inc(sm["s_mt"], 1)

            def score(n, j):
                e = GH * n + j
                g = n // NSTEP
                qc, kt, q0, cols = STEPS[n % NSTEP]
                if n % NSTEP == 0 and j == 0:
                    pe.wait_ge(sm["s_mrow"], 16 * (g + 1))
                if e >= 2:
                    pe.wait_ge(sm["s_e1"], e - 1)
                nc.tensor.matmul(pT[:, j % 2, 0:cols], stack(1, g)[0:KM, j, kt * P:kt * P + P],
                                 stack(0, g)[0:KM, j, q0:q0 + cols], start=True, stop=True).then_inc(sm["s_s1"], 1)

            def weigh(n):
                g = n // NSTEP
                qc, kt, q0, cols = STEPS[n % NSTEP]
                pe.wait_ge(sm["s_e1"], GH * n + GH)
                if q0 == kt * P:
                    pe.wait_ge(sm["s_sel"], sel_count(n))
                if n % NSTEP == 0:
                    pe.wait_ge(sm["s_ve_b"], g + 1)
                if kt == 0 and n:
                    pe.wait_ge(sm["s_nrm"], 2 * g + qc)
                for j in range(GH):
                    last = nc.tensor.matmul(pM[32 * j:32 * j + 32, q0 - qc * 512:q0 - qc * 512 + cols],
                                            v_ext[:, g % 2, kt, j, :], pr1[:, n % 2, j, 0:cols],
                                            start=(kt == 0), stop=(kt == 4 * qc + 3))
                last.then_inc(sm["s_pv1"], 1)

            def turn_acc(r):
                pe.wait_ge(sm["s_ace"], r + 1)
                for t in range(4):
                    last = nc.tensor.transpose(pM[:, t * P:t * P + P], acc_sb[:, r % 2, t * P:t * P + P], ident[:, :])
                last.then_inc(sm["s_tr1"], 1)

            def ffn(j, sub):
                if sub == 0:
                    pe.wait_ge(s_xsl[j % 4], 16 * (j // 4 + 1))
                    if j:
                        pe.wait_ge(sm["s_fce"], j)
                    nc.tensor.transpose(pH[:, 0:P], xs_in[:, j % 4, :], ident[:, :]).then_inc(sm["s_fa"], 1)
                elif sub == 1:
                    pe.wait_ge(sm["s_fae"], j + 1)
                    for c in range(FC):
                        last = nc.tensor.matmul(pH[:, c * P:c * P + P], w_tile[:, j % 2, c * P:c * P + P], xlT[:, :],
                                                start=True, stop=True)
                    last.then_inc(sm["s_fb"], 1)
                else:
                    pe.wait_ge(sm["s_relu"], j + 1)
                    for c in range(FC):
                        last = nc.tensor.matmul(pH[:, 0:D], hs[:, j % 2, c * P:c * P + P],
                                                w_tile[:, j % 2, F1 + c * D:F1 + c * D + D],
                                                start=(c == 0), stop=(c == FC - 1))
                    last.then_inc(sm["s_fc"], 1)

            def turn_heads(c):
                pe.wait_ge(sm["s_nrm"], NG * (c // 2 + 1) - 1 + c % 2)
                if c:
                    pe.wait_ge(sm["s_fin1"], c)
                else:
                    pe.wait_ge(sm["s_fce"], NSORT)
                for t in range(4):
                    last = nc.tensor.transpose(pH[:, t * P:t * P + P], o_sb[:, 4 * c + t, :], ident[:, :])
                last.then_inc(sm["s_ot"], 1)

            def project1(c):
                pe.wait_ge(sm["s_ote"], c + 1)
                for t in range(4):
                    last = nc.tensor.matmul(pH[:, t * P:t * P + P], hs[:, c % 2, t * P:t * P + P], wo1[:, :],
                                            start=True, stop=True)
                last.then_inc(sm["s_pj1"], 1)

            for u in range(NU):
                unit(u)
                if u == 1:
                    count_earlier()
            turn_m(0)
            for u in range(NU, units_before(0)):
                unit(u)
            pe.wait_ge(sm["s_rkc"], 1)
            for n in range(NG * NSTEP + 2):
                last_step = n >= NG * NSTEP
                units = range(units_before(n), units_before(n + 1))
                if not last_step:
                    score(n, 0)
                for u in units[:1]:
                    unit(u)
                if not last_step:
                    score(n, 1)
                for u in units[1:]:
                    unit(u)
                if n >= 2 and ends(n - 2) >= 0:
                    turn_acc(ends(n - 2))
                if not last_step:
                    score(n, 2)
                if (n + 4) % NSTEP == 0 and (n + 4) // NSTEP < NG:
                    if ffn_count(n):
                        wait_ffn(pe, ffn_count(n))
                    turn_m((n + 4) // NSTEP)
                if not last_step:
                    score(n, 3)
                if 1 <= n <= NG * NSTEP:
                    weigh(n - 1)
                j, sub = ffn_part(n)
                if sub >= 0:
                    pe.wait_ge(sm["s_mte"], min(NG, 1 + (n + 4) // NSTEP))
                    ffn(j, sub)
                for c, first in enumerate(OUTS):
                    if n == first:
                        turn_heads(c)
                    if n == first + 1:
                        project1(c)

            turn_heads(NC - 1)
            project1(NC - 1)

        @block.vector
        def _(dve):
            def ln_var(turn_, tiles, first=None):
                n1 = tiles[-1] + 1
                for t in tiles:
                    dve.wait_ge(sm["s_st"], turn_ * NT + t + 1)
                    nc.vector.bn_aggr(mv[:, t, :], stats[:, t, :]).then_inc(sm["s_mv"], 1)
                if first is not None:
                    dve.wait_ge(sm["s_mv"], turn_ * NT + n1)
                    nc.vector.tensor_scalar(var_e[:, first:n1], mv[:, first:n1, 1], EPS, None, ALU.add).then_inc(sm["s_ve"], 1)

            def ln_rstd(k, n0, n1):
                rs_, ve_, nw_ = rstd[:, n0:n1], var_e[:, n0:n1], newt[:, n0:n1]
                dve.wait_ge(sm["s_sd"], k + 1)
                nc.vector.reciprocal(rs_, sdev[:, n0:n1]).then_inc(sm["s_rstd"], 1)
                dve.wait_ge(sm["s_rstd"], 5 * k + 1)
                nc.vector.tensor_tensor(nw_, rs_, rs_, ALU.mult).then_inc(sm["s_rstd"], 1)
                dve.wait_ge(sm["s_rstd"], 5 * k + 2)
                nc.vector.tensor_tensor(nw_, nw_, ve_, ALU.mult).then_inc(sm["s_rstd"], 1)
                dve.wait_ge(sm["s_rstd"], 5 * k + 3)
                nc.vector.tensor_scalar(nw_, nw_, -0.5, 1.5, ALU.mult, ALU.add).then_inc(sm["s_rstd"], 1)
                dve.wait_ge(sm["s_rstd"], 5 * k + 4)
                nc.vector.tensor_tensor(rs_, rs_, nw_, ALU.mult).then_inc(sm["s_rstd"], 1)
                dve.wait_ge(sm["s_rstd"], 5 * k + 5)

            def ln_apply(tiles, src, dst):
                for t in tiles:
                    nc.vector.tensor_scalar(dst[:, t, :], src[:, t, :], mv[:, t, 0:1], rstd[:, t:t + 1],
                                            ALU.subtract, ALU.mult).then_inc(sm["s_xn"], 1)

            def route_a(dve):
                dve.wait_ge(sm["s_rt"], 1)
                nc.vector.tensor_reduce(amax[:, :], aff[:, :, :], AX.X, ALU.max).then_inc(sm["s_rt"], 1)
                dve.wait_ge(sm["s_rt"], 2)
                wide = amax[:, :].unsqueeze(2).to_broadcast([P, NT, E1])
                nc.vector.tensor_tensor(cand[:, :, :], aff[:, :, :], wide, ALU.is_equal).then_inc(sm["s_rt"], 1)
                dve.wait_ge(sm["s_rt"], 3)
                dve.wait_ge(sm["s_k1"], 10)
                em = em8[:, :].unsqueeze(1).to_broadcast([P, NT, E1])
                nc.vector.tensor_tensor(cand[:, :, :], cand[:, :, :], em, ALU.mult).then_inc(sm["s_rt"], 1)
                dve.wait_ge(sm["s_rt"], 4)
                nc.vector.tensor_reduce(emin[:, :], cand[:, :, :], AX.X, ALU.min).then_inc(sm["s_rt"], 1)
                dve.wait_ge(sm["s_rt"], 5)
                em_w = emin[:, :].unsqueeze(2).to_broadcast([P, NT, E1])
                nc.vector.tensor_tensor(onehot[:, :, :], em, em_w, ALU.is_equal).then_inc(sm["s_oh"], 1)
                nc.vector.tensor_tensor(onehotb[:, :, :], em, em_w, ALU.is_equal).then_inc(sm["s_oh"], 1)
                nc.vector.tensor_copy(smallW[:, :, 0:FC], smallT[:, 0:FC * E1].rearrange("p (e c) -> p e c", c=FC)).then_inc(sm["s_smw"], 1)
                nc.vector.tensor_copy(smallW[:, :, FC], smallT[:, FC * E1:(FC + 1) * E1]).then_inc(sm["s_smw"], 1)
                nc.vector.tensor_copy(smallW[:, :, FC + 1], smallT[:, (FC + 1) * E1:(FC + 2) * E1]).then_inc(sm["s_smw"], 1)

            def route_b(dve):
                n = 5

                def step(ins):
                    nonlocal n
                    n += 1
                    ins.then_inc(sm["s_rt"], 1)
                    dve.wait_ge(sm["s_rt"], n)
                dve.wait_ge(sm["s_rkc"], 1)
                src = rank[:, 1, :, :]
                for k in range(4):
                    sh, dst = 1 << k, cum[:, k % 2, :, :]
                    step(nc.vector.tensor_copy(dst[:, 0:sh, :], src[:, 0:sh, :]))
                    step(nc.vector.tensor_tensor(dst[:, sh:NT, :], src[:, sh:NT, :], src[:, 0:NT - sh, :], ALU.add))
                    src = dst
                count = src[:, NT - 1, :].unsqueeze(2).to_broadcast([P, E1, NT])
                step(nc.vector.tensor_tensor(full[:, :, :], count, m128[:, :].unsqueeze(1).to_broadcast([P, E1, NT]), ALU.is_gt))
                step(nc.vector.tensor_reduce(ctile[:, 0, :], full[:, :, :], AX.X, ALU.add))
                step(nc.vector.tensor_copy(ctile[:, 1, :], ctile[:, 0, :]))
                for e in range(1, E1):
                    step(nc.vector.tensor_tensor(ctile[:, 1, e:e + 1], ctile[:, 1, e:e + 1], ctile[:, 1, e - 1:e], ALU.add))
                step(nc.vector.tensor_tensor(ctile[:, 2, :], ctile[:, 1, :], ctile[:, 0, :], ALU.subtract))
                base = ctile[:, 2, :].unsqueeze(1).to_broadcast([P, NT, E1])
                step(nc.vector.tensor_tensor(cand[:, :, :], src, rank[:, 1, :, :], ALU.subtract))
                step(nc.vector.scalar_tensor_tensor(cand[:, :, :], base, float(P), cand[:, :, :], ALU.mult, ALU.add))
                nc.vector.tensor_tensor(tile_c[:, :, :], ctile[:, 1, :].unsqueeze(1).to_broadcast([P, NSORT, E1]),
                                        iota_j[:, :].unsqueeze(2).to_broadcast([P, NSORT, E1]), ALU.is_le).then_inc(sm["s_te"], 1)
                dve.wait_ge(sm["s_te"], 1)
                nc.vector.tensor_reduce(tile_f[:, :], tile_c[:, :, :], AX.X, ALU.add).then_inc(sm["s_te"], 1)
                dve.wait_ge(sm["s_te"], 2)
                nc.vector.tensor_scalar(tile_e[:, :], tile_f[:, :], float(E1 - 1), None, ALU.min).then_inc(sm["s_te"], 1)
                dve.wait_ge(sm["s_te"], 3)
                nc.vector.tensor_tensor(cand[:, :, :], cand[:, :, :], rank[:, 0, :, :], ALU.add).then_inc(sm["s_te"], 1)
                dve.wait_ge(sm["s_te"], 4)
                nc.vector.tensor_tensor(cand[:, :, :], cand[:, :, :], onehot[:, :, :], ALU.mult).then_inc(sm["s_te"], 1)
                dve.wait_ge(sm["s_te"], 5)
                nc.vector.tensor_reduce(pos_f[:, :], cand[:, :, :], AX.X, ALU.add).then_inc(sm["s_te"], 1)
                dve.wait_ge(sm["s_te"], 6)
                nc.vector.tensor_copy(pos[:, :], pos_f[:, :]).then_inc(sm["s_te"], 1)

            nc.vector.memset(half_off[0:64, :], 0.0).then_inc(sm["s_ones"], 1)
            nc.vector.memset(half_off[64:P, :], float(S)).then_inc(sm["s_ones"], 1)
            so = s_off[:, :].rearrange("p (n two) -> p n two", two=2)
            for h in range(2):
                for c in range(2):
                    nc.vector.memset(so[64 * h:64 * h + 64, :, c], float(T * (2 * c + h))).then_inc(sm["s_ones"], 1)
            for h in range(2):
                for c in (2 * h, 2 * h + 1):
                    dve.wait_ge(s_x[c], 16)
                    for t in range(4 * c, 4 * c + 4):
                        nc.vector.bn_stats(stats[:, t, :], x_sb[:, t, :]).then_inc(sm["s_st"], 1)
                ln_var(0, range(BT * h, BT * h + BT), BT * h)
            for h in range(2):
                ln_rstd(h, BT * h, BT * h + BT)
                ln_apply(range(BT * h, BT * h + BT), x_sb, xn)
            dve.wait_ge(sm["s_vo0"], 1)
            nc.vector.tensor_copy(w_vo, pH[:, 0:P]).then_inc(sm["s_vo0e"], 1)
            nc.vector.tensor_tensor(bvo[:, 0, :], pH[:, P:2 * P], bvo[:, 1, :], ALU.add).then_inc(sm["s_vo0e"], 1)
            dve.wait_ge(sm["s_bload"], 64)
            dve.wait_ge(sm["s_lg"], 1)
            nc.vector.tensor_copy(logits[:, :], pS[:, 0, :]).then_inc(sm["s_lgc"], 1)
            dst = [pS[:, 1, 0:512], pS[:, 1, 512:1024], pM[:, :], pH[:, :]]
            for c in range(NC):
                dve.wait_ge(sm["s_pj"], 3 * c + 3)
                nc.vector.tensor_copy(v_sb[:, 4 * c:4 * c + 4, :],
                                      dst[(3 * c + 2) % 4].rearrange("p (t d) -> p t d", d=D)).then_inc(sm["s_pje_v"], 1)

            dve.wait_ge(sm["s_w1load"], 64)
            dve.wait_ge(sm["s_b1load1"], 96)
            for dst_, src_ in ((brow_p, brow_qk[:, :]), (wqp, wq1[:, :]), (wkp, wku[:, 0:P])):
                nc.vector.tensor_copy(dst_[:, :].rearrange("p (g d j) -> p g d j", d=DH, j=GH),
                                      src_.rearrange("p (g j d) -> p g d j", d=DH, j=GH)).then_inc(sm["s_perm"], 1)

            def finish(i):
                dve.wait_ge(sm["s_exp"], i + 1)
                nc.vector.reciprocal(rinv[:, i:i + 1], rsum[:, i:i + 1]).then_inc(sm["s_ri"], 1)
                dve.wait_ge(sm["s_pv"], i + 1)
                if i == 0:
                    dve.wait_ge(sm["s_accz"], 16 * NACC)
                    dve.wait_ge(sm["s_xs0"], 32)
                dve.wait_ge(sm["s_ri"], i + 1)
                nc.vector.scalar_tensor_tensor(s_sb[:, i, :], (pM, pH)[i % 2][:, 0:D], rinv[:, i:i + 1], bvo[:, 0, :],
                                               ALU.mult, ALU.add).then_inc(sm["s_fin"], 1)

            def rowmax(i):
                dve.wait_ge(sm["s_S"], i + 1)
                nc.vector.tensor_reduce(nmax[:, i:i + 1], pS[:, i % 2, :], AX.X, ALU.max, negate=True).then_inc(sm["s_max"], 1)
                dve.wait_ge(sm["s_max"], i + 1)
                nc.vector.tensor_scalar(nbias[:, i:i + 1], nmax[:, i:i + 1], SC0, None, ALU.mult).then_inc(sm["s_nm"], 1)

            def top_round(r):
                if r == 0:
                    dve.wait_ge(sm["s_lgc"], 1)
                else:
                    dve.wait_ge(sm["s_t3"], r)
                r8 = slice(8 * r, 8 * r + 8)
                nc.vector.max(top_v[:, r8], logits[:, :]).then_inc(sm["s_t1"], 1)
                dve.wait_ge(sm["s_t1"], r + 1)
                nc.vector.max_index(top_i[:, r8], top_v[:, r8], logits[:, :]).then_inc(sm["s_t2"], 1)
                nc.vector.match_replace(logits[:, :], top_v[:, r8], logits[:, :], -3.0e38).then_inc(sm["s_t3"], 1)

            def merge():
                dve.wait_ge(sm["s_t2"], CAP // 8)
                dve.wait_ge(sm["s_ones"], 6)
                nc.vector.tensor_scalar(top_f[:, :], top_i[:, :], half_off[:, 0:1], None, ALU.add).then_inc(sm["s_tf"], 1)
                dve.wait_ge(sm["s_tf"], 1)
                dve.wait_ge(sm["s_hb"], 32)
                lo, hi = top_v[0:E0, :], hi_v[:, ::-1]
                lo_i, hi_i = top_f[0:E0, :], hi_f[:, ::-1]
                nc.vector.tensor_tensor(slot_v[:, :], lo, hi, ALU.max).then_inc(sm["s_sl"], 1)
                nc.vector.tensor_tensor(slot_m[:, :], lo, hi, ALU.is_ge).then_inc(sm["s_sl"], 1)
                nc.vector.tensor_tensor(slot_d[:, :], lo_i, hi_i, ALU.subtract).then_inc(sm["s_sl"], 1)
                dve.wait_ge(sm["s_sl"], 3)
                nc.vector.tensor_reduce(slot_s[:, 0:1], slot_v[:, :], AX.X, ALU.max, negate=True).then_inc(sm["s_wn"], 1)
                nc.vector.tensor_tensor(slot_d[:, :], slot_d[:, :], slot_m[:, :], ALU.mult).then_inc(sm["s_sl"], 1)
                dve.wait_ge(sm["s_sl"], 4)
                for j in range(2):
                    nc.vector.tensor_tensor(slots[:, 2 + j, :], slot_d[:, :], hi_i, ALU.add).then_inc(sm["s_sl"], 1)

            def weights():
                dve.wait_ge(sm["s_we"], 1)
                nc.vector.reciprocal(slot_s[:, 2:3], slot_s[:, 1:2]).then_inc(sm["s_wn"], 1)
                dve.wait_ge(sm["s_wn"], 2)
                nc.vector.tensor_scalar(slots[:, 0:2, :], slot_m[:, :].unsqueeze(1).to_broadcast([E0, 2, CAP]),
                                        slot_s[:, 2:3], None, ALU.mult).then_inc(sm["s_sl"], 1)

            def columns():
                dve.wait_ge(sm["s_ctr"], 1)
                for h in range(2):
                    part = slice(64 * h, 64 * h + 64)
                    for k, dst_ in ((0, w_col), (1, i_col)):
                        src = pM[part, 256 + E0 * k:256 + E0 * k + E0].rearrange("p (n two) -> p n two", two=2)
                        nc.vector.tensor_copy(dst_[part, :], src[:, :, h]).then_inc(sm["s_cc"], 1)
                dve.wait_ge(sm["s_cc"], 4)
                nc.vector.tensor_copy(g_idx[:, :], i_col[:, :]).then_inc(sm["s_so"], 1)
                nc.vector.tensor_tensor(s_idx[:, :], i_col[:, :], s_off[:, :], ALU.add).then_inc(sm["s_so"], 1)

            for i in range(NT):
                rowmax(i)
                if i >= 2:
                    finish(i - 2)
                if i < CAP // 8:
                    top_round(i)
                if i == CAP // 8:
                    merge()
                if i == CAP // 8 + 2:
                    weights()
                if i == SLOT_STEP:
                    columns()
            finish(NT - 2)
            finish(NT - 1)

            def lift(p):
                dve.wait_ge(sm["s_xgt"], p + 1)
                if p >= 2:
                    dve.wait_ge(sm["s_h"], p - 1)
                nc.vector.tensor_copy(xgT[:, p % 2, :], pT[:, p % 2, 0:P]).then_inc(sm["s_xge"], 1)

            def scale_y(p):
                dve.wait_ge(sm["s_y"], p + 1)
                if p >= 4:
                    dve.wait_ge(s_sc[p % 2], 16 * (p // 2 - 1))
                nc.vector.tensor_scalar(y_sb[:, p % 4, :], (pM, pH)[p % 2][:, 0:D], w_col[:, p:p + 1], None,
                                        ALU.mult).then_inc(sm["s_ysc"], 1)

            lift(0)
            def bias_h(p):
                dve.wait_ge(sm["s_ht"], p + 1)
                if p >= 2:
                    dve.wait_ge(sm["s_y"], p - 1)
                nc.vector.tensor_tensor(hg[:, p % 2, :].rearrange("p (e s c) -> p e s c", e=2, s=NS),
                                        pS[:, p % 2, 512:1024].rearrange("p (s e c) -> p e s c", s=NS, e=2),
                                        b1T[:, 2 * NS * p:2 * NS * (p + 1)].rearrange("p (e s) -> p e s", e=2)
                                        .unsqueeze(3).to_broadcast([P, 2, NS, 64]), ALU.add).then_inc(sm["s_hbias"], 1)

            for p in range(NP):
                if p:
                    bias_h(p - 1)
                if p + 1 < NP:
                    lift(p + 1)
                if p >= 2:
                    scale_y(p - 2)
            bias_h(NP - 1)
            scale_y(NP - 2)
            scale_y(NP - 1)
            dve.wait_ge(sm["s_xrows"], 64)

            def join_layers(b):
                for c in (2 * b, 2 * b + 1):
                    t4 = slice(4 * c, 4 * c + 4)
                    dve.wait_ge(s_x[c], 16 + 16 * NACC)
                    nc.vector.tensor_tensor(accs[:, 0:2, t4, :], accs[:, 0:2, t4, :], accs[:, 2:4, t4, :], ALU.add).then_inc(sm["s_sum"], 1)
                    dve.wait_ge(sm["s_sum"], 2 * c + 1)
                    nc.vector.tensor_tensor(accs[:, 0, t4, :], accs[:, 0, t4, :], accs[:, 1, t4, :], ALU.add).then_inc(sm["s_sum"], 1)
                for c in (2 * b, 2 * b + 1):
                    t4 = slice(4 * c, 4 * c + 4)
                    dve.wait_ge(sm["s_silu"], c + 1)
                    nc.vector.tensor_tensor(s_sb[:, t4, :], s_sb[:, t4, :], accs[:, 1, t4, :], ALU.mult).then_inc(sm["s_x1"], 1)
                    dve.wait_ge(sm["s_x1"], 2 * c + 1)
                    nc.vector.tensor_tensor(x_sb[:, t4, :], x_sb[:, t4, :], s_sb[:, t4, :], ALU.add).then_inc(sm["s_x1"], 1)
                    dve.wait_ge(sm["s_x1"], 2 * c + 2)
                    for t in range(4 * c, 4 * c + 4):
                        nc.vector.bn_stats(stats[:, t, :], x_sb[:, t, :]).then_inc(sm["s_st"], 1)
                ln_var(1, range(b * BT, b * BT + BT), b * BT)

            def join_latents(b):
                for c in (2 * b, 2 * b + 1):
                    dve.wait_ge(sm["s_lae"], 2 * c + 2)
                    half = slice(512 * (c % 2), 512 * (c % 2) + 512)
                    nc.vector.tensor_tensor(latT[:, 512 * c:512 * c + 512], latA[:, half], latB[:, half], ALU.add).then_inc(sm["s_lat"], 1)

            def experts_stats(b):
                for t in range(b * BT, b * BT + BT):
                    dve.wait_ge(sm["s_xn"], NT + t + 1)
                    nc.vector.bn_stats(stats[:, t, :], xn[:, t, :]).then_inc(sm["s_st"], 1)
                ln_var(2, range(b * BT, b * BT + BT), 0 if b == B - 1 else None)

            def take_parts(b):
                bs = slice(b * S, b * S + S)
                for st in range(2):
                    for side in range(2):
                        dve.wait_ge(sm["s_cp"], 6 * b + 2 * st + side + 1)
                        rest = qk_mem[:, side, bs]
                        nc.vector.tensor_tensor(rest, rest, parts[side][:, st, bs], ALU.subtract).then_inc(sm["s_sub"], 1)

            def bias_v(c):
                dve.wait_ge(sm["s_vv"], c + 1)
                nc.vector.tensor_tensor(v_sb[:, 4 * c:4 * c + 4, :], (pM, pH)[c % 2][:, :].rearrange("p (t d) -> p t d", d=D),
                                        brow1[:, 0:1, :].to_broadcast([P, 4, D]), ALU.add).then_inc(sm["s_v1e"], 1)

            join_layers(0)
            ln_rstd(2, 0, BT)
            ln_apply(range(BT), x_sb, xn)
            join_layers(1)
            join_latents(0)
            ln_rstd(3, BT, NT)
            ln_apply(range(BT, NT), x_sb, xn)
            experts_stats(0)
            take_parts(0)
            bias_v(0)
            bias_v(1)
            join_latents(1)
            experts_stats(1)
            take_parts(1)
            dve.wait_ge(sm["s_af"], 1)
            nc.vector.tensor_copy(aff[:, :, :].rearrange("p t e -> p (t e)"), pS[:, 0, 0:NT * E1]).then_inc(sm["s_rt"], 1)
            bias_v(2)
            bias_v(3)
            route_a(dve)
            ln_rstd(4, 0, NT)
            nc.vector.scalar_tensor_tensor(nbias[:, :], mv[:, :, 0], -1.0, rstd[:, :], ALU.mult, ALU.mult).then_inc(sm["s_lnb"], 1)

            def unit(u):
                g = u // NU
                j, heads, qt = UNITS[u % NU]
                dve.wait_ge(sm["s_u"], u + 1)
                if u % NU == 0 and g:
                    dve.wait_ge(sm["s_msp"], 5 * g)
                keys = (qt + 1) * P
                if heads == 2:
                    nc.vector.tensor_reduce(negm[:, j:j + 2, qt],
                                            pS[:, u % 2, :].rearrange("p (a k) -> p a k", a=2)[:, :, 0:keys],
                                            AX.X, ALU.max, negate=True).then_inc(sm["s_um"], 1)
                else:
                    nc.vector.tensor_reduce(negm[:, j, qt:qt + 1], pS[:, u % 2, 0:keys],
                                            AX.X, ALU.max, negate=True).then_inc(sm["s_um"], 1)
                if u % NU == NU - 1:
                    split_m(g)

            def split_m(g):
                dve.wait_ge(sm["s_um"], NU * (g + 1))
                if g:
                    dve.wait_ge(sm["s_mt"], g)
                nc.vector.tensor_copy(mparts[:, 0, :, :], negm[:, :, :]).then_inc(sm["s_msp"], 1)
                dve.wait_ge(sm["s_msp"], 5 * g + 1)
                nc.vector.tensor_tensor(negr[:, :, :], negm[:, :, :], mparts[:, 0, :, :], ALU.subtract).then_inc(sm["s_msp"], 1)
                dve.wait_ge(sm["s_msp"], 5 * g + 2)
                nc.vector.tensor_copy(mparts[:, 1, :, :], negr[:, :, :]).then_inc(sm["s_msp"], 1)
                dve.wait_ge(sm["s_msp"], 5 * g + 3)
                nc.vector.tensor_tensor(negr[:, :, :], negr[:, :, :], mparts[:, 1, :, :], ALU.subtract).then_inc(sm["s_msp"], 1)
                dve.wait_ge(sm["s_msp"], 5 * g + 4)
                nc.vector.tensor_copy(mparts[:, 2, :, :], negr[:, :, :]).then_inc(sm["s_msp"], 1)

            def rows_m(g):
                dve.wait_ge(sm["s_mt"], g + 1)
                if g:
                    dve.wait_ge(sm["s_mscr"], 16 * g)
                nc.vector.tensor_copy(mrows[:, :], pH[:, :].bitcast(bf16)[0:3 * GH * BT, 0:P]).then_inc(sm["s_mte"], 1)

            def fetch_w(j):
                if j >= 2:
                    dve.wait_ge(sm["s_fc"], j - 1)
                    dve.wait_ge(sm["s_fae"], j - 1)
                    dve.wait_ge(sm["s_fbe"], j - 1)
                    dve.wait_ge(sm["s_fce"], j - 1)
                if j == 0:
                    dve.wait_ge(sm["s_te"], 3)
                    dve.wait_ge(sm["s_pos"], 16 * NT)
                    dve.wait_ge(sm["s_wall"], 16 * (2 + E1))
                    dve.wait_ge(sm["s_smw"], 3)
                e = dve.value_load(tile_e[0:1, j:j + 1], min_val=0, max_val=E1 - 1)
                nc.vector.tensor_copy(w_tile[:, j % 2, :], wall[:, bass.ds(e, 1), 0:2 * F1].rearrange("p a n -> p (a n)")).then_inc(sm["s_wj"], 1)
                nc.vector.tensor_copy(b2_tile[:, j % 2, :], wall[:, bass.ds(e, 1), 2 * F1:2 * F1 + D].rearrange("p a n -> p (a n)")).then_inc(sm["s_wj"], 1)
                nc.vector.tensor_copy(s_tile[:, j % 2, :], smallW[:, bass.ds(e, 1), :].rearrange("p a n -> p (a n)")).then_inc(sm["s_wj"], 1)

            def add_bias(c):
                dve.wait_ge(sm["s_pj1"], c + 1)
                if c == 0:
                    dve.wait_ge(sm["s_fc"], NSORT)
                nc.vector.tensor_tensor(s_fin[:, 4 * c:4 * c + 4, :], pH[:, :].rearrange("p (t d) -> p t d", d=D),
                                        brow1[:, 1:2, :].to_broadcast([P, 4, D]), ALU.add).then_inc(sm["s_fin1"], 1)

            def weigh_experts():
                dve.wait_ge(sm["s_al"], 1)
                nc.vector.tensor_scalar(alpha[:, 1, :], alpha[:, 0, :], 1.0, None, ALU.add).then_inc(sm["s_als"], 1)
                dve.wait_ge(sm["s_als"], 1)
                nc.vector.reciprocal(alpha[:, 2, :], alpha[:, 1, :]).then_inc(sm["s_als"], 1)
                dve.wait_ge(sm["s_als"], 2)
                dve.wait_ge(sm["s_g1"], 16 * NT)
                for t in range(NT):
                    nc.vector.scalar_tensor_tensor(f_sb[:, t, :], f_sb[:, t, :], alpha[:, 2, t:t + 1], xn[:, t, :],
                                                   ALU.mult, ALU.add).then_inc(sm["s_als"], 1)

            def normalise(r):
                g, qc = r // 2, r % 2
                b, g4 = g // (NG // B), g % (NG // B)
                dve.wait_ge(sm["s_tr1"], r + 1)
                acc = pM[:, :].rearrange("p (t j c) -> p t j c", t=4, j=GH)
                nc.vector.reciprocal(rden[:, :, :], acc[:, :, :, DH]).then_inc(sm["s_rd1"], 1)
                dve.wait_ge(sm["s_rd1"], r + 1)
                t0 = b * BT + 4 * qc
                o = o_sb[:, t0:t0 + 4, g4 * GH * DH:(g4 + 1) * GH * DH].rearrange("p t (j d) -> p t j d", d=DH)
                nc.vector.tensor_tensor(o, acc[:, :, :, 0:DH], rden[:, :, :].unsqueeze(3).to_broadcast([P, 4, GH, DH]),
                                        ALU.mult).then_inc(sm["s_nrm"], 1)

            for u in range(NU):
                unit(u)
                if u == 1:
                    dve.wait_ge(sm["s_rk"], 1)
                    nc.vector.tensor_copy(rank[:, :, :, :].rearrange("p a t e -> p (a t e)"), pT[:, 0, 0:2 * NT * E1]).then_inc(sm["s_rkc"], 1)
            rows_m(0)
            for u in range(NU, units_before(0)):
                unit(u)
            route_b(dve)
            dve.wait_ge(sm["s_scr"], 16 * 12)
            for n in range(NG * NSTEP + 2):
                j, sub = ffn_part(n - 1)
                if sub == 1:
                    dve.wait_ge(sm["s_fb"], j + 1)
                    if j >= 2:
                        dve.wait_ge(sm["s_fc"], j - 1)
                    nc.vector.tensor_tensor(hs[:, j % 2, :].rearrange("p (c t) -> p c t", c=FC),
                                            pH[:, :].rearrange("p (c t) -> p c t", c=FC),
                                            s_tile[:, j % 2, 0:FC].unsqueeze(2).to_broadcast([P, FC, P]),
                                            ALU.add).then_inc(sm["s_fbe"], 1)
                if sub == 2:
                    dve.wait_ge(sm["s_fc"], j + 1)
                    if j >= 2:
                        dve.wait_ge(s_ysd[j % 2], 16 * (j // 2))
                    nc.vector.tensor_tensor(ys_sb[:, j % 2, :], pH[:, 0:D], b2_tile[:, j % 2, :],
                                            ALU.add).then_inc(sm["s_fce"], 1)
                for c, first in enumerate(OUTS):
                    if n == first + 2:
                        add_bias(c)
                for u in range(units_before(n), units_before(n + 1)):
                    unit(u)
                if n >= 2 and ends(n - 2) >= 0:
                    normalise(ends(n - 2))
                if (n + 4) % NSTEP == 0 and (n + 4) // NSTEP < NG:
                    rows_m((n + 4) // NSTEP)
                if n == FFN0 - 2:
                    fetch_w(0)
                if n == FFN0 - 1:
                    fetch_w(1)
                j, sub = ffn_part(n)
                if sub == 1 and 1 <= j and j + 1 < NSORT:
                    fetch_w(j + 1)
            weigh_experts()

            def combine(c):
                t4 = slice(4 * c, 4 * c + 4)
                dve.wait_ge(sm["s_gate"], c + 1)
                dve.wait_ge(sm["s_fin1"], c + 1)
                nc.vector.tensor_tensor(s_fin[:, t4, :], s_fin[:, t4, :], f_sb[:, t4, :], ALU.mult).then_inc(sm["s_fin2"], 1)
                dve.wait_ge(sm["s_fin2"], 2 * c + 1)
                nc.vector.tensor_tensor(x_sb[:, t4, :], x_sb[:, t4, :], s_fin[:, t4, :], ALU.add).then_inc(sm["s_fin2"], 1)

            combine(0)
            combine(1)
            add_bias(NC - 1)
            combine(2)
            combine(3)

        @block.scalar
        def _(act):
            def first_tokens_out(c):
                act.wait_ge(sm["s_xtr"], c + 1)
                nc.scalar.copy(xnT[:, c * 512:c * 512 + 512], pT[:, (c + 1) % 2, :]).then_inc(sm["s_xt"], 1)

            for h in range(2):
                act.wait_ge(sm["s_ve"], h + 1)
                nc.scalar.activation(sdev[:, BT * h:BT * h + BT], var_e[:, BT * h:BT * h + BT], ACT.Sqrt).then_inc(sm["s_sd"], 1)
            act.wait_ge(sm["s_wtr"], 1)
            nc.scalar.copy(w_T[:, :, :].rearrange("p a b -> p (a b)"), pT[:, 0, :]).then_inc(sm["s_wt"], 1)
            first_tokens_out(0)
            first_tokens_out(1)
            act.wait_ge(sm["s_wtr"], 2)
            act.wait_ge(sm["s_zero"], 3)
            nc.scalar.copy(wr_T[:, 0:E0], pM[:, 0:E0]).then_inc(sm["s_wt"], 1)
            nc.scalar.copy(bvT[:, :], pM[:, 320:448]).then_inc(sm["s_wt"], 1)
            nc.scalar.copy(b1T[:, :], pM[:, 64:64 + E0 * NS]).then_inc(sm["s_wt"], 1)
            nc.scalar.copy(cenT[:, :], pM[:, 256:256 + E1]).then_inc(sm["s_wt"], 1)
            nc.scalar.copy(smallT[:, :], pM[:, 272:272 + 6 * E1]).then_inc(sm["s_wt"], 1)
            first_tokens_out(2)
            first_tokens_out(3)
            act.wait_ge(sm["s_bload"], 64)
            dst = [pS[:, 1, 0:512], pS[:, 1, 512:1024], pM[:, :], pH[:, :]]
            for c in range(NC):
                for j in range(2):
                    n = 3 * c + j
                    act.wait_ge(sm["s_pj"], n + 1)
                    nc.scalar.activation((qT, kT)[j][:, c * 512:c * 512 + 512], dst[n % 4], ACT.Identity,
                                         bias=bqk[:, j:j + 1]).then_inc(sm["s_pje_a"], 1)

            def exps(i):
                act.wait_ge(sm["s_nm"], i + 1)
                if i >= 2:
                    act.wait_ge(sm["s_tr"], 2 * (i - 1))
                nc.scalar.activation(probs[:, i % 2, :], pS[:, i % 2, :], ACT.Exp, bias=nbias[:, i:i + 1], scale=SC0,
                                     accum_out=rsum[:, i:i + 1]).then_inc(sm["s_exp"], 1)

            for i in range(NT):
                exps(i)
                for h in range(2):
                    act.wait_ge(sm["s_tr"], 2 * i + h + 1)
                    if i >= 2:
                        act.wait_ge(sm["s_pv"], i - 1)
                    nc.scalar.copy(probsT[:, i % 2, h * 512:h * 512 + 512], pT[:, h, :]).then_inc(sm["s_ev"], 1)
                if i == CAP // 8 + 1:
                    act.wait_ge(sm["s_wn"], 1)
                    nc.scalar.activation(slot_m[:, :], slot_v[:, :], ACT.Exp, bias=slot_s[:, 0:1],
                                         accum_out=slot_s[:, 1:2]).then_inc(sm["s_we"], 1)
            def gelu_h(p):
                act.wait_ge(sm["s_hbias"], p + 1)
                nc.scalar.activation(hg[:, p % 2, :], hg[:, p % 2, :], ACT.Gelu).then_inc(sm["s_gelu"], 1)

            for p in range(NP):
                act.wait_ge(sm["s_h"], p + 1)
                if p >= 2:
                    act.wait_ge(sm["s_ht"], p - 1)
                nc.scalar.copy(hb[:, p % 2, :], pS[:, p % 2, 0:512]).then_inc(sm["s_hr"], 1)
                if p:
                    gelu_h(p - 1)
            gelu_h(NP - 1)

            def silus(b):
                for c in (2 * b, 2 * b + 1):
                    t4 = slice(4 * c, 4 * c + 4)
                    act.wait_ge(sm["s_sum"], 2 * c + 2)
                    nc.scalar.activation(accs[:, 1, t4, :], accs[:, 0, t4, :], ACT.Silu).then_inc(sm["s_silu"], 1)

            def roots(k, bt):
                act.wait_ge(sm["s_ve"], k + 1)
                nc.scalar.activation(sdev[:, bt], var_e[:, bt], ACT.Sqrt).then_inc(sm["s_sd"], 1)

            def tokens_out(b):
                for c in (2 * b, 2 * b + 1):
                    act.wait_ge(sm["s_xtr"], NC + c + 1)
                    nc.scalar.copy(xnT[:, c * 512:c * 512 + 512], pT[:, c % 2, :]).then_inc(sm["s_xt"], 1)

            def q_out(b):
                for c in (2 * b, 2 * b + 1):
                    act.wait_ge(sm["s_q1"], c + 1)
                    nc.scalar.activation(qT[:, c * 512:c * 512 + 512], pS[:, 0, (c % 2) * 512:(c % 2) * 512 + 512],
                                         ACT.Identity, bias=bcol1[:, 0:1]).then_inc(sm["s_q1e"], 1)

            def latents(b):
                for c in (2 * b, 2 * b + 1):
                    act.wait_ge(sm["s_la"], c + 1)
                    if b:
                        act.wait_ge(sm["s_lat"], c - 1)
                    for h in range(2):
                        nc.scalar.activation((latA, latB)[h][:, (c % 2) * 512:(c % 2) * 512 + 512], pT[0:LAT, h, :], ACT.Gelu,
                                             bias=bkd[:, h:h + 1]).then_inc(sm["s_lae"], 1)

            def k_out(b):
                for c in (2 * b, 2 * b + 1):
                    act.wait_ge(sm["s_kk"], c + 1)
                    nc.scalar.activation(kT[:, c * 512:c * 512 + 512], pS[:, 1, (c % 2) * 512:(c % 2) * 512 + 512],
                                         ACT.Identity, bias=bcol1[:, 1:2]).then_inc(sm["s_kke"], 1)

            def part(b, st):
                if st == 0:
                    act.wait_ge(sm["s_q1e"], 2 * b + 2)
                    act.wait_ge(sm["s_kke"], 2 * b + 2)
                bs = slice(b * S, b * S + S)
                for side in range(2):
                    if st:
                        act.wait_ge(sm["s_sub"], 4 * b + 2 * (st - 1) + side + 1)
                    nc.scalar.copy(parts[side][:, st, bs], qk_mem[:, side, bs]).then_inc(sm["s_cp"], 1)

            silus(0)
            roots(2, slice(0, BT))
            act.wait_ge(sm["s_btr"], 1)
            nc.scalar.copy(bcol1[:, :], pM[:, 0:2]).then_inc(sm["s_bte"], 1)
            act.wait_ge(sm["s_bte"], 1)
            tokens_out(0)
            silus(1)
            q_out(0)
            latents(0)
            roots(3, slice(BT, NT))
            k_out(0)
            part(0, 0)
            tokens_out(1)
            part(0, 1)
            part(0, 2)
            q_out(1)
            latents(1)
            k_out(1)
            for st in range(3):
                part(1, st)
            roots(4, slice(0, NT))
            act.wait_ge(sm["s_lnb"], 1)
            for t in range(NT):
                if t == 0:
                    act.wait_ge(sm["s_x1"], 8)
                nc.scalar.activation(s_sb[:, t, :], xn[:, t, :], ACT.Identity, bias=nbias[:, t:t + 1],
                                     scale=rstd[:, t:t + 1]).then_inc(sm["s_xn"], 1)
            act.wait_ge(sm["s_oh"], 2)
            nc.scalar.activation(alpha[:, 0, :], amax[:, :], ACT.Exp, scale=-1.0).then_inc(sm["s_al"], 1)

            def exps1(n, j):
                qc, kt, q0, cols = STEPS[n % NSTEP]
                act.wait_ge(sm["s_s1"], GH * n + j + 1)
                if n >= 2:
                    act.wait_ge(sm["s_pv1"], n - 1)
                nc.scalar.activation(pr1[:, n % 2, j, 0:cols], pT[:, j % 2, 0:cols], ACT.Exp, scale=SC1).then_inc(sm["s_e1"], 1)

            def move_heads(c):
                act.wait_ge(sm["s_ot"], c + 1)
                nc.scalar.copy(hs[:, c % 2, :], pH[:, :]).then_inc(sm["s_ote"], 1)

            for n in range(NG * NSTEP + 2):
                if n < NG * NSTEP:
                    exps1(n, 0)
                    exps1(n, 1)
                j, sub = ffn_part(n - 1)
                if sub == 0:
                    act.wait_ge(sm["s_fa"], j + 1)
                    act.wait_ge(sm["s_wj"], 3 * j + 3)
                    if j:
                        act.wait_ge(sm["s_fb"], j)
                    nc.scalar.activation(xlT[:, :], pH[:, 0:P], ACT.Identity, bias=s_tile[:, j % 2, FC + 1:FC + 2],
                                         scale=s_tile[:, j % 2, FC:FC + 1]).then_inc(sm["s_fae"], 1)
                if sub == 1:
                    act.wait_ge(sm["s_fbe"], j + 1)
                    nc.scalar.activation(hs[:, j % 2, :], hs[:, j % 2, :], ACT.Relu).then_inc(sm["s_relu"], 1)
                for c, first in enumerate(OUTS):
                    if n == first + 1:
                        move_heads(c)
                if n < NG * NSTEP:
                    exps1(n, 2)
                    exps1(n, 3)
                r = ends(n - 1)
                if r >= 0:
                    act.wait_ge(sm["s_pv1"], n)
                    if r >= 2:
                        act.wait_ge(sm["s_tr1"], r - 1)
                    nc.scalar.copy(acc_sb[:, r % 2, :], pM[:, :]).then_inc(sm["s_ace"], 1)

            def gate(c):
                t4 = slice(4 * c, 4 * c + 4)
                act.wait_ge(sm["s_als"], 2 + 4 * c + 4)
                nc.scalar.activation(f_sb[:, t4, :], f_sb[:, t4, :], ACT.Silu).then_inc(sm["s_gate"], 1)

            gate(0)
            gate(1)
            move_heads(NC - 1)
            gate(2)
            gate(3)


_INS = ['L0_attn_x', 'L0_attn_w_q', 'L0_attn_b_q', 'L0_attn_w_k', 'L0_attn_b_k', 'L0_attn_w_v', 'L0_attn_b_v',
        'L0_attn_w_out', 'L0_attn_b_out', 'L0_ffn_Wr', 'L0_ffn_W1', 'L0_ffn_b1', 'L0_ffn_W2', 'L0_ffn_b2']
_INS1 = ['L1_attn_Wq', 'L1_attn_bq', 'L1_attn_Wkd', 'L1_attn_bkd', 'L1_attn_Wku', 'L1_attn_bku', 'L1_attn_Wo',
         'L1_attn_bo', 'L1_ffn_centroids', 'L1_ffn_ln_g', 'L1_ffn_ln_b', 'L1_ffn_w1', 'L1_ffn_b1', 'L1_ffn_w2',
         'L1_ffn_b2']


def kernel(**inputs):
    import numpy as _np
    import concourse.bacc as _bacc
    from concourse import mybir as _mybir
    from concourse.bass_utils import run_bass_kernel_spmd as _run
    nc = _bacc.Bacc("TRN2", target_bir_lowering=False, num_devices=1)
    arrays, aps = {}, {}
    for name in _INS + _INS1:
        v = _np.ascontiguousarray(inputs[name])
        arrays[f"in_{name}_dram"] = v
        aps[name] = nc.dram_tensor(f"in_{name}_dram", v.shape, _mybir.dt.from_np(v.dtype), kind="ExternalInput").ap()
    o = nc.dram_tensor("out_0_dram", (2, 1024, 128), _mybir.dt.float32, kind="ExternalOutput").ap()
    build(nc, aps, o)
    r = _run(nc, [arrays], core_ids=[0])
    return r.results[0]["out_0_dram"]
```

```python
import concourse.bass as bass
from concourse import mybir
from contextlib import ExitStack


def build(nc, a, out):
    fp32 = mybir.dt.float32
    bf16 = mybir.dt.bfloat16
    u32 = mybir.dt.uint32
    ALU = mybir.AluOpType
    ACT = mybir.ActivationFunctionType
    AX = mybir.AxisListType

    x_dram, wr_dram = a["L0_attn_x"], a["L0_ffn_Wr"]
    B, S, D = x_dram.shape
    P = 128
    T = B * S
    NT = T // P
    BT = S // P
    E0 = wr_dram.shape[0]
    NS, KY = a["L0_ffn_W2"].shape[1], a["L0_ffn_W2"].shape[3]
    CAP = int(1.5 * T / E0)
    NP = E0 // 2
    RING = 12
    EPS = 1e-5
    SC0 = float(D) ** -0.5
    NC = T // 512
    H1, DH = 16, 8
    SC1 = float(DH) ** -0.5
    E1, _, F1 = a["L1_ffn_w1"].shape
    FC = F1 // P
    LAT = a["L1_attn_Wku"].shape[0]
    GH = 4
    NG = B * H1 // GH
    KQ = 72
    KM = KQ + 3
    NSORT = NT + E1 - 1
    NEG = -1.0e30
    STEPS = []
    for qc in range(S // 512):
        for kt in range(4 * qc + 4):
            q0 = max(kt * P, qc * 512)
            STEPS.append((qc, kt, q0, (qc + 1) * 512 - q0))
    NSTEP = len(STEPS)
    UNITS = []
    for u in range(8):
        UNITS += [(u // 2, 1, 4 + 2 * (u % 2)), (u // 2, 1, 5 + 2 * (u % 2)), (2 * (u // 4), 2, u % 4)]
    NU = len(UNITS)
    SLOT_STEP = 12
    AHEAD = NU + 8
    FFN0 = 11
    OUT0 = FFN0 + 3 * NSORT + 1
    OUTS = [OUT0, OUT0 + 3, NG * NSTEP - 6]

    SPREAD0 = (NG * NU - AHEAD) // 2

    def gathered(n):
        m = sum(1 if STEPS[i % NSTEP][2] == STEPS[i % NSTEP][1] * P else 2 for i in range(OUT0 + 1, n))
        return min(NT, m)

    def units_before(n):
        return min(NG * NU, NU + 5 + 3 * n, AHEAD + 2 * n)

    ctx = ExitStack()
    with ctx:
        def sb(name, shape, dt=fp32):
            return ctx.enter_context(nc.sbuf_tensor(name, shape, dt))

        def pb(name, shape, dt=fp32):
            return ctx.enter_context(nc.psum_tensor(name, shape, dt))

        def sem(name):
            return ctx.enter_context(nc.semaphore(name))

        xn_rows = nc.dram_tensor("xn_rows", [T, D], fp32, kind="Internal").ap()
        NACC = 4
        acc_rows = nc.dram_tensor("acc_rows", [NACC * T, D], fp32, kind="Internal").ap()
        q_scr = nc.dram_tensor("q_scr", [B, 3, NG // B, DH, GH * S], bf16, kind="Internal").ap()
        k_scr = nc.dram_tensor("k_scr", [B, 3, NG // B, DH, GH * S], bf16, kind="Internal").ap()
        m_scr = nc.dram_tensor("m_scr", [NG, 3 * GH * BT, P], bf16, kind="Internal").ap()
        xs_rows = nc.dram_tensor("xs_rows", [NSORT * P, D], fp32, kind="Internal").ap()
        ys_rows = nc.dram_tensor("ys_rows", [NSORT * P, D], fp32, kind="Internal").ap()

        ident = sb("ident", [P, P])
        x_sb = sb("x_sb", [P, NT, D])
        xn = sb("xn", [P, NT, D])
        xnT = sb("xnT", [P, T])
        qk_mem = sb("qk_mem", [P, 2, T])
        qT, kT = qk_mem[:, 0, :], qk_mem[:, 1, :]
        v_sb = sb("v_sb", [P, NT, D])
        s_sb = sb("s_sb", [P, NT, D])
        stats = sb("stats", [P, NT, 6])
        mv = sb("mv", [P, NT, 2])
        rstd = sb("rstd", [P, NT])
        var_e = sb("var_e", [P, NT])
        sdev = sb("sdev", [P, NT])
        newt = sb("newt", [P, NT])
        w_in = sb("w_in", [P, 4, P])
        w_T = sb("w_T", [P, 4, P])
        wr_in = sb("wr_in", [E0, D])
        wr_T = sb("wr_T", [P, 64])
        bqk = sb("bqk", [P, 2])
        bvo = sb("bvo", [P, 2, D])
        zeros = s_sb
        mem1 = sb("mem1", [P, E1 * (2 * F1 + D)])
        logits = mem1[:, 0:S]
        top_v = sb("top_v", [P, CAP])
        top_i = sb("top_i", [P, CAP], u32)
        top_f = sb("top_f", [P, CAP])
        half_off = sb("half_off", [P, 1])
        hi_v = sb("hi_v", [E0, CAP])
        hi_f = sb("hi_f", [E0, CAP])
        slot_v = sb("slot_v", [E0, CAP])
        slot_m = sb("slot_m", [E0, CAP])
        slot_d = sb("slot_d", [E0, CAP])
        slot_s = sb("slot_s", [E0, 4])
        slots = sb("slots", [E0, 4, CAP])
        w_col = sb("w_col", [P, NP])
        i_col = sb("i_col", [P, NP])
        s_off = sb("s_off", [P, NP])
        g_idx = sb("g_idx", [P, NP], u32)
        s_idx = sb("s_idx", [P, NP], u32)
        probs = mem1[:, S:3 * S].rearrange("p (a s) -> p a s", a=2)
        probsT = mem1[:, 3 * S:5 * S].rearrange("p (a s) -> p a s", a=2)
        nmax = sb("nmax", [P, NT])
        nbias = sb("nbias", [P, NT])
        rsum = sb("rsum", [P, NT])
        rinv = sb("rinv", [P, NT])
        bvT = sb("bvT", [P, P])
        w_vo = w_in[:, 0, :]
        w1r = sb("w1r", [P, RING, 2 * NS, P])
        w2s = sb("w2s", [P, E0 * NS, KY])
        b1_in = sb("b1_in", [96, 2, P])
        b1T = sb("b1T", [P, E0 * NS])
        pairind = sb("pairind", [2, P])
        b2p = mem1[0:2, S:S + NP * D].rearrange("p (n d) -> p n d", d=D)
        xg = mem1[:, 5 * S:5 * S + NP * D].rearrange("p (n d) -> p n d", d=D)
        xgT = sb("xgT", [P, 2, P])
        hb = sb("hb", [P, 2, 512])
        hg = sb("hg", [P, 2, 512])
        y_sb = sb("y_sb", [P, 4, D])
        w1r_flat = w1r[:, :, :, :].rearrange("p a b c -> p (a b c)")
        w2s_flat = w2s[:, :, :].rearrange("p a b -> p (a b)")
        accs = w1r_flat[:, 0:NACC * T].rearrange("p (a t d) -> p a t d", a=NACC, d=D)
        identb = sb("identb", [P, P], bf16)
        causal = sb("causal", [P, P], bf16)
        before = sb("before", [P, P], bf16)
        onesb = sb("onesb", [P, P], bf16)
        wq1 = sb("wq1", [P, P])
        wkd = sb("wkd", [P, 2 * LAT])
        wku = sb("wku", [2 * LAT, 2 * P])
        wo1 = sb("wo1", [P, P])
        brow_qk = sb("brow_qk", [2, P])
        brow_p = sb("brow_p", [2, P])
        wqp = sb("wqp", [P, P])
        wkp = sb("wkp", [2 * LAT, P])
        bcol1 = sb("bcol1", [P, 2])
        bkd = sb("bkd", [2 * LAT, 1])
        brow1 = sb("brow1", [P, 2, D])
        cen_in = sb("cen_in", [E1, D])
        cenT = sb("cenT", [P, E1])
        small_in = sb("small_in", [6 * E1, D])
        smallT = sb("smallT", [P, 6 * E1])
        wall = mem1[:, :].rearrange("p (e n) -> p e n", e=E1)
        w_tile = s_sb[:, :, :].rearrange("p t d -> p (t d)").rearrange("p (a n) -> p a n", a=2)
        b2_tile = sb("b2_tile", [P, 2, D])
        s_tile = sb("s_tile", [P, 2, 6])
        latT = w1r_flat[0:2 * LAT, NACC * T:NACC * T + T]
        parts_mem = w2s_flat.bitcast(bf16)
        parts = [parts_mem[:, 3 * T * i:3 * T * i + 3 * T].rearrange("p (a t) -> p a t", a=3) for i in range(2)]
        stack_mem = w1r_flat.bitcast(bf16)
        SM = GH * S

        def stack(side, g):
            o = (2 * (g % 3) + side) * SM
            return stack_mem[:, o:o + SM].rearrange("p (j t) -> p j t", j=GH)
        pr1 = qk_mem[:, :, :].rearrange("p a t -> p (a t)").rearrange("p (r j t) -> p r j t", r=2, j=GH)
        v_ext = xnT[:, :].rearrange("p (a t j c) -> p a t j c", a=2, t=BT, j=GH)
        s_fin = s_sb
        o_sb = w2s_flat[:, 0:T].rearrange("p (t d) -> p t d", d=D)
        f_sb = w2s_flat[:, T:2 * T].rearrange("p (t d) -> p t d", d=D)
        acc_sb = hb
        smallW = sb("smallW", [P, E1, 6])
        xs_in = y_sb
        xlT = sb("xlT", [P, P])
        hs = hg
        ys_sb = sb("ys_sb", [P, 2, D])
        negm = sb("negm", [P, GH, BT])
        negr = sb("negr", [P, GH, BT])
        mparts = sb("mparts", [P, 3, GH, BT], bf16)
        mrows = sb("mrows", [3 * GH * BT, P], bf16)
        rden = sb("rden", [P, 4, GH])
        rt_mem = hg[:, :, :].rearrange("p a n -> p (a n)")
        aff, cand, onehot, full = [rt_mem[:, i * NT * E1:(i + 1) * NT * E1] for i in range(4)]
        aff, cand, onehot = [v.rearrange("p (t e) -> p t e", e=E1) for v in (aff, cand, onehot)]
        full = full.rearrange("p (e t) -> p e t", e=E1)
        rank = rt_mem[:, 4 * NT * E1:6 * NT * E1].rearrange("p (a t e) -> p a t e", a=2, e=E1)
        cum = rt_mem[:, 6 * NT * E1:8 * NT * E1].rearrange("p (a t e) -> p a t e", a=2, e=E1)
        tile_c = hb[:, 0, 0:NSORT * E1].rearrange("p (j e) -> p j e", e=E1)
        amax = sb("amax", [P, NT])
        emin = sb("emin", [P, NT])
        onehotb = sb("onehotb", [P, NT, E1], bf16)
        ctile = sb("ctile", [P, 4, E1])
        em8 = sb("em8", [P, E1])
        m128 = sb("m128", [P, NT])
        iota_j = sb("iota_j", [P, NSORT])
        tile_f = sb("tile_f", [P, NSORT])
        tile_e = sb("tile_e", [P, NSORT], mybir.dt.int32)
        pos_f = sb("pos_f", [P, NT])
        pos = sb("pos", [P, NT], u32)
        alpha = sb("alpha", [P, 3, NT])

        pS = pb("pS", [P, 2, S])
        pT = pb("pT", [P, 2, 512])
        pM = pb("pM", [P, 512])
        pH = pb("pH", [P, 512])

        names = ("s_const s_xrows s_zero s_ones "
                 "s_st s_mv s_ve s_sd s_rstd s_xn s_wload s_wrload s_bload s_b1load s_b2load s_w2load "
                 "s_wtr s_wt s_xtr s_xt s_vo0 s_vo0e s_lg s_lgc s_pj s_pje_a s_pje_v "
                 "s_S s_max s_nm s_exp s_tr s_ev s_pv s_ri s_fin "
                 "s_t1 s_t2 s_t3 s_tf s_hb s_sl s_we s_wn s_ctr s_cc s_so "
                 "s_k1 s_w1load s_b1load1 s_cload s_wall s_xs0 s_silu s_x1 s_af s_rt s_oh s_rk s_rkc "
                 "s_q1 s_q1e s_la s_lae s_kk s_kke s_vv s_v1e s_cp s_sub s_scr "
                 "s_u s_um s_msp s_mt s_mte s_mrow s_s1 s_e1 s_sel s_pv1 s_ace s_tr1 s_rd1 s_nrm s_ve_b "
                 "s_pos s_te s_wj s_fa s_fae s_fb s_fbe s_relu s_fc s_fce s_al s_als s_gate "
                 "s_fin2 s_perm s_btr s_bte s_mscr s_ot s_ote s_pj1 s_fin1 s_vz s_vo s_smw s_lnb "
                 "s_xgt s_xge s_h s_hr s_ht s_hbias s_gelu s_y s_ysc s_accz s_sum s_sum2 s_out").split()
        sm = {n: sem(n) for n in names}
        s_x = [sem(f"s_xin{c}") for c in range(4)]
        s_g = [sem(f"s_gat{i}") for i in range(4)]
        s_w1 = [sem(f"s_w1_{i}") for i in range(RING)]
        s_sc = [sem(f"s_sc{i}") for i in range(2)]
        s_stk = [sem(f"s_stk{i}") for i in range(3)]
        s_ysd = [sem(f"s_ysd{i}") for i in range(2)]
        s_xsl = [sem(f"s_xsl{i}") for i in range(4)]
        block = ctx.enter_context(nc.Block())

        x_t = x_dram.rearrange("b (t p) d -> p (b t) d", p=P)
        out_t = out.rearrange("b (t p) d -> p (b t) d", p=P)
        xn_t = xn_rows.rearrange("(t p) d -> p t d", p=P)
        acc_t = acc_rows.rearrange("(a t p) d -> p a t d", p=P, a=NACC)
        w1_v = a["L0_ffn_W1"].rearrange("e s d m -> d (e s) m")
        w2_v = a["L0_ffn_W2"].rearrange("e s m k -> m (e s) k")

        def q_bank(c):
            return pS[:, 0, c * 512:c * 512 + 512] if c < 2 else (pM, pH)[c % 2][:, :]

        def k_bank(c):
            return pS[:, 1, c * 512:c * 512 + 512] if c < 2 else pT[:, c % 2, :]

        def part_count(b, side, st):
            return 4 * b + 2 * st + side + 1

        def ffn_part(n):
            m = n - FFN0
            return (m // 3, m % 3) if 0 <= m < 3 * NSORT else (-1, -1)

        def sel_count(n):
            return sum(1 for m in range(n + 1) if STEPS[m % NSTEP][2] == STEPS[m % NSTEP][1] * P)

        def ends(n):
            if n < 0 or n >= NG * NSTEP:
                return -1
            qc, kt = STEPS[n % NSTEP][:2]
            return 2 * (n // NSTEP) + qc if kt == 4 * qc + 3 else -1

        def ffn_count(n):
            return min(max(n - FFN0, 0), 3 * NSORT)

        def wait_ffn(eng, m):
            j, sub = (m - 1) // 3, (m - 1) % 3
            eng.wait_ge(sm[("s_fae", "s_fbe", "s_fce")[sub]], j + 1)

        def stack_ready(eng, g):
            eng.wait_ge(s_stk[g % 3], 16 * 6 * (g // 3 + 1))

        @block.sync
        def _(sp):
            for c in range(4):
                sp.dma_start(x_sb[:, 4 * c:4 * c + 4, :], x_t[:, 4 * c:4 * c + 4, :]).then_inc(s_x[c], 16)
            for j in range(4):
                w = a[("L0_attn_w_q", "L0_attn_w_k", "L0_attn_w_v", "L0_attn_w_out")[j]]
                sp.dma_start(w_in[:, j, :], w).then_inc(sm["s_wload"], 16)
            sp.dma_start(wr_in[:, :], wr_dram).then_inc(sm["s_wrload"], 16)
            for j in range(2):
                bcol = a[("L0_attn_b_q", "L0_attn_b_k")[j]]
                sp.dma_start(bqk[:, j:j + 1], bcol.rearrange("(p a) -> p a", a=1)).then_inc(sm["s_bload"], 16)
                brow = a[("L0_attn_b_v", "L0_attn_b_out")[j]]
                sp.dma_start(bvo[:, j, :], brow.partition_broadcast(P)).then_inc(sm["s_bload"], 16)
            b1_v = a["L0_ffn_b1"].rearrange("e s m -> (e s) m")
            for j in range(2):
                sp.dma_start(b1_in[:, j, :], b1_v[96 * j:96 * j + 96, :]).then_inc(sm["s_b1load"], 16)
            sp.dma_start(cen_in[:, :], a["L1_ffn_centroids"]).then_inc(sm["s_cload"], 16)
            sp.dma_start(small_in[0:4 * E1, :], a["L1_ffn_b1"].rearrange("e (c p) -> (e c) p", p=P)).then_inc(sm["s_cload"], 16)
            sp.dma_start(small_in[4 * E1:5 * E1, :], a["L1_ffn_ln_g"]).then_inc(sm["s_cload"], 16)
            sp.dma_start(small_in[5 * E1:6 * E1, :], a["L1_ffn_ln_b"]).then_inc(sm["s_cload"], 16)
            sp.dma_start(wq1[:, :], a["L1_attn_Wq"]).then_inc(sm["s_w1load"], 16)
            sp.dma_start(wkd[:, :], a["L1_attn_Wkd"]).then_inc(sm["s_w1load"], 16)
            for h in range(2):
                sp.dma_start(wku[LAT * h:LAT * h + LAT, :], a["L1_attn_Wku"]).then_inc(sm["s_w1load"], 16)
            sp.dma_start(wo1[:, :], a["L1_attn_Wo"]).then_inc(sm["s_w1load"], 16)
            col = lambda v: v.rearrange("(p a) -> p a", a=1)
            bku, bkd_v = a["L1_attn_bku"], a["L1_attn_bkd"]
            row = lambda v: v.rearrange("(a p) -> a p", a=1)
            sp.dma_start(brow_qk[0:1, :], row(a["L1_attn_bq"])).then_inc(sm["s_b1load1"], 16)
            sp.dma_start(brow_qk[1:2, :], row(bku[0:P])).then_inc(sm["s_b1load1"], 16)
            sp.dma_start(bkd[:, :], col(bkd_v)).then_inc(sm["s_b1load1"], 16)
            sp.dma_start(brow1[:, 0, :], bku[P:2 * P].partition_broadcast(P)).then_inc(sm["s_b1load1"], 16)
            sp.dma_start(brow1[:, 1, :], a["L1_attn_bo"].partition_broadcast(P)).then_inc(sm["s_b1load1"], 16)
            sp.wait_ge(sm["s_const"], 1)
            xs_t = xs_rows.rearrange("(j p) d -> p j d", p=P)
            zer = zeros[:, :, :]
            sp.dma_start(xs_t[:, 0:NT, :], zer).then_inc(sm["s_xs0"], 16)
            sp.dma_start(xs_t[:, NT:NSORT, :], zer[:, 0:NSORT - NT, :]).then_inc(sm["s_xs0"], 16)
            for j in range(NACC):
                sp.dma_start(acc_t[:, j, :, :], zeros[:, :, :]).then_inc(sm["s_accz"], 16)
            for c in range(4):
                sp.wait_ge(sm["s_xn"], 4 * c + 4)
                sp.dma_start(xn_t[:, 4 * c:4 * c + 4, :], xn[:, 4 * c:4 * c + 4, :]).then_inc(sm["s_xrows"], 16)
            for p in range(4):
                sp.dma_start(w1r[:, p, :, :], w1_v[:, 8 * p:8 * p + 8, :]).then_inc(s_w1[p], 16)
            for j in range(4):
                sp.dma_start(w2s[:, 48 * j:48 * j + 48, :], w2_v[:, 48 * j:48 * j + 48, :]).then_inc(sm["s_w2load"], 16)
            for p in range(4, RING):
                sp.dma_start(w1r[:, p, :, :], w1_v[:, 8 * p:8 * p + 8, :]).then_inc(s_w1[p], 16)
            sp.wait_ge(sm["s_tf"], 1)
            sp.dma_start(hi_v[:, :], top_v[64:64 + E0, :]).then_inc(sm["s_hb"], 16)
            sp.dma_start(hi_f[:, :], top_f[64:64 + E0, :]).then_inc(sm["s_hb"], 16)
            sp.wait_ge(sm["s_pv"], NT)
            sp.dma_start(b2p, a["L0_ffn_b2"].rearrange("(p r) s k -> r p (s k)", r=2)).then_inc(sm["s_b2load"], 16)
            for p in range(RING, NP):
                sp.wait_ge(sm["s_h"], p - RING + 1)
                sp.dma_start(w1r[:, p - RING, :, :], w1_v[:, 8 * p:8 * p + 8, :]).then_inc(s_w1[p - RING], 16)
            for i in range(2):
                sp.wait_ge(s_sc[i], 16 * (NP // 2))
            sp.wait_ge(sm["s_h"], NP)
            for c in range(4):
                for j in range(NACC):
                    sp.dma_start(accs[:, j, 4 * c:4 * c + 4, :], acc_t[:, j, 4 * c:4 * c + 4, :]).then_inc(s_x[c], 16)
            w1f = a["L1_ffn_w1"].rearrange("e d f -> d e f")
            w2f = a["L1_ffn_w2"].rearrange("e (c p) d -> p e c d", p=P)
            sp.dma_start(wall[:, :, 0:F1], w1f).then_inc(sm["s_wall"], 16)
            for e in range(E1):
                sp.dma_start(wall[:, e, F1:2 * F1].rearrange("p (c d) -> p c d", d=D), w2f[:, e, :, :]).then_inc(sm["s_wall"], 16)
            sp.dma_start(wall[:, :, 2 * F1:2 * F1 + D], a["L1_ffn_b2"].partition_broadcast(P)).then_inc(sm["s_wall"], 16)

            def load_stack(g):
                b, g4 = g // (NG // B), g % (NG // B)
                sp.wait_ge(sm["s_scr"], 16 * 6 * (b + 1))
                if g < 3:
                    sp.wait_ge(sm["s_vo"], g + 1)
                if g == 2:
                    sp.wait_ge(sm["s_vv"], NC)
                if g >= 3:
                    sp.wait_ge(sm["s_s1"], GH * NSTEP * (g - 2))
                for x in range(3):
                    rows = slice(3 * DH * x, 3 * DH * x + 3 * DH)
                    for side in range(2):
                        part = (q_scr[b, x, g4].unsqueeze(0).to_broadcast([3, DH, GH * S]), k_scr[b, :, g4])[side]
                        sp.dma_start(stack(side, g)[rows, :, :].rearrange("p j t -> p (j t)"),
                                     part).then_inc(s_stk[g % 3], 16)

            def store_parts(b):
                for st in range(3):
                    for side in range(2):
                        sp.wait_ge(sm["s_cp" if st < 2 else "s_sub"], part_count(b, side, min(st, 1)))
                        sp.dma_start((q_scr, k_scr)[side][b, st].rearrange("g d (j t) -> (g d j) t", j=GH),
                                     parts[side][:, st, b * S:b * S + S]).then_inc(sm["s_scr"], 16)

            def store_m(g):
                sp.wait_ge(sm["s_mte"], g + 1)
                sp.dma_start(m_scr[g], mrows[:, :]).then_inc(sm["s_mscr"], 16)
                sp.wait_ge(sm["s_mscr"], 16 * (g + 1))
                sp.dma_start(stack(0, g)[KQ:KM, :, :].rearrange("p j t -> p (j t)"),
                             m_scr[g].rearrange("(a n) q -> a (n q)", a=3)).then_inc(sm["s_mrow"], 16)

            store_parts(0)
            load_stack(0)
            store_parts(1)
            load_stack(1)
            load_stack(2)
            store_m(0)
            sp.wait_ge(sm["s_pos"], 16 * NT)
            for j in range(3):
                sp.dma_start(xs_in[:, j % 4, :], xs_t[:, j, :]).then_inc(s_xsl[j % 4], 16)
            for n in range(NG * NSTEP + 2):
                g = (n + 4) // NSTEP
                if (n + 4) % NSTEP == 0 and g < NG:
                    store_m(g)
                if n % NSTEP == 0 and n // NSTEP + 2 < NG and n:
                    load_stack(n // NSTEP + 2)
                j, sub = ffn_part(n)
                if sub == 0 and j + 3 < NSORT:
                    if j >= 1:
                        sp.wait_ge(sm["s_fa"], j)
                    sp.dma_start(xs_in[:, (j + 3) % 4, :], xs_t[:, j + 3, :]).then_inc(s_xsl[(j + 3) % 4], 16)
                if sub == 2:
                    sp.wait_ge(sm["s_fce"], j + 1)
                    sp.dma_start(ys_rows[j * P:j * P + P, :], ys_sb[:, j % 2, :]).then_inc(s_ysd[j % 2], 16)
            for c in range(4):
                sp.wait_ge(sm["s_fin2"], 2 * c + 2)
                sp.dma_start(out_t[:, 4 * c:4 * c + 4, :], x_sb[:, 4 * c:4 * c + 4, :]).then_inc(sm["s_out"], 16)
            for i in range(2):
                sp.wait_ge(s_ysd[i], 16 * ((NSORT + 1 - i) // 2))
            sp.wait_ge(sm["s_scr"], 16 * 12)
            sp.wait_ge(sm["s_xrows"], 64)
            sp.wait_ge(sm["s_xs0"], 32)
            sp.wait_ge(sm["s_accz"], 16 * NACC)
            sp.wait_ge(sm["s_out"], 64)

        @block.gpsimd
        def _(pool):
            pool.memset(zeros[:, :, :], 0.0).then_inc(sm["s_const"], 1)
            pool.memset(ident[:, :], 0.0).then_inc(sm["s_zero"], 1)
            pool.memset(wr_T[:, :], 0.0).then_inc(sm["s_zero"], 1)
            pool.memset(pairind[:, :], 0.0).then_inc(sm["s_zero"], 1)
            pool.memset(identb[:, :], 0.0).then_inc(sm["s_k1"], 1)
            pool.memset(causal[:, :], 0.0).then_inc(sm["s_k1"], 1)
            pool.memset(before[:, :], 1.0).then_inc(sm["s_k1"], 1)
            pool.memset(onesb[:, :], 1.0).then_inc(sm["s_k1"], 1)
            pool.iota(em8[:, :], [[1, E1]], base=-E1, channel_multiplier=0, allow_small_or_imprecise_dtypes=True).then_inc(sm["s_k1"], 1)
            pool.iota(m128[:, :], [[P, NT]], base=0, channel_multiplier=0, allow_small_or_imprecise_dtypes=True).then_inc(sm["s_k1"], 1)
            pool.iota(iota_j[:, :], [[1, NSORT]], base=0, channel_multiplier=0, allow_small_or_imprecise_dtypes=True).then_inc(sm["s_k1"], 1)
            pool.wait_ge(sm["s_k1"], 7)
            pool.affine_select(out=identb[:, :], in_=identb[:, :], compare_op=ALU.not_equal, fill=1.0,
                               base=0, pattern=[[-1, P]], channel_multiplier=1).then_inc(sm["s_k1"], 1)
            pool.affine_select(out=causal[:, :], in_=causal[:, :], compare_op=ALU.is_ge, fill=NEG,
                               base=0, pattern=[[-1, P]], channel_multiplier=1).then_inc(sm["s_k1"], 1)
            pool.affine_select(out=before[:, :], in_=before[:, :], compare_op=ALU.is_gt, fill=0.0,
                               base=0, pattern=[[1, P]], channel_multiplier=-1).then_inc(sm["s_k1"], 1)
            pool.wait_ge(sm["s_zero"], 3)
            pool.affine_select(out=ident[:, :], in_=ident[:, :], compare_op=ALU.not_equal, fill=1.0,
                               base=0, pattern=[[-1, P]], channel_multiplier=1).then_inc(sm["s_const"], 1)
            pool.affine_select(out=pairind[:, :].rearrange("r (e c) -> r e c", e=2),
                               in_=pairind[:, :].rearrange("r (e c) -> r e c", e=2), compare_op=ALU.not_equal, fill=1.0,
                               base=0, pattern=[[-1, 2], [0, 64]], channel_multiplier=1).then_inc(sm["s_const"], 1)

            pool.wait_ge(sm["s_xrows"], 64)
            pool.wait_ge(sm["s_so"], 2)

            def gather(p):
                if p >= 4:
                    pool.wait_ge(s_g[p % 4], 16 * (p // 4))
                pool.indirect_dma_start(out=xg[:, p, :], out_offset=None, in_=xn_rows,
                                        in_offset=bass.IndirectOffsetOnAxis(ap=g_idx[:, p:p + 1], axis=0),
                                        ).then_inc(s_g[p % 4], 16)
            for p in range(6):
                gather(p)
            pool.wait_ge(sm["s_accz"], 16 * NACC)
            for p in range(NP):
                if p + 6 < NP:
                    gather(p + 6)
                pool.wait_ge(sm["s_ysc"], p + 1)
                if p >= 2:
                    pool.wait_ge(s_sc[p % 2], 16 * (p // 2))
                pool.indirect_dma_start(out=acc_rows,
                                        out_offset=bass.IndirectOffsetOnAxis(ap=s_idx[:, p:p + 1], axis=0),
                                        in_=y_sb[:, p % 4, :], in_offset=None,
                                        compute_op=ALU.add).then_inc(s_sc[p % 2], 16)

            def build_v(g):
                if g >= 2:
                    pool.wait_ge(sm["s_pv1"], NSTEP * (g - 1))
                b, g4 = g // (NG // B), g % (NG // B)
                src = v_sb[:, b * BT:b * BT + BT, g4 * GH * DH:(g4 + 1) * GH * DH].rearrange("p t (j d) -> p t j d", d=DH)
                pool.tensor_copy(v_ext[:, g % 2, :, :, 0:DH], src).then_inc(sm["s_ve_b"], 1)

            for c in (2, 3):
                t4 = slice(4 * c, 4 * c + 4)
                pool.wait_ge(s_x[c], 16 + 16 * NACC)
                pool.tensor_tensor(accs[:, 0:2, t4, :], accs[:, 0:2, t4, :], accs[:, 2:4, t4, :], ALU.add).then_inc(sm["s_sum2"], 1)
                pool.wait_ge(sm["s_sum2"], 2 * (c - 2) + 1)
                pool.tensor_tensor(accs[:, 0, t4, :], accs[:, 0, t4, :], accs[:, 1, t4, :], ALU.add).then_inc(sm["s_sum2"], 1)
            pool.wait_ge(sm["s_x1"], 8)
            for g in range(3):
                pool.memset(stack(1, g)[64:KM, :, :], 1.0).then_inc(sm["s_vo"], 1)
            pool.wait_ge(sm["s_v1e"], NC)
            pool.wait_ge(sm["s_vv"], NC)
            pool.wait_ge(sm["s_af"], 1)
            pool.wait_ge(sm["s_vo"], 3)
            pool.memset(xnT[:, :], 0.0).then_inc(sm["s_vz"], 1)
            pool.wait_ge(sm["s_vz"], 1)
            pool.memset(v_ext[:, :, :, :, DH:DH + 1], 1.0).then_inc(sm["s_vz"], 1)
            build_v(0)
            build_v(1)
            pool.wait_ge(sm["s_te"], 7)
            pool.wait_ge(sm["s_xn"], 3 * NT)
            pool.wait_ge(sm["s_xs0"], 32)

            def sort_tile(t):
                pool.indirect_dma_start(out=xs_rows, out_offset=bass.IndirectOffsetOnAxis(ap=pos[:, t:t + 1], axis=0),
                                        in_=s_sb[:, t, :], in_offset=None).then_inc(sm["s_pos"], 16)

            for t in range(2):
                sort_tile(t)

            for n in range(NG * NSTEP + 2):
                if n < NG * NSTEP:
                    qc, kt, q0, cols = STEPS[n % NSTEP]
                    if q0 == kt * P:
                        pool.wait_ge(sm["s_e1"], GH * n + GH)
                        blk_ = pr1[:, n % 2, :, 0:P]
                        pool.affine_select(out=blk_, in_=blk_, compare_op=ALU.is_ge, fill=0.0, base=0,
                                           pattern=[[0, GH], [1, P]], channel_multiplier=-1).then_inc(sm["s_sel"], 1)
                for t in range(2 * n + 2, 2 * n + 4) if 2 * n + 2 < NT else ():
                    sort_tile(t)
                if n % NSTEP == NSTEP - 3 and 2 <= n // NSTEP + 1 < NG:
                    build_v(n // NSTEP + 1)
                if n == OUT0 + 1:
                    for i in range(2):
                        pool.wait_ge(s_ysd[i], 16 * ((NSORT + 1 - i) // 2))
                for t in range(gathered(n), gathered(n + 1)):
                    pool.indirect_dma_start(out=f_sb[:, t, :], out_offset=None, in_=ys_rows,
                                            in_offset=bass.IndirectOffsetOnAxis(ap=pos[:, t:t + 1], axis=0)).then_inc(s_g[t // 4], 16)

        @block.tensor
        def _(pe):
            def turn_first(c):
                pe.wait_ge(sm["s_xn"], 4 * c + 4)
                if c == 1:
                    pe.wait_ge(sm["s_wt"], 1)
                if c >= 2:
                    pe.wait_ge(sm["s_xt"], c - 1)
                for j in range(4):
                    last = nc.tensor.transpose(pT[:, (c + 1) % 2, j * P:j * P + P], xn[:, 4 * c + j, :], ident[:, :])
                last.then_inc(sm["s_xtr"], 1)

            pe.wait_ge(sm["s_const"], 3)
            pe.wait_ge(sm["s_wload"], 64)
            for j in range(4):
                last = nc.tensor.transpose(pT[:, 0, j * P:j * P + P], w_in[:, j, :], ident[:, :])
            last.then_inc(sm["s_wtr"], 1)
            turn_first(0)
            turn_first(1)
            pe.wait_ge(sm["s_wrload"], 16)
            pe.wait_ge(sm["s_b1load"], 32)
            nc.tensor.transpose(pM[:, 0:E0], wr_in[:, :], ident[0:E0, 0:E0])
            for j in range(2):
                last = nc.tensor.transpose(pM[:, 64 + 96 * j:160 + 96 * j], b1_in[:, j, :], ident[0:96, 0:96])
            pe.wait_ge(sm["s_bload"], 64)
            nc.tensor.transpose(pM[:, 320:448], bvo[:, 0, :], ident[:, :])
            pe.wait_ge(sm["s_cload"], 64)
            nc.tensor.transpose(pM[:, 256:256 + E1], cen_in[:, :], ident[0:E1, 0:E1])
            last = nc.tensor.transpose(pM[:, 272:272 + 6 * E1], small_in[:, :], ident[0:6 * E1, 0:6 * E1])
            last.then_inc(sm["s_wtr"], 1)
            turn_first(2)
            turn_first(3)
            pe.wait_ge(sm["s_wt"], 6)
            nc.tensor.matmul(pH[:, 0:P], w_in[:, 2, :], w_T[:, 3, :], start=True, stop=True)
            nc.tensor.matmul(pH[:, P:2 * P], bvT[:, :], w_T[:, 3, :], start=True, stop=True).then_inc(sm["s_vo0"], 1)
            for c in range(NC):
                pe.wait_ge(sm["s_xt"], c + 1)
                h = c // 2
                last = nc.tensor.matmul(pS[64 * h:64 * h + 64, 0, (c % 2) * 512:(c % 2) * 512 + 512], wr_T[:, :],
                                        xnT[:, c * 512:c * 512 + 512], start=True, stop=True)
            last.then_inc(sm["s_lg"], 1)
            dst = [pS[:, 1, 0:512], pS[:, 1, 512:1024], pM[:, :], pH[:, :]]
            pe.wait_ge(sm["s_vo0e"], 2)
            n = 0
            for c in range(NC):
                for j in range(3):
                    if n >= 4:
                        cc, jj = (n - 4) // 3, (n - 4) % 3
                        if jj < 2:
                            pe.wait_ge(sm["s_pje_a"], 2 * cc + jj + 1)
                        else:
                            pe.wait_ge(sm["s_pje_v"], cc + 1)
                    if j < 2:
                        last = nc.tensor.matmul(dst[n % 4], w_T[:, j, :], xnT[:, c * 512:c * 512 + 512], start=True, stop=True)
                    else:
                        for t in range(4):
                            last = nc.tensor.matmul(dst[n % 4][:, t * P:t * P + P],
                                                    xnT[:, c * 512 + t * P:c * 512 + t * P + P], w_vo,
                                                    start=True, stop=True)
                    last.then_inc(sm["s_pj"], 1)
                    n += 1

            def scores(i):
                b = i // BT
                if i == 0:
                    pe.wait_ge(sm["s_lgc"], 1)
                    pe.wait_ge(sm["s_pje_a"], 2 * NC)
                    pe.wait_ge(sm["s_pje_v"], NC)
                if i >= 2:
                    pe.wait_ge(sm["s_exp"], i - 1)
                for h in range(2):
                    last = nc.tensor.matmul(pS[:, i % 2, h * 512:h * 512 + 512], qT[:, i * P:i * P + P],
                                            kT[:, b * S + h * 512:b * S + h * 512 + 512], start=True, stop=True)
                last.then_inc(sm["s_S"], 1)

            def turn(i):
                pe.wait_ge(sm["s_exp"], i + 1)
                for h in range(2):
                    if i:
                        pe.wait_ge(sm["s_ev"], 2 * (i - 1) + h + 1)
                    for j in range(4):
                        last = nc.tensor.transpose(pT[:, h, j * P:j * P + P],
                                                   probs[:, i % 2, (4 * h + j) * P:(4 * h + j + 1) * P], ident[:, :])
                    last.then_inc(sm["s_tr"], 1)

            def values(i):
                b = i // BT
                pe.wait_ge(sm["s_ev"], 2 * i + 2)
                if i >= 2:
                    pe.wait_ge(sm["s_fin"], i - 1)
                if i == SLOT_STEP:
                    pe.wait_ge(sm["s_cc"], 4)
                for j in range(BT):
                    last = nc.tensor.matmul((pM, pH)[i % 2][:, 0:D], probsT[:, i % 2, j * P:j * P + P], v_sb[:, b * BT + j, :],
                                            start=(j == 0), stop=(j == BT - 1))
                last.then_inc(sm["s_pv"], 1)

            def turn_slots():
                pe.wait_ge(sm["s_sl"], 7)
                pe.wait_ge(sm["s_fin"], SLOT_STEP - 1)
                nc.tensor.transpose(pM[:, 256:256 + E0], slots[:, 0:2, :].rearrange("e a c -> e (a c)"), ident[0:E0, 0:E0])
                nc.tensor.transpose(pM[:, 304:304 + E0], slots[:, 2:4, :].rearrange("e a c -> e (a c)"),
                                    ident[0:E0, 0:E0]).then_inc(sm["s_ctr"], 1)

            scores(0)
            for i in range(NT):
                if i + 1 < NT:
                    scores(i + 1)
                if i:
                    values(i - 1)
                if i == SLOT_STEP:
                    turn_slots()
                turn(i)
            values(NT - 1)

            def spread(p):
                pe.wait_ge(s_g[p % 4], 16 * (p // 4 + 1))
                if p >= 2:
                    pe.wait_ge(sm["s_xge"], p - 1)
                nc.tensor.transpose(pT[:, p % 2, 0:P], xg[:, p, :], ident[:, :]).then_inc(sm["s_xgt"], 1)

            def up(p):
                pe.wait_ge(sm["s_xge"], p + 1)
                pe.wait_ge(s_w1[p % RING], 16 * (p // RING + 1))
                if p >= 2:
                    pe.wait_ge(sm["s_hr"], p - 1)
                for e in range(2):
                    last = nc.tensor.matmul(pS[64 * e:64 * e + 64, p % 2, 0:512], xgT[:, p % 2, 64 * e:64 * e + 64],
                                            w1r[:, p % RING, NS * e:NS * e + NS, :], start=True, stop=True)
                last.then_inc(sm["s_h"], 1)

            def turn_h(p):
                pe.wait_ge(sm["s_hr"], p + 1)
                if p >= 2:
                    pe.wait_ge(sm["s_hbias"], p - 1)
                for s in range(NS):
                    last = nc.tensor.transpose(pS[:, p % 2, 512 + P * s:512 + P * s + P], hb[:, p % 2, P * s:P * s + P], ident[:, :])
                last.then_inc(sm["s_ht"], 1)

            def down(p):
                pe.wait_ge(sm["s_gelu"], p + 1)
                if p == 0:
                    pe.wait_ge(sm["s_b2load"], 16)
                    pe.wait_ge(sm["s_w2load"], 64)
                    pe.wait_ge(sm["s_cc"], 4)
                    pe.wait_ge(sm["s_fin"], NT)
                if p >= 2:
                    pe.wait_ge(sm["s_ysc"], p - 1)
                yb = (pM, pH)[p % 2]
                nc.tensor.matmul(yb[:, 0:D], pairind[:, :], b2p[:, p, :], start=True, stop=False,
                                 skip_group_check=True)
                for n in range(2 * NS):
                    e, s = n // NS, n % NS
                    last = nc.tensor.matmul(yb[64 * e:64 * e + 64, KY * s:KY * s + KY],
                                            hg[:, p % 2, 64 * n:64 * n + 64], w2s[:, (2 * p + e) * NS + s, :],
                                            start=False, stop=(n == 2 * NS - 1), skip_group_check=True)
                last.then_inc(sm["s_y"], 1)

            spread(0)
            for p in range(NP):
                up(p)
                if p:
                    turn_h(p - 1)
                if p + 1 < NP:
                    spread(p + 1)
                if p >= 2:
                    down(p - 2)
            turn_h(NP - 1)
            down(NP - 2)
            down(NP - 1)

            pe.wait_ge(sm["s_perm"], 3)
            pe.wait_ge(sm["s_ysc"], NP - 1)
            pe.wait_ge(sm["s_w1load"], 80)
            nc.tensor.transpose(pM[:, 0:2], brow_p[:, :], ident[0:2, 0:2])
            nc.tensor.transpose(pM[:, P:2 * P], brow1[:, 0, :], ident[:, :]).then_inc(sm["s_btr"], 1)
            pe.wait_ge(sm["s_bte"], 2)
            nc.tensor.matmul(pH[:, 0:P], bvT[:, :], wo1[:, :], start=True, stop=True).then_inc(sm["s_btr"], 1)

            def turn_tokens(b):
                for c in (2 * b, 2 * b + 1):
                    pe.wait_ge(sm["s_xn"], NT + 4 * c + 4)
                    if b:
                        pe.wait_ge(sm["s_lae"], 2)
                    for j in range(4):
                        last = nc.tensor.transpose(pT[:, c % 2, j * P:j * P + P], xn[:, 4 * c + j, :], ident[:, :])
                    last.then_inc(sm["s_xtr"], 1)

            def make_q(b):
                for c in (2 * b, 2 * b + 1):
                    pe.wait_ge(sm["s_xt"], NC + c + 1)
                    if b:
                        pe.wait_ge(sm["s_v1e"], c - 1)
                    nc.tensor.matmul(q_bank(c), wqp[:, :],
                                     xnT[:, c * 512:c * 512 + 512], start=True, stop=True).then_inc(sm["s_q1"], 1)
                for c in (2 * b, 2 * b + 1):
                    nc.tensor.matmul(pT[0:2 * LAT, c % 2, :], wkd[:, :],
                                     xnT[:, c * 512:c * 512 + 512], start=True, stop=True).then_inc(sm["s_la"], 1)

            def make_k(b):
                for c in (2 * b, 2 * b + 1):
                    pe.wait_ge(sm["s_lae"], c + 1)
                    nc.tensor.matmul(k_bank(c), wkp[:, :],
                                     latT[:, c * 512:c * 512 + 512], start=True, stop=True).then_inc(sm["s_kk"], 1)

            def make_v(b):
                for c in (2 * b, 2 * b + 1):
                    if c >= 2:
                        pe.wait_ge(sm["s_q1e"], c + 1)
                    for t in range(4):
                        last = nc.tensor.matmul((pM, pH)[c % 2][:, t * P:t * P + P], latT[:, (4 * c + t) * P:(4 * c + t + 1) * P],
                                                wku[:, P:2 * P], start=True, stop=True)
                    last.then_inc(sm["s_vv"], 1)

            def affinities():
                pe.wait_ge(sm["s_kke"], NC)
                for t in range(NT):
                    last = nc.tensor.matmul(pT[:, 1, t * E1:t * E1 + E1], xnT[:, t * P:t * P + P], cenT[:, :],
                                            start=True, stop=True)
                last.then_inc(sm["s_af"], 1)

            turn_tokens(0)
            make_q(0)
            make_k(0)
            turn_tokens(1)
            pe.wait_ge(sm["s_bte"], 3)
            make_v(0)
            make_q(1)

            def count_earlier():
                pe.wait_ge(sm["s_oh"], 2)
                pe.wait_ge(sm["s_kke"], NC)
                pe.wait_ge(sm["s_k1"], 10)
                oh = onehotb[:, :, :].rearrange("p t e -> p (t e)")
                nc.tensor.matmul(pT[:, 0, 0:NT * E1], before[:, :], oh, start=True, stop=True)
                nc.tensor.matmul(pT[:, 0, NT * E1:2 * NT * E1], onesb[:, :], oh, start=True, stop=True).then_inc(sm["s_rk"], 1)

            def unit(u):
                g = u // NU
                j, heads, qt = UNITS[u % NU]
                if u % NU == 0:
                    stack_ready(pe, g)
                if u == 0:
                    pe.wait_ge(sm["s_q1e"], 2)
                    pe.wait_ge(sm["s_kke"], 2)
                if u >= 2:
                    pe.wait_ge(sm["s_um"], u - 1)
                keys = (qt + 1) * P
                if heads == 2:
                    spans = [(j, 0, 0, keys), (j + 1, 512, 0, keys)]
                else:
                    spans = [(j, 0, 0, 512), (j, 512, 512, keys - 512)]
                for h, at, k0, w in spans:
                    diag = heads == 2 or k0
                    last = nc.tensor.matmul(pS[:, u % 2, at:at + w], stack(0, g)[0:KQ, h, qt * P:qt * P + P],
                                            stack(1, g)[0:KQ, h, k0:k0 + w], start=True, stop=not diag)
                    if diag:
                        last = nc.tensor.matmul(pS[:, u % 2, at + w - P:at + w], identb[:, :], causal[:, :],
                                                start=False, stop=True)
                last.then_inc(sm["s_u"], 1)

            def turn_m(g):
                pe.wait_ge(sm["s_msp"], 5 * g + 5)
                nc.tensor.transpose(pH[:, :].bitcast(bf16)[0:3 * GH * BT, 0:P],
                                    mparts[:, :, :, :].rearrange("p a j t -> p (a j t)"), identb[:, :]).then_inc(sm["s_mt"], 1)

            def score(n, j):
                e = GH * n + j
                g = n // NSTEP
                qc, kt, q0, cols = STEPS[n % NSTEP]
                if n % NSTEP == 0 and j == 0:
                    pe.wait_ge(sm["s_mrow"], 16 * (g + 1))
                if n == SPREAD0:
                    pe.wait_ge(sm["s_um"], NG * NU)
                elif n > SPREAD0:
                    pe.wait_ge(sm["s_e1"], e - GH + 1)
                elif e >= 2:
                    pe.wait_ge(sm["s_e1"], e - 1)
                bank = pS[:, j // 2, 512 * (j % 2):512 * (j % 2) + cols] if n >= SPREAD0 else pT[:, j % 2, 0:cols]
                nc.tensor.matmul(bank, stack(1, g)[0:KM, j, kt * P:kt * P + P],
                                 stack(0, g)[0:KM, j, q0:q0 + cols], start=True, stop=True).then_inc(sm["s_s1"], 1)

            def weigh(n):
                g = n // NSTEP
                qc, kt, q0, cols = STEPS[n % NSTEP]
                pe.wait_ge(sm["s_e1"], GH * n + GH)
                if q0 == kt * P:
                    pe.wait_ge(sm["s_sel"], sel_count(n))
                if n % NSTEP == 0:
                    pe.wait_ge(sm["s_ve_b"], g + 1)
                if kt == 0 and n:
                    pe.wait_ge(sm["s_nrm"], 2 * g + qc)
                for j in range(GH):
                    last = nc.tensor.matmul(pM[32 * j:32 * j + 32, q0 - qc * 512:q0 - qc * 512 + cols],
                                            v_ext[:, g % 2, kt, j, :], pr1[:, n % 2, j, 0:cols],
                                            start=(kt == 0), stop=(kt == 4 * qc + 3))
                last.then_inc(sm["s_pv1"], 1)

            def turn_acc(r):
                pe.wait_ge(sm["s_ace"], r + 1)
                for t in range(4):
                    last = nc.tensor.transpose(pM[:, t * P:t * P + P], acc_sb[:, r % 2, t * P:t * P + P], ident[:, :])
                last.then_inc(sm["s_tr1"], 1)

            def ffn(j, sub):
                if sub == 0:
                    pe.wait_ge(s_xsl[j % 4], 16 * (j // 4 + 1))
                    if j:
                        pe.wait_ge(sm["s_fce"], j)
                    nc.tensor.transpose(pH[:, 0:P], xs_in[:, j % 4, :], ident[:, :]).then_inc(sm["s_fa"], 1)
                elif sub == 1:
                    pe.wait_ge(sm["s_fae"], j + 1)
                    for c in range(FC):
                        last = nc.tensor.matmul(pH[:, c * P:c * P + P], w_tile[:, j % 2, c * P:c * P + P], xlT[:, :],
                                                start=True, stop=True)
                    last.then_inc(sm["s_fb"], 1)
                else:
                    pe.wait_ge(sm["s_relu"], j + 1)
                    for c in range(FC):
                        last = nc.tensor.matmul(pH[:, 0:D], hs[:, j % 2, c * P:c * P + P],
                                                w_tile[:, j % 2, F1 + c * D:F1 + c * D + D],
                                                start=(c == 0), stop=(c == FC - 1))
                    last.then_inc(sm["s_fc"], 1)

            def turn_heads(c):
                pe.wait_ge(sm["s_nrm"], NG * (c // 2 + 1) - 1 + c % 2)
                if c:
                    pe.wait_ge(sm["s_fin1"], c)
                else:
                    pe.wait_ge(sm["s_fce"], NSORT)
                    pe.wait_ge(sm["s_mte"], NG)
                for t in range(4):
                    last = nc.tensor.transpose(pH[:, t * P:t * P + P], o_sb[:, 4 * c + t, :], ident[:, :])
                last.then_inc(sm["s_ot"], 1)

            def project1(c):
                pe.wait_ge(sm["s_ote"], c + 1)
                for t in range(4):
                    last = nc.tensor.matmul(pH[:, t * P:t * P + P], hs[:, c % 2, t * P:t * P + P], wo1[:, :],
                                            start=True, stop=True)
                last.then_inc(sm["s_pj1"], 1)

            for u in range(NU):
                unit(u)
                if u == 1:
                    make_k(1)
                    make_v(1)
                if u == 3:
                    affinities()
                if u == 9:
                    count_earlier()
            turn_m(0)
            for u in range(NU, units_before(0)):
                unit(u)
            pe.wait_ge(sm["s_rkc"], 1)
            for n in range(NG * NSTEP + 2):
                last_step = n >= NG * NSTEP
                units = range(units_before(n), units_before(n + 1))
                if not last_step:
                    score(n, 0)
                for u in units[:1]:
                    unit(u)
                if not last_step:
                    score(n, 1)
                if n >= 2 and ends(n - 2) >= 0:
                    turn_acc(ends(n - 2))
                for u in units[1:]:
                    unit(u)
                if not last_step:
                    score(n, 2)
                if (n + 4) % NSTEP == 0 and (n + 4) // NSTEP < NG:
                    if ffn_count(n):
                        wait_ffn(pe, ffn_count(n))
                    turn_m((n + 4) // NSTEP)
                if not last_step:
                    score(n, 3)
                if 1 <= n <= NG * NSTEP:
                    weigh(n - 1)
                j, sub = ffn_part(n)
                if sub >= 0:
                    pe.wait_ge(sm["s_mte"], min(NG, 1 + (n + 4) // NSTEP))
                    ffn(j, sub)
                for c, first in enumerate(OUTS):
                    if n == first:
                        turn_heads(c)
                    if n == first + 1:
                        project1(c)

            turn_heads(NC - 1)
            project1(NC - 1)

        @block.vector
        def _(dve):
            def ln_var(turn_, tiles, first=None):
                n1 = tiles[-1] + 1
                for t in tiles:
                    dve.wait_ge(sm["s_st"], turn_ * NT + t + 1)
                    nc.vector.bn_aggr(mv[:, t, :], stats[:, t, :]).then_inc(sm["s_mv"], 1)
                if first is not None:
                    dve.wait_ge(sm["s_mv"], turn_ * NT + n1)
                    nc.vector.tensor_scalar(var_e[:, first:n1], mv[:, first:n1, 1], EPS, None, ALU.add).then_inc(sm["s_ve"], 1)

            def ln_rstd(k, n0, n1):
                rs_, ve_, nw_ = rstd[:, n0:n1], var_e[:, n0:n1], newt[:, n0:n1]
                dve.wait_ge(sm["s_sd"], k + 1)
                nc.vector.reciprocal(rs_, sdev[:, n0:n1]).then_inc(sm["s_rstd"], 1)
                dve.wait_ge(sm["s_rstd"], 5 * k + 1)
                nc.vector.tensor_tensor(nw_, rs_, rs_, ALU.mult).then_inc(sm["s_rstd"], 1)
                dve.wait_ge(sm["s_rstd"], 5 * k + 2)
                nc.vector.tensor_tensor(nw_, nw_, ve_, ALU.mult).then_inc(sm["s_rstd"], 1)
                dve.wait_ge(sm["s_rstd"], 5 * k + 3)
                nc.vector.tensor_scalar(nw_, nw_, -0.5, 1.5, ALU.mult, ALU.add).then_inc(sm["s_rstd"], 1)
                dve.wait_ge(sm["s_rstd"], 5 * k + 4)
                nc.vector.tensor_tensor(rs_, rs_, nw_, ALU.mult).then_inc(sm["s_rstd"], 1)
                dve.wait_ge(sm["s_rstd"], 5 * k + 5)

            def ln_apply(tiles, src, dst):
                for t in tiles:
                    nc.vector.tensor_scalar(dst[:, t, :], src[:, t, :], mv[:, t, 0:1], rstd[:, t:t + 1],
                                            ALU.subtract, ALU.mult).then_inc(sm["s_xn"], 1)

            def route_a(dve):
                dve.wait_ge(sm["s_rt"], 1)
                nc.vector.tensor_reduce(amax[:, :], aff[:, :, :], AX.X, ALU.max).then_inc(sm["s_rt"], 1)
                dve.wait_ge(sm["s_rt"], 2)
                wide = amax[:, :].unsqueeze(2).to_broadcast([P, NT, E1])
                nc.vector.tensor_tensor(cand[:, :, :], aff[:, :, :], wide, ALU.is_equal).then_inc(sm["s_rt"], 1)
                dve.wait_ge(sm["s_rt"], 3)
                dve.wait_ge(sm["s_k1"], 10)
                em = em8[:, :].unsqueeze(1).to_broadcast([P, NT, E1])
                nc.vector.tensor_tensor(cand[:, :, :], cand[:, :, :], em, ALU.mult).then_inc(sm["s_rt"], 1)
                dve.wait_ge(sm["s_rt"], 4)
                nc.vector.tensor_reduce(emin[:, :], cand[:, :, :], AX.X, ALU.min).then_inc(sm["s_rt"], 1)
                dve.wait_ge(sm["s_rt"], 5)
                em_w = emin[:, :].unsqueeze(2).to_broadcast([P, NT, E1])
                nc.vector.tensor_tensor(onehot[:, :, :], em, em_w, ALU.is_equal).then_inc(sm["s_oh"], 1)
                nc.vector.tensor_tensor(onehotb[:, :, :], em, em_w, ALU.is_equal).then_inc(sm["s_oh"], 1)
                nc.vector.tensor_copy(smallW[:, :, 0:FC], smallT[:, 0:FC * E1].rearrange("p (e c) -> p e c", c=FC)).then_inc(sm["s_smw"], 1)
                nc.vector.tensor_copy(smallW[:, :, FC], smallT[:, FC * E1:(FC + 1) * E1]).then_inc(sm["s_smw"], 1)
                nc.vector.tensor_copy(smallW[:, :, FC + 1], smallT[:, (FC + 1) * E1:(FC + 2) * E1]).then_inc(sm["s_smw"], 1)

            def sum_counts(k):
                if k:
                    dve.wait_ge(sm["s_rt"], 5 + 2 * k)
                else:
                    dve.wait_ge(sm["s_rkc"], 1)
                src = cum[:, (k - 1) % 2, :, :] if k else rank[:, 1, :, :]
                sh, dst = 1 << k, cum[:, k % 2, :, :]
                nc.vector.tensor_copy(dst[:, 0:sh, :], src[:, 0:sh, :]).then_inc(sm["s_rt"], 1)
                nc.vector.tensor_tensor(dst[:, sh:NT, :], src[:, sh:NT, :], src[:, 0:NT - sh, :], ALU.add).then_inc(sm["s_rt"], 1)

            def compare_counts():
                dve.wait_ge(sm["s_rt"], 13)
                count = cum[:, 1, NT - 1, :].unsqueeze(2).to_broadcast([P, E1, NT])
                nc.vector.tensor_tensor(full[:, :, :], count, m128[:, :].unsqueeze(1).to_broadcast([P, E1, NT]),
                                        ALU.is_gt).then_inc(sm["s_rt"], 1)

            def count_tiles():
                dve.wait_ge(sm["s_rt"], 14)
                nc.vector.tensor_reduce(ctile[:, 0, :], full[:, :, :], AX.X, ALU.add).then_inc(sm["s_rt"], 1)

            def sum_tiles(k):
                dve.wait_ge(sm["s_rt"], 15 + 2 * k)
                sh, src, dst = 1 << k, (0, 1, 2)[k], (1, 2, 1)[k]
                nc.vector.tensor_copy(ctile[:, dst, 0:sh], ctile[:, src, 0:sh]).then_inc(sm["s_rt"], 1)
                nc.vector.tensor_tensor(ctile[:, dst, sh:E1], ctile[:, src, sh:E1], ctile[:, src, 0:E1 - sh],
                                        ALU.add).then_inc(sm["s_rt"], 1)

            def place(k):
                if k == 0:
                    dve.wait_ge(sm["s_rt"], 21)
                    nc.vector.tensor_tensor(ctile[:, 3, :], ctile[:, 1, :], ctile[:, 0, :], ALU.subtract).then_inc(sm["s_rt"], 1)
                    nc.vector.tensor_tensor(cand[:, :, :], cum[:, 1, :, :], rank[:, 1, :, :], ALU.subtract).then_inc(sm["s_rt"], 1)
                    nc.vector.tensor_tensor(tile_c[:, :, :], ctile[:, 1, :].unsqueeze(1).to_broadcast([P, NSORT, E1]),
                                            iota_j[:, :].unsqueeze(2).to_broadcast([P, NSORT, E1]), ALU.is_le).then_inc(sm["s_te"], 1)
                if k == 1:
                    dve.wait_ge(sm["s_rt"], 23)
                    base = ctile[:, 3, :].unsqueeze(1).to_broadcast([P, NT, E1])
                    nc.vector.scalar_tensor_tensor(cand[:, :, :], base, float(P), cand[:, :, :], ALU.mult, ALU.add).then_inc(sm["s_rt"], 1)
                    dve.wait_ge(sm["s_te"], 1)
                    nc.vector.tensor_reduce(tile_f[:, :], tile_c[:, :, :], AX.X, ALU.add).then_inc(sm["s_te"], 1)
                if k == 2:
                    dve.wait_ge(sm["s_te"], 2)
                    nc.vector.tensor_scalar(tile_e[:, :], tile_f[:, :], float(E1 - 1), None, ALU.min).then_inc(sm["s_te"], 1)
                    dve.wait_ge(sm["s_rt"], 24)
                    nc.vector.tensor_tensor(cand[:, :, :], cand[:, :, :], rank[:, 0, :, :], ALU.add).then_inc(sm["s_te"], 1)
                if k == 3:
                    dve.wait_ge(sm["s_te"], 4)
                    nc.vector.tensor_tensor(cand[:, :, :], cand[:, :, :], onehot[:, :, :], ALU.mult).then_inc(sm["s_te"], 1)
                if k == 4:
                    dve.wait_ge(sm["s_te"], 5)
                    nc.vector.tensor_reduce(pos_f[:, :], cand[:, :, :], AX.X, ALU.add).then_inc(sm["s_te"], 1)
                if k == 5:
                    dve.wait_ge(sm["s_te"], 6)
                    nc.vector.tensor_copy(pos[:, :], pos_f[:, :]).then_inc(sm["s_te"], 1)

            nc.vector.memset(half_off[0:64, :], 0.0).then_inc(sm["s_ones"], 1)
            nc.vector.memset(half_off[64:P, :], float(S)).then_inc(sm["s_ones"], 1)
            so = s_off[:, :].rearrange("p (n two) -> p n two", two=2)
            for h in range(2):
                for c in range(2):
                    nc.vector.memset(so[64 * h:64 * h + 64, :, c], float(T * (2 * c + h))).then_inc(sm["s_ones"], 1)
            for h in range(2):
                for c in (2 * h, 2 * h + 1):
                    dve.wait_ge(s_x[c], 16)
                    for t in range(4 * c, 4 * c + 4):
                        nc.vector.bn_stats(stats[:, t, :], x_sb[:, t, :]).then_inc(sm["s_st"], 1)
                ln_var(0, range(BT * h, BT * h + BT), BT * h)
            for h in range(2):
                ln_rstd(h, BT * h, BT * h + BT)
                ln_apply(range(BT * h, BT * h + BT), x_sb, xn)
            dve.wait_ge(sm["s_vo0"], 1)
            nc.vector.tensor_copy(w_vo, pH[:, 0:P]).then_inc(sm["s_vo0e"], 1)
            nc.vector.tensor_tensor(bvo[:, 0, :], pH[:, P:2 * P], bvo[:, 1, :], ALU.add).then_inc(sm["s_vo0e"], 1)
            dve.wait_ge(sm["s_bload"], 64)
            dve.wait_ge(sm["s_lg"], 1)
            nc.vector.tensor_copy(logits[:, :], pS[:, 0, :]).then_inc(sm["s_lgc"], 1)
            dst = [pS[:, 1, 0:512], pS[:, 1, 512:1024], pM[:, :], pH[:, :]]
            for c in range(NC):
                dve.wait_ge(sm["s_pj"], 3 * c + 3)
                nc.vector.tensor_copy(v_sb[:, 4 * c:4 * c + 4, :],
                                      dst[(3 * c + 2) % 4].rearrange("p (t d) -> p t d", d=D)).then_inc(sm["s_pje_v"], 1)

            dve.wait_ge(sm["s_w1load"], 80)
            dve.wait_ge(sm["s_b1load1"], 80)
            for dst_, src_ in ((brow_p, brow_qk[:, :]), (wqp, wq1[:, :]), (wkp, wku[:, 0:P])):
                nc.vector.tensor_copy(dst_[:, :].rearrange("p (g d j) -> p g d j", d=DH, j=GH),
                                      src_.rearrange("p (g j d) -> p g d j", d=DH, j=GH)).then_inc(sm["s_perm"], 1)

            def finish(i):
                dve.wait_ge(sm["s_exp"], i + 1)
                nc.vector.reciprocal(rinv[:, i:i + 1], rsum[:, i:i + 1]).then_inc(sm["s_ri"], 1)
                dve.wait_ge(sm["s_pv"], i + 1)
                if i == 0:
                    dve.wait_ge(sm["s_accz"], 16 * NACC)
                    dve.wait_ge(sm["s_xs0"], 32)
                dve.wait_ge(sm["s_ri"], i + 1)
                nc.vector.scalar_tensor_tensor(s_sb[:, i, :], (pM, pH)[i % 2][:, 0:D], rinv[:, i:i + 1], bvo[:, 0, :],
                                               ALU.mult, ALU.add).then_inc(sm["s_fin"], 1)

            def rowmax(i):
                dve.wait_ge(sm["s_S"], i + 1)
                nc.vector.tensor_reduce(nmax[:, i:i + 1], pS[:, i % 2, :], AX.X, ALU.max, negate=True).then_inc(sm["s_max"], 1)
                dve.wait_ge(sm["s_max"], i + 1)
                nc.vector.tensor_scalar(nbias[:, i:i + 1], nmax[:, i:i + 1], SC0, None, ALU.mult).then_inc(sm["s_nm"], 1)

            def top_round(r):
                if r == 0:
                    dve.wait_ge(sm["s_lgc"], 1)
                else:
                    dve.wait_ge(sm["s_t3"], r)
                r8 = slice(8 * r, 8 * r + 8)
                nc.vector.max(top_v[:, r8], logits[:, :]).then_inc(sm["s_t1"], 1)
                dve.wait_ge(sm["s_t1"], r + 1)
                nc.vector.max_index(top_i[:, r8], top_v[:, r8], logits[:, :]).then_inc(sm["s_t2"], 1)
                nc.vector.match_replace(logits[:, :], top_v[:, r8], logits[:, :], -3.0e38).then_inc(sm["s_t3"], 1)

            def merge():
                dve.wait_ge(sm["s_t2"], CAP // 8)
                dve.wait_ge(sm["s_ones"], 6)
                nc.vector.tensor_scalar(top_f[:, :], top_i[:, :], half_off[:, 0:1], None, ALU.add).then_inc(sm["s_tf"], 1)
                dve.wait_ge(sm["s_tf"], 1)
                dve.wait_ge(sm["s_hb"], 32)
                lo, hi = top_v[0:E0, :], hi_v[:, ::-1]
                lo_i, hi_i = top_f[0:E0, :], hi_f[:, ::-1]
                nc.vector.tensor_tensor(slot_v[:, :], lo, hi, ALU.max).then_inc(sm["s_sl"], 1)
                nc.vector.tensor_tensor(slot_m[:, :], lo, hi, ALU.is_ge).then_inc(sm["s_sl"], 1)
                nc.vector.tensor_tensor(slot_d[:, :], lo_i, hi_i, ALU.subtract).then_inc(sm["s_sl"], 1)
                dve.wait_ge(sm["s_sl"], 3)
                nc.vector.tensor_reduce(slot_s[:, 0:1], slot_v[:, :], AX.X, ALU.max, negate=True).then_inc(sm["s_wn"], 1)
                nc.vector.tensor_tensor(slot_d[:, :], slot_d[:, :], slot_m[:, :], ALU.mult).then_inc(sm["s_sl"], 1)
                dve.wait_ge(sm["s_sl"], 4)
                for j in range(2):
                    nc.vector.tensor_tensor(slots[:, 2 + j, :], slot_d[:, :], hi_i, ALU.add).then_inc(sm["s_sl"], 1)

            def weights():
                dve.wait_ge(sm["s_we"], 1)
                nc.vector.reciprocal(slot_s[:, 2:3], slot_s[:, 1:2]).then_inc(sm["s_wn"], 1)
                dve.wait_ge(sm["s_wn"], 2)
                nc.vector.tensor_scalar(slots[:, 0:2, :], slot_m[:, :].unsqueeze(1).to_broadcast([E0, 2, CAP]),
                                        slot_s[:, 2:3], None, ALU.mult).then_inc(sm["s_sl"], 1)

            def columns():
                dve.wait_ge(sm["s_ctr"], 1)
                for h in range(2):
                    part = slice(64 * h, 64 * h + 64)
                    for k, dst_ in ((0, w_col), (1, i_col)):
                        src = pM[part, 256 + E0 * k:256 + E0 * k + E0].rearrange("p (n two) -> p n two", two=2)
                        nc.vector.tensor_copy(dst_[part, :], src[:, :, h]).then_inc(sm["s_cc"], 1)
                dve.wait_ge(sm["s_cc"], 4)
                nc.vector.tensor_copy(g_idx[:, :], i_col[:, :]).then_inc(sm["s_so"], 1)
                nc.vector.tensor_tensor(s_idx[:, :], i_col[:, :], s_off[:, :], ALU.add).then_inc(sm["s_so"], 1)

            for i in range(NT):
                rowmax(i)
                if i >= 2:
                    finish(i - 2)
                if i < CAP // 8:
                    top_round(i)
                if i == CAP // 8:
                    merge()
                if i == CAP // 8 + 2:
                    weights()
                if i == SLOT_STEP:
                    columns()
            finish(NT - 2)
            finish(NT - 1)

            def lift(p):
                dve.wait_ge(sm["s_xgt"], p + 1)
                if p >= 2:
                    dve.wait_ge(sm["s_h"], p - 1)
                nc.vector.tensor_copy(xgT[:, p % 2, :], pT[:, p % 2, 0:P]).then_inc(sm["s_xge"], 1)

            def scale_y(p):
                dve.wait_ge(sm["s_y"], p + 1)
                if p >= 4:
                    dve.wait_ge(s_sc[p % 2], 16 * (p // 2 - 1))
                nc.vector.tensor_scalar(y_sb[:, p % 4, :], (pM, pH)[p % 2][:, 0:D], w_col[:, p:p + 1], None,
                                        ALU.mult).then_inc(sm["s_ysc"], 1)

            lift(0)
            def bias_h(p):
                dve.wait_ge(sm["s_ht"], p + 1)
                if p >= 2:
                    dve.wait_ge(sm["s_y"], p - 1)
                nc.vector.tensor_tensor(hg[:, p % 2, :].rearrange("p (e s c) -> p e s c", e=2, s=NS),
                                        pS[:, p % 2, 512:1024].rearrange("p (s e c) -> p e s c", s=NS, e=2),
                                        b1T[:, 2 * NS * p:2 * NS * (p + 1)].rearrange("p (e s) -> p e s", e=2)
                                        .unsqueeze(3).to_broadcast([P, 2, NS, 64]), ALU.add).then_inc(sm["s_hbias"], 1)

            for p in range(NP):
                if p:
                    bias_h(p - 1)
                if p + 1 < NP:
                    lift(p + 1)
                if p >= 2:
                    scale_y(p - 2)
            bias_h(NP - 1)
            scale_y(NP - 2)
            scale_y(NP - 1)
            dve.wait_ge(sm["s_xrows"], 64)

            def sum_results():
                for c in (0, 1):
                    t4 = slice(4 * c, 4 * c + 4)
                    dve.wait_ge(s_x[c], 16 + 16 * NACC)
                    nc.vector.tensor_tensor(accs[:, 0:2, t4, :], accs[:, 0:2, t4, :], accs[:, 2:4, t4, :], ALU.add).then_inc(sm["s_sum"], 1)
                    dve.wait_ge(sm["s_sum"], 2 * c + 1)
                    nc.vector.tensor_tensor(accs[:, 0, t4, :], accs[:, 0, t4, :], accs[:, 1, t4, :], ALU.add).then_inc(sm["s_sum"], 1)

            def join_layers(c):
                t4 = slice(4 * c, 4 * c + 4)
                dve.wait_ge(sm["s_silu"], c + 1)
                nc.vector.tensor_tensor(s_sb[:, t4, :], s_sb[:, t4, :], accs[:, 1, t4, :], ALU.mult).then_inc(sm["s_x1"], 1)
                dve.wait_ge(sm["s_x1"], 2 * c + 1)
                nc.vector.tensor_tensor(x_sb[:, t4, :], x_sb[:, t4, :], s_sb[:, t4, :], ALU.add).then_inc(sm["s_x1"], 1)
                dve.wait_ge(sm["s_x1"], 2 * c + 2)
                for t in range(4 * c, 4 * c + 4):
                    nc.vector.bn_stats(stats[:, t, :], x_sb[:, t, :]).then_inc(sm["s_st"], 1)

            def experts_stats(b):
                for t in range(b * BT, b * BT + BT):
                    dve.wait_ge(sm["s_xn"], NT + t + 1)
                    nc.vector.bn_stats(stats[:, t, :], xn[:, t, :]).then_inc(sm["s_st"], 1)
                ln_var(2, range(b * BT, b * BT + BT), 0 if b == B - 1 else None)

            def take_part(b, side, st):
                bs = slice(b * S, b * S + S)
                dve.wait_ge(sm["s_cp"], part_count(b, side, st))
                rest = qk_mem[:, side, bs]
                nc.vector.tensor_tensor(parts[side][:, 2, bs] if st else rest, rest, parts[side][:, st, bs],
                                        ALU.subtract).then_inc(sm["s_sub"], 1)

            sum_results()
            join_layers(0)
            join_layers(1)
            ln_var(1, range(0, BT), 0)
            ln_rstd(2, 0, BT)
            ln_apply(range(BT), x_sb, xn)
            dve.wait_ge(sm["s_btr"], 2)
            nc.vector.tensor_tensor(brow1[:, 1, :], brow1[:, 1, :], pH[:, 0:P], ALU.add).then_inc(sm["s_bte"], 1)
            join_layers(2)
            take_part(0, 0, 0)
            join_layers(3)
            ln_var(1, range(BT, NT), BT)
            take_part(0, 1, 0)
            ln_rstd(3, BT, NT)
            take_part(0, 0, 1)
            take_part(0, 1, 1)
            ln_apply(range(BT, NT), x_sb, xn)
            experts_stats(0)
            experts_stats(1)

            def unit(u):
                g = u // NU
                j, heads, qt = UNITS[u % NU]
                dve.wait_ge(sm["s_u"], u + 1)
                if u % NU == 0 and g:
                    dve.wait_ge(sm["s_msp"], 5 * g)
                keys = (qt + 1) * P
                if heads == 2:
                    nc.vector.tensor_reduce(negm[:, j:j + 2, qt],
                                            pS[:, u % 2, :].rearrange("p (a k) -> p a k", a=2)[:, :, 0:keys],
                                            AX.X, ALU.max, negate=True).then_inc(sm["s_um"], 1)
                else:
                    nc.vector.tensor_reduce(negm[:, j, qt:qt + 1], pS[:, u % 2, 0:keys],
                                            AX.X, ALU.max, negate=True).then_inc(sm["s_um"], 1)
                if u % NU == NU - 1:
                    split_m(g)

            def split_m(g):
                dve.wait_ge(sm["s_um"], NU * (g + 1))
                if g:
                    dve.wait_ge(sm["s_mt"], g)
                nc.vector.tensor_copy(mparts[:, 0, :, :], negm[:, :, :]).then_inc(sm["s_msp"], 1)
                dve.wait_ge(sm["s_msp"], 5 * g + 1)
                nc.vector.tensor_tensor(negr[:, :, :], negm[:, :, :], mparts[:, 0, :, :], ALU.subtract).then_inc(sm["s_msp"], 1)
                dve.wait_ge(sm["s_msp"], 5 * g + 2)
                nc.vector.tensor_copy(mparts[:, 1, :, :], negr[:, :, :]).then_inc(sm["s_msp"], 1)
                dve.wait_ge(sm["s_msp"], 5 * g + 3)
                nc.vector.tensor_tensor(negr[:, :, :], negr[:, :, :], mparts[:, 1, :, :], ALU.subtract).then_inc(sm["s_msp"], 1)
                dve.wait_ge(sm["s_msp"], 5 * g + 4)
                nc.vector.tensor_copy(mparts[:, 2, :, :], negr[:, :, :]).then_inc(sm["s_msp"], 1)

            def rows_m(g):
                dve.wait_ge(sm["s_mt"], g + 1)
                if g:
                    dve.wait_ge(sm["s_mscr"], 16 * g)
                nc.vector.tensor_copy(mrows[:, :], pH[:, :].bitcast(bf16)[0:3 * GH * BT, 0:P]).then_inc(sm["s_mte"], 1)

            def fetch_w(j):
                if j >= 2:
                    dve.wait_ge(sm["s_fc"], j - 1)
                    dve.wait_ge(sm["s_fae"], j - 1)
                    dve.wait_ge(sm["s_fbe"], j - 1)
                    dve.wait_ge(sm["s_fce"], j - 1)
                if j == 0:
                    dve.wait_ge(sm["s_te"], 3)
                    dve.wait_ge(sm["s_pos"], 16 * NT)
                    dve.wait_ge(sm["s_wall"], 16 * (2 + E1))
                    dve.wait_ge(sm["s_smw"], 3)
                e = dve.value_load(tile_e[0:1, j:j + 1], min_val=0, max_val=E1 - 1)
                nc.vector.tensor_copy(w_tile[:, j % 2, :], wall[:, bass.ds(e, 1), 0:2 * F1].rearrange("p a n -> p (a n)")).then_inc(sm["s_wj"], 1)
                nc.vector.tensor_copy(b2_tile[:, j % 2, :], wall[:, bass.ds(e, 1), 2 * F1:2 * F1 + D].rearrange("p a n -> p (a n)")).then_inc(sm["s_wj"], 1)
                nc.vector.tensor_copy(s_tile[:, j % 2, :], smallW[:, bass.ds(e, 1), :].rearrange("p a n -> p (a n)")).then_inc(sm["s_wj"], 1)

            def add_bias(c):
                dve.wait_ge(sm["s_pj1"], c + 1)
                if c == 0:
                    dve.wait_ge(sm["s_fc"], NSORT)
                nc.vector.tensor_tensor(s_fin[:, 4 * c:4 * c + 4, :], pH[:, :].rearrange("p (t d) -> p t d", d=D),
                                        brow1[:, 1:2, :].to_broadcast([P, 4, D]), ALU.add).then_inc(sm["s_fin1"], 1)

            def weigh_experts(c):
                if c == 0:
                    dve.wait_ge(sm["s_al"], 1)
                    nc.vector.tensor_scalar(alpha[:, 1, :], alpha[:, 0, :], 1.0, None, ALU.add).then_inc(sm["s_als"], 1)
                    dve.wait_ge(sm["s_als"], 1)
                    nc.vector.reciprocal(alpha[:, 2, :], alpha[:, 1, :]).then_inc(sm["s_als"], 1)
                    dve.wait_ge(sm["s_als"], 2)
                dve.wait_ge(s_g[c], 16 * (NP // 4) + 64)
                for t in range(4 * c, 4 * c + 4):
                    nc.vector.scalar_tensor_tensor(f_sb[:, t, :], f_sb[:, t, :], alpha[:, 2, t:t + 1], xn[:, t, :],
                                                   ALU.mult, ALU.add).then_inc(sm["s_als"], 1)

            def normalise(r):
                g, qc = r // 2, r % 2
                b, g4 = g // (NG // B), g % (NG // B)
                dve.wait_ge(sm["s_tr1"], r + 1)
                acc = pM[:, :].rearrange("p (t j c) -> p t j c", t=4, j=GH)
                nc.vector.reciprocal(rden[:, :, :], acc[:, :, :, DH]).then_inc(sm["s_rd1"], 1)
                dve.wait_ge(sm["s_rd1"], r + 1)
                t0 = b * BT + 4 * qc
                o = o_sb[:, t0:t0 + 4, g4 * GH * DH:(g4 + 1) * GH * DH].rearrange("p t (j d) -> p t j d", d=DH)
                nc.vector.tensor_tensor(o, acc[:, :, :, 0:DH], rden[:, :, :].unsqueeze(3).to_broadcast([P, 4, GH, DH]),
                                        ALU.mult).then_inc(sm["s_nrm"], 1)

            for u in range(NU):
                unit(u)
                if u < 4:
                    take_part(1, u % 2, u // 2)
                if u == 7:
                    dve.wait_ge(sm["s_af"], 1)
                    nc.vector.tensor_copy(aff[:, :, :].rearrange("p t e -> p (t e)"), pT[:, 1, 0:NT * E1]).then_inc(sm["s_rt"], 1)
                    route_a(dve)
                if u == 9:
                    ln_rstd(4, 0, NT)
                    nc.vector.scalar_tensor_tensor(nbias[:, :], mv[:, :, 0], -1.0, rstd[:, :], ALU.mult, ALU.mult).then_inc(sm["s_lnb"], 1)
                if u == 10:
                    dve.wait_ge(sm["s_rk"], 1)
                    nc.vector.tensor_copy(rank[:, :, :, :].rearrange("p a t e -> p (a t e)"), pT[:, 0, 0:2 * NT * E1]).then_inc(sm["s_rkc"], 1)
                if 11 <= u < 15:
                    sum_counts(u - 11)
                if u == 15:
                    compare_counts()
                if u == 16:
                    count_tiles()
                if 17 <= u < 20:
                    sum_tiles(u - 17)
                if u >= 20:
                    place(u - 20)
            rows_m(0)
            for u in range(NU, units_before(0)):
                unit(u)
                place(u - 20)
            dve.wait_ge(sm["s_scr"], 16 * 12)
            for n in range(NG * NSTEP + 2):
                j, sub = ffn_part(n - 1)
                if sub == 1:
                    dve.wait_ge(sm["s_fb"], j + 1)
                    if j >= 2:
                        dve.wait_ge(sm["s_fc"], j - 1)
                    nc.vector.tensor_tensor(hs[:, j % 2, :].rearrange("p (c t) -> p c t", c=FC),
                                            pH[:, :].rearrange("p (c t) -> p c t", c=FC),
                                            s_tile[:, j % 2, 0:FC].unsqueeze(2).to_broadcast([P, FC, P]),
                                            ALU.add).then_inc(sm["s_fbe"], 1)
                if sub == 2:
                    dve.wait_ge(sm["s_fc"], j + 1)
                    if j >= 2:
                        dve.wait_ge(s_ysd[j % 2], 16 * (j // 2))
                    nc.vector.tensor_tensor(ys_sb[:, j % 2, :], pH[:, 0:D], b2_tile[:, j % 2, :],
                                            ALU.add).then_inc(sm["s_fce"], 1)
                for c, first in enumerate(OUTS):
                    if n == first + 2:
                        add_bias(c)
                units = range(units_before(n), units_before(n + 1))
                for u in units[:1]:
                    unit(u)
                if n >= 2 and ends(n - 2) >= 0:
                    normalise(ends(n - 2))
                for u in units[1:]:
                    unit(u)
                if (n + 4) % NSTEP == 0 and (n + 4) // NSTEP < NG:
                    rows_m((n + 4) // NSTEP)
                if n == FFN0 - 2:
                    fetch_w(0)
                if n == FFN0 - 1:
                    fetch_w(1)
                j, sub = ffn_part(n)
                if sub == 0 and 1 <= j and j + 1 < NSORT:
                    fetch_w(j + 1)
                for c in range(NC - 1):
                    if n == NG * NSTEP - 6 + 2 * c:
                        weigh_experts(c)
            weigh_experts(NC - 1)

            def combine(c):
                t4 = slice(4 * c, 4 * c + 4)
                dve.wait_ge(sm["s_gate"], c + 1)
                dve.wait_ge(sm["s_fin1"], c + 1)
                nc.vector.tensor_tensor(s_fin[:, t4, :], s_fin[:, t4, :], f_sb[:, t4, :], ALU.mult).then_inc(sm["s_fin2"], 1)
                dve.wait_ge(sm["s_fin2"], 2 * c + 1)
                nc.vector.tensor_tensor(x_sb[:, t4, :], x_sb[:, t4, :], s_fin[:, t4, :], ALU.add).then_inc(sm["s_fin2"], 1)

            combine(0)
            combine(1)
            combine(2)
            add_bias(NC - 1)
            combine(3)

        @block.scalar
        def _(act):
            def first_tokens_out(c):
                act.wait_ge(sm["s_xtr"], c + 1)
                nc.scalar.copy(xnT[:, c * 512:c * 512 + 512], pT[:, (c + 1) % 2, :]).then_inc(sm["s_xt"], 1)

            for h in range(2):
                act.wait_ge(sm["s_ve"], h + 1)
                nc.scalar.activation(sdev[:, BT * h:BT * h + BT], var_e[:, BT * h:BT * h + BT], ACT.Sqrt).then_inc(sm["s_sd"], 1)
            act.wait_ge(sm["s_wtr"], 1)
            nc.scalar.copy(w_T[:, :, :].rearrange("p a b -> p (a b)"), pT[:, 0, :]).then_inc(sm["s_wt"], 1)
            first_tokens_out(0)
            first_tokens_out(1)
            act.wait_ge(sm["s_wtr"], 2)
            act.wait_ge(sm["s_zero"], 3)
            nc.scalar.copy(wr_T[:, 0:E0], pM[:, 0:E0]).then_inc(sm["s_wt"], 1)
            nc.scalar.copy(bvT[:, :], pM[:, 320:448]).then_inc(sm["s_wt"], 1)
            nc.scalar.copy(b1T[:, :], pM[:, 64:64 + E0 * NS]).then_inc(sm["s_wt"], 1)
            nc.scalar.copy(cenT[:, :], pM[:, 256:256 + E1]).then_inc(sm["s_wt"], 1)
            nc.scalar.copy(smallT[:, :], pM[:, 272:272 + 6 * E1]).then_inc(sm["s_wt"], 1)
            first_tokens_out(2)
            first_tokens_out(3)
            act.wait_ge(sm["s_bload"], 64)
            dst = [pS[:, 1, 0:512], pS[:, 1, 512:1024], pM[:, :], pH[:, :]]
            for c in range(NC):
                for j in range(2):
                    n = 3 * c + j
                    act.wait_ge(sm["s_pj"], n + 1)
                    nc.scalar.activation((qT, kT)[j][:, c * 512:c * 512 + 512], dst[n % 4], ACT.Identity,
                                         bias=bqk[:, j:j + 1]).then_inc(sm["s_pje_a"], 1)

            def exps(i):
                act.wait_ge(sm["s_nm"], i + 1)
                if i >= 2:
                    act.wait_ge(sm["s_tr"], 2 * (i - 1))
                nc.scalar.activation(probs[:, i % 2, :], pS[:, i % 2, :], ACT.Exp, bias=nbias[:, i:i + 1], scale=SC0,
                                     accum_out=rsum[:, i:i + 1]).then_inc(sm["s_exp"], 1)

            for i in range(NT):
                exps(i)
                for h in range(2):
                    act.wait_ge(sm["s_tr"], 2 * i + h + 1)
                    if i >= 2:
                        act.wait_ge(sm["s_pv"], i - 1)
                    nc.scalar.copy(probsT[:, i % 2, h * 512:h * 512 + 512], pT[:, h, :]).then_inc(sm["s_ev"], 1)
                if i == CAP // 8 + 1:
                    act.wait_ge(sm["s_wn"], 1)
                    nc.scalar.activation(slot_m[:, :], slot_v[:, :], ACT.Exp, bias=slot_s[:, 0:1],
                                         accum_out=slot_s[:, 1:2]).then_inc(sm["s_we"], 1)
            def gelu_h(p):
                act.wait_ge(sm["s_hbias"], p + 1)
                nc.scalar.activation(hg[:, p % 2, :], hg[:, p % 2, :], ACT.Gelu).then_inc(sm["s_gelu"], 1)

            for p in range(NP):
                act.wait_ge(sm["s_h"], p + 1)
                if p >= 2:
                    act.wait_ge(sm["s_ht"], p - 1)
                nc.scalar.copy(hb[:, p % 2, :], pS[:, p % 2, 0:512]).then_inc(sm["s_hr"], 1)
                if p:
                    gelu_h(p - 1)
            gelu_h(NP - 1)

            def silus(b):
                for c in (2 * b, 2 * b + 1):
                    t4 = slice(4 * c, 4 * c + 4)
                    act.wait_ge(sm[("s_sum", "s_sum2")[b]], 2 * (c % 2) + 2)
                    nc.scalar.activation(accs[:, 1, t4, :], accs[:, 0, t4, :], ACT.Silu).then_inc(sm["s_silu"], 1)

            def roots(k, bt):
                act.wait_ge(sm["s_ve"], k + 1)
                nc.scalar.activation(sdev[:, bt], var_e[:, bt], ACT.Sqrt).then_inc(sm["s_sd"], 1)

            def tokens_out(b):
                for c in (2 * b, 2 * b + 1):
                    act.wait_ge(sm["s_xtr"], NC + c + 1)
                    nc.scalar.copy(xnT[:, c * 512:c * 512 + 512], pT[:, c % 2, :]).then_inc(sm["s_xt"], 1)

            def q_out(b):
                for c in (2 * b, 2 * b + 1):
                    act.wait_ge(sm["s_q1"], c + 1)
                    nc.scalar.activation(qT[:, c * 512:c * 512 + 512], q_bank(c),
                                         ACT.Identity, bias=bcol1[:, 0:1]).then_inc(sm["s_q1e"], 1)

            def latents(b):
                for c in (2 * b, 2 * b + 1):
                    act.wait_ge(sm["s_la"], c + 1)
                    nc.scalar.activation(latT[:, c * 512:c * 512 + 512], pT[0:2 * LAT, c % 2, :], ACT.Gelu,
                                         bias=bkd[:, 0:1]).then_inc(sm["s_lae"], 1)

            def k_out(b):
                for c in (2 * b, 2 * b + 1):
                    act.wait_ge(sm["s_kk"], c + 1)
                    nc.scalar.activation(kT[:, c * 512:c * 512 + 512], k_bank(c),
                                         ACT.Identity, bias=bcol1[:, 1:2]).then_inc(sm["s_kke"], 1)

            def v_out(b):
                for c in (2 * b, 2 * b + 1):
                    act.wait_ge(sm["s_vv"], c + 1)
                    nc.scalar.copy(v_sb[:, 4 * c:4 * c + 4, :],
                                   (pM, pH)[c % 2][:, :].rearrange("p (t d) -> p t d", d=D)).then_inc(sm["s_v1e"], 1)

            def part(b, side, st):
                if st == 0:
                    act.wait_ge(sm[("s_q1e", "s_kke")[side]], 2 * b + 2)
                else:
                    act.wait_ge(sm["s_sub"], part_count(b, side, 0))
                bs = slice(b * S, b * S + S)
                nc.scalar.copy(parts[side][:, st, bs], qk_mem[:, side, bs]).then_inc(sm["s_cp"], 1)

            silus(0)
            roots(2, slice(0, BT))
            act.wait_ge(sm["s_btr"], 1)
            nc.scalar.copy(bcol1[:, :], pM[:, 0:2]).then_inc(sm["s_bte"], 1)
            nc.scalar.copy(bvT[:, :], pM[:, P:2 * P]).then_inc(sm["s_bte"], 1)
            act.wait_ge(sm["s_bte"], 2)
            tokens_out(0)
            silus(1)
            q_out(0)
            part(0, 0, 0)
            latents(0)
            k_out(0)
            part(0, 1, 0)
            roots(3, slice(BT, NT))
            part(0, 0, 1)
            part(0, 1, 1)
            tokens_out(1)
            v_out(0)
            q_out(1)
            part(1, 0, 0)
            latents(1)
            k_out(1)
            part(1, 1, 0)
            part(1, 0, 1)
            part(1, 1, 1)
            v_out(1)
            roots(4, slice(0, NT))
            act.wait_ge(sm["s_lnb"], 1)
            for t in range(NT):
                if t == 0:
                    act.wait_ge(sm["s_x1"], 8)
                nc.scalar.activation(s_sb[:, t, :], xn[:, t, :], ACT.Identity, bias=nbias[:, t:t + 1],
                                     scale=rstd[:, t:t + 1]).then_inc(sm["s_xn"], 1)
            act.wait_ge(sm["s_oh"], 2)
            nc.scalar.activation(alpha[:, 0, :], amax[:, :], ACT.Exp, scale=-1.0).then_inc(sm["s_al"], 1)

            def exps2(n, a):
                qc, kt, q0, cols = STEPS[n % NSTEP]
                act.wait_ge(sm["s_s1"], GH * n + 2 * a + 2)
                act.wait_ge(sm["s_pv1"], n - 1)
                nc.scalar.activation(pr1[:, n % 2, 2 * a:2 * a + 2, 0:cols],
                                     pS[:, a, :].rearrange("p (j q) -> p j q", j=2)[:, :, 0:cols],
                                     ACT.Exp, scale=SC1).then_inc(sm["s_e1"], 2)

            def exps1(n, j):
                qc, kt, q0, cols = STEPS[n % NSTEP]
                act.wait_ge(sm["s_s1"], GH * n + j + 1)
                if n >= 2:
                    act.wait_ge(sm["s_pv1"], n - 1)
                nc.scalar.activation(pr1[:, n % 2, j, 0:cols], pT[:, j % 2, 0:cols], ACT.Exp, scale=SC1).then_inc(sm["s_e1"], 1)

            def move_heads(c):
                act.wait_ge(sm["s_ot"], c + 1)
                nc.scalar.copy(hs[:, c % 2, :], pH[:, :]).then_inc(sm["s_ote"], 1)

            for n in range(NG * NSTEP + 2):
                if n < SPREAD0:
                    exps1(n, 0)
                    exps1(n, 1)
                elif n < NG * NSTEP:
                    exps2(n, 0)
                j, sub = ffn_part(n - 1)
                if sub == 0:
                    act.wait_ge(sm["s_fa"], j + 1)
                    act.wait_ge(sm["s_wj"], 3 * j + 3)
                    if j:
                        act.wait_ge(sm["s_fb"], j)
                    nc.scalar.activation(xlT[:, :], pH[:, 0:P], ACT.Identity, bias=s_tile[:, j % 2, FC + 1:FC + 2],
                                         scale=s_tile[:, j % 2, FC:FC + 1]).then_inc(sm["s_fae"], 1)
                if sub == 1:
                    act.wait_ge(sm["s_fbe"], j + 1)
                    nc.scalar.activation(hs[:, j % 2, :], hs[:, j % 2, :], ACT.Relu).then_inc(sm["s_relu"], 1)
                for c, first in enumerate(OUTS):
                    if n == first + 1:
                        move_heads(c)
                if n < SPREAD0:
                    exps1(n, 2)
                    exps1(n, 3)
                elif n < NG * NSTEP:
                    exps2(n, 1)
                r = ends(n - 1)
                if r >= 0:
                    act.wait_ge(sm["s_pv1"], n)
                    if r >= 2:
                        act.wait_ge(sm["s_tr1"], r - 1)
                    nc.scalar.copy(acc_sb[:, r % 2, :], pM[:, :]).then_inc(sm["s_ace"], 1)

            def gate(c):
                t4 = slice(4 * c, 4 * c + 4)
                act.wait_ge(sm["s_als"], 2 + 4 * c + 4)
                nc.scalar.activation(f_sb[:, t4, :], f_sb[:, t4, :], ACT.Silu).then_inc(sm["s_gate"], 1)

            gate(0)
            gate(1)
            gate(2)
            move_heads(NC - 1)
            gate(3)


_INS = ['L0_attn_x', 'L0_attn_w_q', 'L0_attn_b_q', 'L0_attn_w_k', 'L0_attn_b_k', 'L0_attn_w_v', 'L0_attn_b_v',
        'L0_attn_w_out', 'L0_attn_b_out', 'L0_ffn_Wr', 'L0_ffn_W1', 'L0_ffn_b1', 'L0_ffn_W2', 'L0_ffn_b2']
_INS1 = ['L1_attn_Wq', 'L1_attn_bq', 'L1_attn_Wkd', 'L1_attn_bkd', 'L1_attn_Wku', 'L1_attn_bku', 'L1_attn_Wo',
         'L1_attn_bo', 'L1_ffn_centroids', 'L1_ffn_ln_g', 'L1_ffn_ln_b', 'L1_ffn_w1', 'L1_ffn_b1', 'L1_ffn_w2',
         'L1_ffn_b2']


def kernel(**inputs):
    import numpy as _np
    import concourse.bacc as _bacc
    from concourse import mybir as _mybir
    from concourse.bass_utils import run_bass_kernel_spmd as _run
    nc = _bacc.Bacc("TRN2", target_bir_lowering=False, num_devices=1)
    arrays, aps = {}, {}
    for name in _INS + _INS1:
        v = _np.ascontiguousarray(inputs[name])
        arrays[f"in_{name}_dram"] = v
        aps[name] = nc.dram_tensor(f"in_{name}_dram", v.shape, _mybir.dt.from_np(v.dtype), kind="ExternalInput").ap()
    o = nc.dram_tensor("out_0_dram", (2, 1024, 128), _mybir.dt.float32, kind="ExternalOutput").ap()
    build(nc, aps, o)
    r = _run(nc, [arrays], core_ids=[0])
    return r.results[0]["out_0_dram"]
```
